# Optimizing a Trainium2 kernel written in Bass

```python
import numpy as np
import jax
import jax.numpy as jnp

def _softmax(x, axis=-1):
    return jax.nn.softmax(x, axis=axis)

def _gelu(x):
    return jax.nn.gelu(x, approximate=True)

def _silu(x):
    return jax.nn.silu(x)

def _sigmoid(x):
    return jax.nn.sigmoid(x)

def _layernorm(x, axis=-1, eps=1e-05):
    m = jnp.mean(x, axis=axis, keepdims=True)
    v = jnp.var(x, axis=axis, keepdims=True)
    return (x - m) / jnp.sqrt(v + eps)

def _scatter_add(tgt, idx, src, axis=0):
    return tgt.at[idx].add(src)

def _segment_sum(src, seg, n):
    return jax.ops.segment_sum(src, seg, n)
kernel_name = 'mk_seq_postln_d1_jaxref_r8_d11328'

def setup_inputs(seed: int=0):
    np.random.seed(seed)
    _w = jnp.asarray

    def _L0_attn_setup():
        import jax, jax.numpy as jnp
        import numpy as np
        B_SZ, SEQ, D_MODEL = (1, 256, 128)
        D_IN, N_STATE, DT_RANK, KSIZE = (256, 16, 64, 3)

        def selective_scan(u, delta, A, Bm, Cm, D):
            dA = jnp.einsum('bld,dn->bldn', delta, A)
            dB_u = jnp.einsum('bld,bld,bln->bldn', delta, u, Bm)
            dA_shift = jnp.concatenate([dA[:, 1:], jnp.zeros_like(dA[:, :1])], axis=1)
            dA_cs = jnp.exp(jnp.flip(jnp.cumsum(jnp.flip(dA_shift, axis=1), axis=1), axis=1))
            xs = jnp.cumsum(dB_u * dA_cs, axis=1) / (dA_cs + 1e-12)
            y = jnp.einsum('bldn,bln->bld', xs, Cm)
            return y + u * D
        key = jax.random.key(seed)
        ks = jax.random.split(key, 7)
        x = jax.random.normal(ks[0], (B_SZ, SEQ, D_MODEL), jnp.float32)
        W_in = jax.random.normal(ks[1], (D_MODEL, 2 * D_IN), jnp.float32) * 0.02
        conv_w = jax.random.normal(ks[2], (D_IN, 1, KSIZE), jnp.float32) * 0.1
        W_x = jax.random.normal(ks[3], (D_IN, DT_RANK + 2 * N_STATE), jnp.float32) * 0.02
        W_delta = jax.random.normal(ks[4], (DT_RANK, D_IN), jnp.float32) * 0.02
        b_delta = jnp.zeros((D_IN,), jnp.float32)
        A_log = jnp.tile(jnp.arange(1, N_STATE + 1, dtype=jnp.float32)[None, :], (D_IN, 1))
        D = jnp.ones((D_IN,), jnp.float32)
        W_out = jax.random.normal(ks[5], (D_IN, D_MODEL), jnp.float32) * 0.02
        return dict(x=x, W_in=W_in, conv_w=conv_w, W_x=W_x, W_delta=W_delta, b_delta=b_delta, A_log=A_log, D=D, W_out=W_out)
    _L0_attn_in = _L0_attn_setup()

    def _L0_ffn_setup():
        import jax, jax.numpy as jnp
        import numpy as np
        DIM = 128
        HIDDEN = 512
        E = 8
        K = 2

        def _ffn_hidden(h, multiple_of=32):
            h = int(2 * h / 3)
            return multiple_of * ((h + multiple_of - 1) // multiple_of)
        EXP_HID = _ffn_hidden(HIDDEN)
        SH_HID = _ffn_hidden(HIDDEN // 2)

        def _swiglu(t, a, b, c):
            return jax.nn.silu(t @ a) * (t @ c) @ b
        key = jax.random.key(seed)
        ks = jax.random.split(key, 8)

        def xavier(k, shape, fan_in, fan_out):
            lim = np.sqrt(6.0 / (fan_in + fan_out)).astype(np.float32)
            return jax.random.uniform(k, shape, jnp.float32, -lim, lim)
        return {'x': jax.random.normal(ks[0], (2, 256, DIM), jnp.float32), 'gate_w': xavier(ks[1], (E, DIM), DIM, E), 'w1': xavier(ks[2], (E, DIM, EXP_HID), DIM, EXP_HID), 'w2': xavier(ks[3], (E, EXP_HID, DIM), EXP_HID, DIM), 'w3': xavier(ks[4], (E, DIM, EXP_HID), DIM, EXP_HID), 'sw1': xavier(ks[5], (DIM, SH_HID), DIM, SH_HID), 'sw2': xavier(ks[6], (SH_HID, DIM), SH_HID, DIM), 'sw3': xavier(ks[7], (DIM, SH_HID), DIM, SH_HID)}
    _L0_ffn_in = _L0_ffn_setup()
    _d = {'L0_attn_x': _L0_attn_in['x'], 'L0_attn_W_in': _L0_attn_in['W_in'], 'L0_attn_conv_w': _L0_attn_in['conv_w'], 'L0_attn_W_x': _L0_attn_in['W_x'], 'L0_attn_W_delta': _L0_attn_in['W_delta'], 'L0_attn_b_delta': _L0_attn_in['b_delta'], 'L0_attn_A_log': _L0_attn_in['A_log'], 'L0_attn_D': _L0_attn_in['D'], 'L0_attn_W_out': _L0_attn_in['W_out'], 'L0_ffn_gate_w': _L0_ffn_in['gate_w'], 'L0_ffn_w1': _L0_ffn_in['w1'], 'L0_ffn_w2': _L0_ffn_in['w2'], 'L0_ffn_w3': _L0_ffn_in['w3'], 'L0_ffn_sw1': _L0_ffn_in['sw1'], 'L0_ffn_sw2': _L0_ffn_in['sw2'], 'L0_ffn_sw3': _L0_ffn_in['sw3']}
    _x0 = _d['L0_attn_x']
    _d['L0_attn_x'] = jax.random.normal(jax.random.fold_in(jax.random.key(seed), 1), (2, 2048, 128), dtype=_x0.dtype)
    del _x0
    return _d

def reference(L0_attn_x, L0_attn_W_in, L0_attn_conv_w, L0_attn_W_x, L0_attn_W_delta, L0_attn_b_delta, L0_attn_A_log, L0_attn_D, L0_attn_W_out, L0_ffn_gate_w, L0_ffn_w1, L0_ffn_w2, L0_ffn_w3, L0_ffn_sw1, L0_ffn_sw2, L0_ffn_sw3):

    def _L0_attn_ref(x, W_in, conv_w, W_x, W_delta, b_delta, A_log, D, W_out):
        import jax, jax.numpy as jnp
        import numpy as np
        B_SZ, SEQ, D_MODEL = (1, 256, 128)
        D_IN, N_STATE, DT_RANK, KSIZE = (256, 16, 64, 3)

        def selective_scan(u, delta, A, Bm, Cm, D):
            dA = jnp.einsum('bld,dn->bldn', delta, A)
            dB_u = jnp.einsum('bld,bld,bln->bldn', delta, u, Bm)
            dA_shift = jnp.concatenate([dA[:, 1:], jnp.zeros_like(dA[:, :1])], axis=1)
            dA_cs = jnp.exp(jnp.flip(jnp.cumsum(jnp.flip(dA_shift, axis=1), axis=1), axis=1))
            xs = jnp.cumsum(dB_u * dA_cs, axis=1) / (dA_cs + 1e-12)
            y = jnp.einsum('bldn,bln->bld', xs, Cm)
            return y + u * D
        d_in = conv_w.shape[0]
        ksz = conv_w.shape[2]
        n = A_log.shape[1]
        dtr = W_delta.shape[0]
        x_and_res = x @ W_in
        xi, res = (x_and_res[..., :d_in], x_and_res[..., d_in:])
        xc = jnp.transpose(xi, (0, 2, 1))
        xc = jax.lax.conv_general_dilated(xc, conv_w, window_strides=(1,), padding=[(ksz - 1, 0)], dimension_numbers=('NCH', 'OIH', 'NCH'), feature_group_count=d_in)
        xi = jnp.transpose(xc, (0, 2, 1))
        xi = xi * jax.nn.sigmoid(xi)
        A = -jnp.exp(A_log)
        x_dbl = xi @ W_x
        delta_lr = x_dbl[..., :dtr]
        Bm = x_dbl[..., dtr:dtr + n]
        Cm = x_dbl[..., dtr + n:]
        delta = jax.nn.softplus(delta_lr @ W_delta + b_delta)
        y = selective_scan(xi, delta, A, Bm, Cm, D)
        y = y * (res * jax.nn.sigmoid(res))
        return y @ W_out

    def _L0_ffn_ref(x, gate_w, w1, w2, w3, sw1, sw2, sw3):
        import jax, jax.numpy as jnp
        import numpy as np
        DIM = 128
        HIDDEN = 512
        E = 8
        K = 2

        def _ffn_hidden(h, multiple_of=32):
            h = int(2 * h / 3)
            return multiple_of * ((h + multiple_of - 1) // multiple_of)
        EXP_HID = _ffn_hidden(HIDDEN)
        SH_HID = _ffn_hidden(HIDDEN // 2)

        def _swiglu(t, a, b, c):
            return jax.nn.silu(t @ a) * (t @ c) @ b
        B, S, D = x.shape
        xt = x.reshape(-1, D)
        T = xt.shape[0]
        logits = xt @ gate_w.T
        scores = jax.nn.softmax(logits, axis=-1)
        topk_w, topk_i = jax.lax.top_k(scores, K)
        comb = jnp.zeros((T, E), x.dtype).at[jnp.arange(T)[:, None], topk_i].add(topk_w)
        y = jnp.zeros_like(xt)
        for e in range(E):
            y = y + comb[:, e:e + 1] * _swiglu(xt, w1[e], w2[e], w3[e])
        y = y.reshape(B, S, D)
        return y + _swiglu(x, sw1, sw2, sw3)
    x = L0_attn_x
    x = _layernorm(x + _L0_attn_ref(x, L0_attn_W_in, L0_attn_conv_w, L0_attn_W_x, L0_attn_W_delta, L0_attn_b_delta, L0_attn_A_log, L0_attn_D, L0_attn_W_out), axis=-1)
    x = _layernorm(x + _L0_ffn_ref(x, L0_ffn_gate_w, L0_ffn_w1, L0_ffn_w2, L0_ffn_w3, L0_ffn_sw1, L0_ffn_sw2, L0_ffn_sw3), axis=-1)
    return x

_drawn_inputs = setup_inputs


def setup_inputs(seed=0):
    import zlib

    import numpy as np

    out = dict(_drawn_inputs(seed))
    spreads = {'L0_attn_b_delta': (0.0, 2.0), 'L0_attn_D': (1.0, 0.6)}
    factors = {'L0_attn_W_in': 8.0,
     'L0_attn_conv_w': 8.0,
     'L0_attn_W_x': 8.0,
     'L0_attn_W_delta': 8.0,
     'L0_attn_A_log': 8.0,
     'L0_attn_W_out': 8.0}
    for name, (base, spread) in spreads.items():
        noise = np.random.default_rng([zlib.crc32(name.encode()), seed]).standard_normal(out[name].shape)
        drawn = base * np.exp(spread * noise) if base else spread * noise
        out[name] = jnp.asarray(drawn.astype(out[name].dtype))
    for name, factor in factors.items():
        out[name] = (out[name] * factor).astype(out[name].dtype)
    return out
```

```python
from contextlib import ExitStack

import concourse.bass as bass
from concourse import mybir

F32 = mybir.dt.float32
BF16 = mybir.dt.bfloat16
I32 = mybir.dt.int32
U32 = mybir.dt.uint32
ACT = mybir.ActivationFunctionType
ALU = mybir.AluOpType
AX = mybir.AxisListType

P = 128
BATCH, SEQ, DM = 2, 2048, 128
TOK = BATCH * SEQ
DIN, NST, RANK, TAPS = 256, 16, 64, 3
DC = DIN // P
BLK = 512
NBLK = TOK // BLK
TPB = BLK // P
TILES = TOK // P
HALO = TAPS - 1
XTW = SEQ + HALO
CH = 64
CPB = BLK // CH
NCH = TOK // CH
CPS = SEQ // CH
BPS = SEQ // BLK
E, K = 8, 2
EH = 352
EC = 3
SH = 192
SHH = SH // 2
N_TILES = TOK * K // P + E
HALF = 4
IDXC = N_TILES + 2 * HALF
LN_EPS = 1e-5
NEG_LN_SCAN_EPS = 27.631021115928547
DEAD = -104.0
MAX_EXP = 88.5
FLOOR = -200.0
A_UNIT = float(2 ** 30)
SOFT_CUT = 1.0 / 256.0
NO_ROW = 1 << 20


class Steps:

    def __init__(self, engine, semaphore):
        self.engine, self.semaphore, self.count, self.shift = engine, semaphore, 0, 0

    def settle(self, instruction):
        instruction.then_inc(self.semaphore, 1)
        self.count += 1
        self.engine.wait_ge(self.semaphore, self.count + self.shift)


class SteppedLoop:

    def __init__(self, engine, steps, count, per):
        self.loop, self.steps, self.turns, self.per = engine.Fori(0, count), steps, count, per

    def __enter__(self):
        i = self.loop.__enter__()
        self.start = self.steps.count
        self.steps.shift = i * self.per
        return i

    def __exit__(self, *what):
        if what[0] is None:
            assert self.steps.count == self.start + self.per, self.steps.count - self.start
        self.steps.shift = 0
        self.steps.count = self.start + self.turns * self.per
        return self.loop.__exit__(*what)


def hold(engine, waited):
    engine.sem_inc(waited, 1)


def ds(start, size):
    return bass.ds(start, size)


def build(nc, x, W_in, conv_w, W_x, W_delta, b_delta, A_log, D, W_out,
          gate_w, w1, w2, w3, sw1, sw2, sw3, out):
    with ExitStack() as ctx:
        def sb(name, shape, dt=F32):
            return ctx.enter_context(nc.sbuf_tensor(name, shape, dt))

        def sem(name):
            return ctx.enter_context(nc.semaphore(name))

        u_all = sb("u_all", [P, DC, TOK])
        y_all = sb("y_all", [P, DC, TOK])
        dl_all = sb("dl_all", [P, DC, TOK])
        xT = sb("xT", [P, BATCH * XTW])
        xdl = sb("xdl", [RANK, TOK])
        bc = sb("bc", [2 * NST, TOK])
        scratch = sb("scratch", [P, 6, DC * BLK])

        uf = u_all[:].rearrange("p c t -> p (c t)")
        w13 = uf[:, 0:E * 2 * EH].rearrange("p (e n) -> p e n", e=E)
        acc = xT[:, 0:TOK].rearrange("p (t d) -> p t d", d=DM)
        y0r = uf[:, 0:2 * BLK].rearrange("p (r i d) -> p r i d", r=2, d=DM)
        y1r = uf[:, 2 * BLK:4 * BLK].rearrange("p (r i d) -> p r i d", r=2, d=DM)
        outr = uf[:, 4 * BLK:6 * BLK].rearrange("p (r i d) -> p r i d", r=2, d=DM)
        df = dl_all[:].rearrange("p c t -> p (c t)")
        res1 = df[:, 0:TOK].rearrange("p (t d) -> p t d", d=DM)
        x1b = df[:, TOK:TOK + 2 * BLK].rearrange("p (r i d) -> p r i d", r=2, d=DM)
        x1T = df[:, TOK + 2 * BLK:TOK + 4 * BLK].rearrange("p (r t) -> p r t", r=2)
        shT = df[0:SHH, TOK + 4 * BLK:TOK + 8 * BLK].rearrange("p (r h t) -> p r h t", r=2, h=2)
        yf = y_all[:].rearrange("p c t -> p (c t)")
        w2s = yf[:, 0:E * EC * DM].rearrange("p (e c n) -> p e c n", e=E, c=EC)
        xin = scratch[:, 0:2, 0:BLK].rearrange("p r (i d) -> p r i d", d=DM)
        z_buf = scratch[:, 0:2, :].rearrange("p r (c t) -> p r c t", c=DC)
        ln_buf = scratch[:, 2:4, :].rearrange("p r (c t) -> p r c t", c=DC)
        sq_buf = scratch[:, 4:6, :].rearrange("p r (c t) -> p r c t", c=DC)
        decay = scratch[:, 0:2, :].rearrange("p c (n t) -> p c n t", n=NST)
        gain = scratch[:, 2:4, :].rearrange("p c (n t) -> p c n t", n=NST)
        dbu = scratch[:, 4, :].rearrange("p (n t) -> p n t", n=NST)
        hs = scratch[:, 5, :].rearrange("p (n t) -> p n t", n=NST)
        ybuf = scratch[:, 0:2, :].rearrange("p r (c t) -> p r c t", c=DC)
        xres = scratch[:, 2:4, 0:BLK].rearrange("p r (i d) -> p r i d", d=DM)
        sgate = scratch[0:SHH, 4, :].rearrange("p (h t) -> p h t", h=2)
        xg = scratch[:, 0, 0:4 * DM].rearrange("p (r d) -> p r d", r=4)
        xgT = scratch[:, 0, 4 * DM:6 * DM].rearrange("p (r d) -> p r d", r=2)
        egate = scratch[:, 1, 0:EH]
        eh = scratch[:, 1, 512:512 + EH]
        ehT = scratch[:, 2, 0:EC * P].rearrange("p (c t) -> p c t", c=EC)
        yo = scratch[:, 3, 0:4 * DM].rearrange("p (r d) -> p r d", r=4)

        win = sb("win", [P, 2 * DIN])
        cwb = sb("cwb", [P, DIN, TAPS])
        wk = sb("wk", [P, TAPS, DIN])
        wx = sb("wx", [P, DC, RANK + 2 * NST])
        wdel = sb("wdel", [RANK, DIN])
        bdel = sb("bdel", [P, DC])
        dskip = sb("dskip", [P, DC])
        alog = sb("alog", [P, DC, NST])
        aneg = sb("aneg", [P, DC, NST])
        amax = sb("amax", [P, DC])
        wout = sb("wout", [P, DC, DM])
        gw = sb("gw", [E, DM])
        gwT = sb("gwT", [P, E])
        s1 = sb("s1", [P, SH])
        s3 = sb("s3", [P, SH])
        s2 = sb("s2", [SHH, 2, DM])
        ident = sb("ident", [P, P])
        ones = sb("ones", [P, P])
        before = sb("before", [P, P])
        iota = sb("iota", [P, P])
        pcol = sb("pcol", [P, 1])
        csum = sb("csum", [P, DC, BATCH, CPS])
        rend = sb("rend", [P, DC, BATCH, CPS])
        dch = sb("dch", [P, DC, CH])
        rch = sb("rch", [P, DC, CH])
        live = sb("live", [P, DC, NCH])
        flagf = sb("flagf", [1, NCH])
        flags = sb("flags", [1, NCH], I32)
        hcar = sb("hcar", [P, DC, NST])
        hmul = sb("hmul", [P, NST])
        du = sb("du", [P, DC, CH])
        ysum = sb("ysum", [P, CH])
        gch = sb("gch", [P, DC, CH])
        bst = sb("bst", [P, 2, TPB, 6])
        bag = sb("bag", [P, 2, TPB, 2])
        mv = sb("mv", [P, TILES, 2])
        rstd = sb("rstd", [P, TILES])
        epst = sb("epst", [P, 3])
        lg = sb("lg", [P, TILES, E])
        sc = sb("sc", [P, TILES, E])
        t3 = sb("t3", [P, TILES, E])
        m1 = sb("m1", [P, TILES, E])
        m2 = sb("m2", [P, TILES, E])
        rk = sb("rk", [P, TILES, E])
        ex = sb("ex", [P, TILES, E])
        col = sb("col", [P, TILES])
        wk2 = sb("wk2", [P, K, TILES])
        slot = sb("slot", [P, K, TILES])
        sloti = sb("sloti", [P, K, TILES], I32)
        hii = sb("hii", [P, K, TILES], I32)
        loi = sb("loi", [P, K, TILES], I32)
        hif = sb("hif", [P, K, TILES])
        lof = sb("lof", [P, K, TILES])
        cnt = sb("cnt", [P, E])
        cnti = sb("cnti", [P, E], I32)
        nti = sb("nti", [P, E], I32)
        ntf = sb("ntf", [P, E])
        tend = sb("tend", [P, E])
        tbeg = sb("tbeg", [P, E])
        desc = sb("desc", [P, E])
        tcol = sb("tcol", [P, K * TILES])
        tex = sb("tex", [1, IDXC, E])
        texs = sb("texs", [1, IDXC])
        texi = sb("texi", [1, IDXC], I32)
        ohl = sb("ohl", [P, 2, P], BF16)
        ohh = sb("ohh", [P, 2, 3, N_TILES], BF16)
        zer = sb("zer", [P, 3 * N_TILES], BF16)
        pid = sb("pid", [P, 3, N_TILES])
        dstf = sb("dstf", [P, N_TILES])
        tokf = sb("tokf", [P, N_TILES])
        toki = sb("toki", [P, N_TILES], I32)
        idx_src = sb("idx_src", [P, IDXC], I32)
        idx_dst = sb("idx_dst", [P, IDXC], I32)
        ring_src = sb("ring_src", [P, 2, HALF], I32)
        ring_dst = sb("ring_dst", [P, 2, HALF], I32)

        ps = ctx.enter_context(nc.psum_tensor("ps", [P, 8, BLK], F32))

        x1_rows = nc.dram_tensor("x1_rows", [TOK, DM], F32).ap()
        y_rows = nc.dram_tensor("y_rows", [K * TOK, DM], F32).ap()

        x_in = [sem(f"x_in{r}") for r in range(2)]
        w_first, w_mix, w_ffn, w_exp = sem("w_first"), sem("w_mix"), sem("w_ffn"), sem("w_exp")
        const_step, consts, halo = sem("const_step"), sem("consts"), sem("halo")
        pool_held, act_held, dve_held = sem("pool_held"), sem("act_held"), sem("dve_held")
        pool_step, dve_step = sem("pool_step"), sem("dve_step")
        wk_ready, alog_ready = sem("wk_ready"), sem("alog_ready")
        gwT_sum, gwT_ready = sem("gwT_sum"), sem("gwT_ready")
        x_turned, xT_ready = sem("x_turned"), sem("xT_ready")
        u_sum, u_ready, g_sum, g_ready = sem("u_sum"), sem("u_ready"), sem("g_sum"), sem("g_ready")
        xd_sum, xd_ready, y_ready = sem("xd_sum"), sem("xd_ready"), sem("y_ready")
        pd_sum, z_ready, z_clamped, ln_ready = sem("pd_sum"), sem("z_ready"), sem("z_clamped"), sem("ln_ready")
        dl_ready, a_exp = sem("dl_ready"), sem("a_exp")
        live_ready, live_sum, flags_ready = sem("live_ready"), sem("live_sum"), sem("flags_ready")
        r_ready, bc_sum = sem("r_ready"), sem("bc_sum")
        za_raw, zr_raw = sem("za_raw"), sem("zr_raw")
        za_ready, zr_ready, decay_ready, gain_ready = sem("za_ready"), sem("zr_ready"), sem("decay_ready"), sem("gain_ready")
        chunk_done, batch_start = sem("chunk_done"), sem("batch_start")
        yb_ready, mix_sum, res_ready = sem("yb_ready"), sem("mix_sum"), sem("res_ready")
        xres_in = [sem(f"xres_in{r}") for r in range(2)]
        mv_ready, std_ready = sem("mv_ready"), sem("std_ready")
        x1_ready, x1_turned, x1T_ready = sem("x1_ready"), sem("x1_turned"), sem("x1T_ready")
        x1_stored = [sem(f"x1_stored{r}") for r in range(2)]
        gate_sum, lg_ready = sem("gate_sum"), sem("lg_ready")
        sh_a, sh_c, sh_silu, sh_h, sh_sum, acc_ready = (sem("sh_a"), sem("sh_c"), sem("sh_silu"),
                                                        sem("sh_h"), sem("sh_sum"), sem("acc_ready"))
        lgx_ready, sce_ready = sem("lgx_ready"), sem("sce_ready")
        m_ready, rank_sum = sem("m_ready"), sem("rank_sum")
        oh_ready, oh_sum = sem("oh_ready"), sem("oh_sum")
        texi_ready = sem("texi_ready")
        src_ready, dst_ready = sem("src_ready"), sem("dst_ready")
        gathered = [sem(f"gathered{r}") for r in range(4)]
        scattered = [sem(f"scattered{r}") for r in range(4)]
        e_turned, eT_ready, e_a, e_c, e_silu, e_h = (sem("e_turned"), sem("eT_ready"), sem("e_a"),
                                                     sem("e_c"), sem("e_silu"), sem("e_h"))
        eh_turned, ehT_ready, e_sum, e_out = sem("eh_turned"), sem("ehT_ready"), sem("e_sum"), sem("e_out")
        y_in = [sem(f"y_in{r}") for r in range(2)]
        fin_read, fmv_ready, fstd_ready, o_ready = sem("fin_read"), sem("fmv_ready"), sem("fstd_ready"), sem("o_ready")
        o_stored = [sem(f"o_stored{r}") for r in range(2)]

        x_rows = x.rearrange("b s d -> (b s) d").rearrange("(n i p) d -> n p i d", i=TPB, p=P)
        o_rows = out.rearrange("b s d -> (b s) d").rearrange("(n i p) d -> n p i d", i=TPB, p=P)
        x1_blocks = x1_rows.rearrange("(n i p) d -> n p i d", i=TPB, p=P)
        y_blocks = y_rows.rearrange("(k n i p) d -> k n p i d", k=K, i=TPB, p=P)

        def row_block(view, n):
            return view[ds(n, 1)].rearrange("a p i d -> (a p) i d")

        def chunk_loops(engine, ops, chunk, skip, start_batch=None):
            with engine.Fori(0, BATCH) as b:
                if start_batch:
                    start_batch(b)
                with engine.Fori(0, BPS) as n:
                    any_live = ops.value_load(flags[0:1, ds(b * CPS + n * CPB + (CPB - 1), 1)], min_val=0, max_val=1)
                    with engine.If(any_live > 0):
                        with engine.Fori(0, CPB) as k:
                            q = b * CPS + n * CPB + k
                            is_live = ops.value_load(flags[0:1, ds(q, 1)], min_val=0, max_val=1)
                            with engine.If(is_live > 0):
                                chunk(q, b)
                            with engine.Else():
                                skip(1, q)
                            ops.nop()
                        ops.nop()
                    with engine.Else():
                        skip(CPB, b * CPS + n * CPB)
                    ops.nop()

        block = ctx.enter_context(nc.Block())

        @block.sync
        def _(sp):
            for r in range(2):
                sp.sem_inc(x1_stored[r], 16)
                sp.sem_inc(o_stored[r], 16)
            for r in range(2):
                sp.dma_start(xin[:, r], x_rows[r]).then_inc(x_in[r], 16)
                if r == 0:
                    sp.dma_start(win[:], W_in).then_inc(w_first, 16)
                    sp.dma_start(cwb[:].rearrange("p d k -> p (d k)"),
                                 conv_w.rearrange("d a k -> (a d k)").partition_broadcast(P)
                                 ).then_inc(w_first, 16)
            mix_loads = [
                (wx[:], W_x.rearrange("(c p) n -> p c n", p=P)),
                (wdel[:], W_delta),
                (bdel[:], b_delta.rearrange("(c p) -> p c", p=P)),
                (dskip[:], D.rearrange("(c p) -> p c", p=P)),
                (alog[:], A_log.rearrange("(c p) n -> p c n", p=P)),
            ]
            ffn_loads = [
                (wout[:], W_out.rearrange("(c p) n -> p c n", p=P)),
                (gw[:], gate_w), (s1[:], sw1), (s3[:], sw3),
                (s2[:], sw2.rearrange("(h p) n -> p h n", p=SHH)),
            ]
            with nc.allow_non_contiguous_dma(reason="columns of 256 numbers"):
                for dst, src in mix_loads:
                    sp.dma_start(dst, src).then_inc(w_mix, 16)
                for dst, src in ffn_loads:
                    sp.dma_start(dst, src).then_inc(w_ffn, 16)
            with sp.Fori(1, NBLK // 2) as i:
                for r in range(2):
                    sp.wait_ge(x_turned, i * 2 + r - 1)
                    sp.dma_start(xin[:, r], row_block(x_rows, i * 2 + r)).then_inc(x_in[r], 16)
            sp.wait_ge(chunk_done, NCH + 1)
            for r in range(2):
                sp.dma_start(xres[:, r], x_rows[r]).then_inc(xres_in[r], 16)
            sp.dma_start(w13[:, :, 0:EH], w1.rearrange("e p n -> p e n")).then_inc(w_exp, 16)
            sp.dma_start(w13[:, :, EH:2 * EH], w3.rearrange("e p n -> p e n")).then_inc(w_exp, 16)
            with sp.Fori(1, NBLK // 2) as i:
                for r in range(2):
                    sp.wait_ge(res_ready, i * 2 + r + 1)
                    sp.dma_start(xres[:, r], row_block(x_rows, i * 2 + r)).then_inc(xres_in[r], 16)
            sp.wait_ge(yb_ready, NBLK)
            for c in range(EC):
                w = min(P, EH - c * P)
                sp.dma_start(w2s[0:w, :, c, :], w2[:, c * P:c * P + w, :].rearrange("e p n -> p e n")
                             ).then_inc(w_exp, 16)
            with sp.Fori(0, NBLK // 2) as i:
                for r in range(2):
                    sp.wait_ge(x1_ready, i * 2 + r + 1)
                    sp.dma_start(row_block(x1_blocks, i * 2 + r), x1b[:, r]).then_inc(x1_stored[r], 16)
            for r in range(4):
                sp.wait_ge(scattered[r], 16 * (N_TILES // 4))
            with sp.Fori(0, NBLK // 2) as i:
                for r in range(2):
                    sp.wait_ge(fin_read, i * 2 + r + 1)
                    for k, ring in enumerate((y0r, y1r)):
                        sp.dma_start(ring[:, r], row_block(y_blocks[k], i * 2 + r)).then_inc(y_in[r], 16)
            with sp.Fori(0, NBLK // 2) as i:
                for r in range(2):
                    sp.wait_ge(o_ready, i * 2 + r + 1)
                    sp.dma_start(row_block(o_rows, i * 2 + r), outr[:, r]).then_inc(o_stored[r], 16)
            for r in range(2):
                sp.wait_ge(o_stored[r], 16 * (NBLK // 2 + 1))

        @block.gpsimd
        def _(pool):
            g = nc.gpsimd
            own = Steps(pool, pool_step)
            g.memset(xT[:, 0:HALO], 0.0).then_inc(halo, 1)
            g.memset(xT[:, XTW:XTW + HALO], 0.0).then_inc(halo, 1)
            own.settle(g.memset(ones[:], 1.0))
            own.settle(g.memset(ident[:], 0.0))
            g.affine_select(out=ident[:], in_=ident[:], compare_op=ALU.not_equal, fill=1.0, base=0,
                            pattern=[[-1, P]], channel_multiplier=1).then_inc(consts, 1)
            g.affine_select(out=before[:], in_=ones[:], compare_op=ALU.is_gt, fill=0.0, base=0,
                            pattern=[[1, P]], channel_multiplier=-1).then_inc(consts, 1)
            g.iota(iota[:], pattern=[[1, P]], base=0, channel_multiplier=0,
                   allow_small_or_imprecise_dtypes=True).then_inc(consts, 1)
            g.iota(pcol[:], pattern=[[0, 1]], base=0, channel_multiplier=1,
                   allow_small_or_imprecise_dtypes=True).then_inc(consts, 1)
            g.iota(desc[:], pattern=[[-1, E]], base=E, channel_multiplier=0,
                   allow_small_or_imprecise_dtypes=True).then_inc(consts, 1)
            g.iota(tcol[:], pattern=[[1, K * TILES]], base=0, channel_multiplier=0,
                   allow_small_or_imprecise_dtypes=True).then_inc(consts, 1)
            g.memset(zer[:], 0.0).then_inc(consts, 1)
            g.memset(idx_src[:], 0).then_inc(consts, 1)
            g.memset(idx_dst[:], NO_ROW).then_inc(consts, 1)
            g.memset(epst[:, 0:1], LN_EPS).then_inc(consts, 1)
            g.memset(epst[:, 1:2], NEG_LN_SCAN_EPS).then_inc(consts, 1)
            g.memset(epst[:, 2:3], 1.0).then_inc(consts, 1)
            g.iota(tex[:], pattern=[[1, IDXC], [0, E]], base=0, channel_multiplier=0,
                   allow_small_or_imprecise_dtypes=True).then_inc(consts, 1)

            def chunk(q, b):
                col0 = q * CH
                pool.wait_ge(chunk_done, q + 1)
                for c in range(DC):
                    ins = g.tensor_tensor(decay[:, c],
                                          dl_all[:, c, ds(col0, CH)].unsqueeze(1).to_broadcast([P, NST, CH]),
                                          aneg[:, c, :].unsqueeze(2).to_broadcast([P, NST, CH]), ALU.mult)
                ins.then_inc(za_raw, 1)
                pool.wait_ge(za_raw, q + 1)
                hold(pool, pool_held)
                g.tensor_scalar(decay[:], decay[:], 0.0, FLOOR / A_UNIT, ALU.min, ALU.max).then_inc(za_ready, 1)
                pool.wait_ge(r_ready, q + 1)
                for c in range(DC):
                    ins = g.tensor_tensor(gain[:, c],
                                          rch[:, c, :].unsqueeze(1).to_broadcast([P, NST, CH]),
                                          aneg[:, c, :].unsqueeze(2).to_broadcast([P, NST, CH]), ALU.mult)
                ins.then_inc(zr_raw, 1)
                pool.wait_ge(zr_raw, q + 1)
                hold(pool, pool_held)
                g.tensor_scalar(gain[:], gain[:], 0.0, FLOOR / A_UNIT, ALU.min, ALU.max).then_inc(zr_ready, 1)
                pool.wait_ge(zr_ready, q + 1)
                hold(pool, pool_held)

            def skip(n, q):
                pool.sem_inc(za_raw, n)
                pool.sem_inc(zr_raw, n)
                pool.sem_inc(za_ready, n)
                pool.sem_inc(zr_ready, n)

            pool.wait_ge(flags_ready, 1)
            chunk_loops(pool, g, chunk, skip)

            pool.wait_ge(chunk_done, NCH + 1)
            with pool.Fori(0, NBLK // 2) as i:
                for r in range(2):
                    pool.wait_ge(mix_sum, i * 2 + r + 1)
                    g.tensor_copy(ybuf[:, r], y_all[:, :, ds(i * 2 * BLK + r * BLK, BLK)]
                                  ).then_inc(yb_ready, 1)

            def gather(slot_, half_ring, j):
                hold(pool, pool_held)
                g.indirect_dma_start(xg[:, slot_], None, x1_rows,
                                     bass.IndirectOffsetOnAxis(ap=ring_src[:, half_ring, j:j + 1].bitcast(U32), axis=0)
                                     ).then_inc(gathered[slot_], 16)

            for r in range(2):
                pool.wait_ge(x1_stored[r], 16 * (NBLK // 2 + 1))
            pool.wait_ge(src_ready, 1)
            for t in range(3):
                gather(t, 0, t)
            with pool.Fori(0, N_TILES // 8) as i:
                for k in range(1, 9):
                    ahead = k + 2
                    if ahead % HALF == 0 or k == 1:
                        pool.wait_ge(src_ready, i * 2 + ahead // HALF + 1)
                    pool.wait_ge(e_turned, i * 8 + k)
                    gather(ahead % 4, (ahead // HALF) % 2, ahead % HALF)
                    behind = k - 1
                    if behind % HALF == 0:
                        pool.wait_ge(dst_ready, i * 2 + behind // HALF + 1)
                    pool.wait_ge(e_out, i * 8 + k + 2)
                    hold(pool, pool_held)
                    g.indirect_dma_start(y_rows,
                                         bass.IndirectOffsetOnAxis(ap=ring_dst[:, (behind // HALF) % 2, behind % HALF:behind % HALF + 1].bitcast(U32), axis=0),
                                         yo[:, behind % 4], None, bounds_check=K * TOK - 1, oob_is_err=False
                                         ).then_inc(scattered[behind % 4], 16)
            for r, last in ((1, N_TILES // 4 + 1), (2, N_TILES // 4 + 1)):
                pool.wait_ge(gathered[r], 16 * last)

        @block.scalar
        def _(act):
            s = nc.scalar
            act.sem_inc(u_ready, 2)
            act.sem_inc(g_ready, 2)
            act.sem_inc(x1T_ready, 1)
            act.sem_inc(e_out, 2)
            with act.Fori(0, NBLK // 2) as i:
                for r in range(2):
                    cols = ds(i * 2 * BLK + r * BLK, BLK)
                    for c in range(DC):
                        act.wait_ge(u_sum, i * 4 + 2 * r + c + 1)
                        s.activation(u_all[:, c, cols], ps[:, c], ACT.Silu).then_inc(u_ready, 1)
                    for c in range(DC):
                        act.wait_ge(g_sum, i * 4 + 2 * r + c + 1)
                        s.activation(y_all[:, c, cols], ps[:, 2 + c], ACT.Silu).then_inc(g_ready, 1)
            act.wait_ge(alog_ready, 1)
            act.wait_ge(consts, 13)
            s.activation(aneg[:], alog[:], ACT.Exp).then_inc(a_exp, 1)
            with act.Fori(0, NBLK // 2) as i:
                for r in range(2):
                    act.wait_ge(pd_sum, i * 2 + r + 1)
                    act.wait_ge(dl_ready, i * 2 + r + 1)
                    for c in range(DC):
                        s.activation(z_buf[:, r, c], ps[:, 2 * r + c], ACT.Exp,
                                     bias=bdel[:, c:c + 1]).then_inc(z_ready, 1)
                for r in range(2):
                    act.wait_ge(z_clamped, i * 2 + r + 1)
                    s.activation(ln_buf[:, r], z_buf[:, r], ACT.Ln, bias=epst[:, 2:3]).then_inc(ln_ready, 1)

            def chunk(q, b):
                act.wait_ge(za_ready, q + 1)
                s.activation(decay[:], decay[:], ACT.Exp, scale=A_UNIT).then_inc(decay_ready, 1)
                act.wait_ge(zr_ready, q + 1)
                act.wait_ge(bc_sum, q + 1)
                s.activation(gch[:], ps[:, 2, 0:DC * CH].rearrange("p (c t) -> p c t", c=DC), ACT.Sigmoid)
                s.activation(gain[:], gain[:], ACT.Sigmoid, bias=epst[:, 1:2],
                             scale=A_UNIT).then_inc(gain_ready, 1)
                act.wait_ge(gain_ready, q + 1)
                hold(act, act_held)

            def skip(n, q):
                act.sem_inc(decay_ready, n)
                act.sem_inc(gain_ready, n)

            act.wait_ge(flags_ready, 1)
            chunk_loops(act, s, chunk, skip)
            act.wait_ge(mv_ready, 1)
            s.activation(rstd[:], mv[:, :, 1], ACT.Sqrt, bias=epst[:, 0:1]).then_inc(std_ready, 1)
            with act.Fori(0, NBLK // 2) as i:
                for r in range(2):
                    act.wait_ge(x1_turned, i * 2 + r + 3)
                    s.copy(x1T[:, r], ps[:, 2]).then_inc(x1T_ready, 1)
                for r in range(2):
                    for h in range(2):
                        act.wait_ge(sh_a, i * 4 + 2 * r + h + 1)
                        act.wait_ge(sh_h, i * 4 + 2 * r + h + 1)
                        s.activation(sgate[:, h], ps[0:SHH, 4 + h], ACT.Silu).then_inc(sh_silu, 1)
            act.wait_ge(lgx_ready, 1)
            s.activation(sc[:], t3[:], ACT.Exp).then_inc(sce_ready, 1)
            act.wait_ge(e_a, 1)
            s.activation(egate, ps[:, 0, 0:EH], ACT.Silu).then_inc(e_silu, 1)

            def eight_tiles(i, first):
                for k in range(1, 9):
                    act.wait_ge(e_a, i * 8 + k + 1)
                    s.activation(egate, ps[:, 0, 0:EH], ACT.Silu).then_inc(e_silu, 1)
                    behind = k - 1
                    act.wait_ge(e_sum, i * 8 + k)
                    if behind >= 4 or not first:
                        act.wait_ge(scattered[behind % 4], 16 * (i * 2 + behind // 4))
                    s.copy(yo[:, behind % 4], ps[:, 4 + behind % 2, 0:DM]).then_inc(e_out, 1)

            eight_tiles(0, True)
            with act.Fori(1, N_TILES // 8) as i:
                eight_tiles(i, False)
            act.wait_ge(fmv_ready, 1)
            s.activation(rstd[:], mv[:, :, 1], ACT.Sqrt, bias=epst[:, 0:1]).then_inc(fstd_ready, 1)

        @block.tensor
        def _(pe):
            t = nc.tensor
            pe.sem_inc(mix_sum, 2)
            pe.sem_inc(x1_turned, 2)
            pe.sem_inc(oh_sum, 2)
            pe.wait_ge(consts, 1)
            with pe.Fori(0, NBLK // 2) as i:
                for r in range(2):
                    pe.wait_ge(x_in[r], 16 * (i + 1))
                    pe.wait_ge(xT_ready, i * 2 + r + 1)
                    for j in range(TPB):
                        last = t.transpose(ps[:, 6 + r, j * P:(j + 1) * P], xin[:, r, j], ident[:])
                    last.then_inc(x_turned, 1)
            pe.wait_ge(wk_ready, TAPS)
            pe.wait_ge(halo, 2)
            pe.wait_ge(w_mix, 16 * 5)
            with pe.Fori(0, BATCH) as b:
                with pe.Fori(0, BPS // 2) as h:
                    for r in range(2):
                        n = b * BPS + h * 2 + r
                        base = b * XTW + h * (2 * BLK) + r * BLK
                        pe.wait_ge(xT_ready, n + 3)
                        for c in range(DC):
                            pe.wait_ge(u_ready, n * 2 + c + 1)
                            for k in range(TAPS):
                                last = t.matmul(ps[:, c], wk[:, k, c * P:(c + 1) * P], xT[:, ds(base + k, BLK)],
                                                start=(k == 0), stop=(k == TAPS - 1))
                            last.then_inc(u_sum, 1)
                        for c in range(DC):
                            pe.wait_ge(g_ready, n * 2 + c + 1)
                            t.matmul(ps[:, 2 + c], win[:, DIN + c * P:DIN + (c + 1) * P],
                                     xT[:, ds(base + HALO, BLK)], start=True, stop=True).then_inc(g_sum, 1)
                        pe.wait_ge(u_ready, n * 2 + 4)
                        pe.wait_ge(xd_ready, n * 2 + 2)
                        for c in range(DC):
                            last = t.matmul(ps[0:RANK + 2 * NST, 4], wx[:, c], u_all[:, c, ds(n * BLK, BLK)],
                                            start=(c == 0), stop=(c == DC - 1))
                        last.then_inc(xd_sum, 1)
            pe.wait_ge(g_ready, 2 * NBLK + 2)
            pe.wait_ge(xd_ready, 2 * NBLK + 2)
            with pe.Fori(0, NBLK // 2) as i:
                for r in range(2):
                    pe.wait_ge(dl_ready, i * 2 + r + 1)
                    for c in range(DC):
                        last = t.matmul(ps[:, 2 * r + c], wdel[:, c * P:(c + 1) * P],
                                        xdl[:, ds(i * 2 * BLK + r * BLK, BLK)], start=True, stop=True)
                    last.then_inc(pd_sum, 1)
            pe.wait_ge(live_ready, 1)
            t.matmul(ps[0:1, 4, 0:DC * NCH], ones[:, 0:1], live[:].rearrange("p c q -> p (c q)"),
                     start=True, stop=True).then_inc(live_sum, 1)

            def chunk(q, b):
                xcol = q * CH + b * HALO + HALO
                pe.wait_ge(chunk_done, q + 1)
                for half in range(2):
                    for n in range(NST):
                        row = half * NST + n
                        last = t.matmul(ps[:, 4 + 2 * half + n // 8, (n % 8) * CH:(n % 8 + 1) * CH],
                                        ident[0:2 * NST, row:row + 1].to_broadcast([2 * NST, P]),
                                        bc[:, ds(q * CH, CH)], start=True, stop=True)
                for c in range(DC):
                    last = t.matmul(ps[:, 2, c * CH:(c + 1) * CH], win[:, DIN + c * P:DIN + (c + 1) * P],
                                    xT[:, ds(xcol, CH)], start=True, stop=True)
                last.then_inc(bc_sum, 1)
                pe.wait_ge(bc_sum, q + 1)

            def skip(n, q):
                pe.sem_inc(bc_sum, n)

            pe.wait_ge(flags_ready, 1)
            chunk_loops(pe, t, chunk, skip)

            pe.wait_ge(w_ffn, 16 * 5)
            with pe.Fori(0, NBLK // 2) as i:
                for r in range(2):
                    pe.wait_ge(yb_ready, i * 2 + r + 1)
                    pe.wait_ge(res_ready, i * 2 + r + 1)
                    for j in range(TPB):
                        for c in range(DC):
                            last = t.matmul(ps[:, r, j * P:(j + 1) * P], ybuf[:, r, c, j * P:(j + 1) * P],
                                            wout[:, c], start=(c == 0), stop=(c == DC - 1))
                    last.then_inc(mix_sum, 1)
            t.transpose(ps[:, 3, 0:E], gw[:], ident[0:E, 0:E]).then_inc(gwT_sum, 1)
            pe.wait_ge(gwT_ready, 1)
            pe.wait_ge(res_ready, NBLK + 2)
            with pe.Fori(0, NBLK // 2) as i:
                for r in range(2):
                    pe.wait_ge(x1_ready, i * 2 + r + 1)
                    pe.wait_ge(x1T_ready, i * 2 + r + 1)
                    for j in range(TPB):
                        last = t.transpose(ps[:, 2, j * P:(j + 1) * P], x1b[:, r, j], ident[:])
                    last.then_inc(x1_turned, 1)
                for r in range(2):
                    pe.wait_ge(x1T_ready, i * 2 + r + 2)
                    pe.wait_ge(lg_ready, i * 2 + r + 1)
                    for j in range(TPB):
                        last = t.matmul(ps[:, 3, j * E:(j + 1) * E], x1T[:, r, j * P:(j + 1) * P], gwT[:],
                                        start=True, stop=True)
                    last.then_inc(gate_sum, 1)
                    for h in range(2):
                        pe.wait_ge(sh_h, i * 4 + 2 * r + h + 1)
                        t.matmul(ps[0:SHH, 4 + h], s1[:, h * SHH:(h + 1) * SHH], x1T[:, r],
                                 start=True, stop=True).then_inc(sh_a, 1)
                        t.matmul(ps[0:SHH, 6 + h], s3[:, h * SHH:(h + 1) * SHH], x1T[:, r],
                                 start=True, stop=True).then_inc(sh_c, 1)
                for r in range(2):
                    pe.wait_ge(sh_h, i * 4 + 2 * r + 4)
                    pe.wait_ge(acc_ready, i * 2 + r + 1)
                    for j in range(TPB):
                        for h in range(2):
                            last = t.matmul(ps[:, r, j * P:(j + 1) * P], shT[:, r, h, j * P:(j + 1) * P],
                                            s2[:, h], start=(h == 0), stop=(h == 1))
                    last.then_inc(sh_sum, 1)
            pe.wait_ge(m_ready, 1)
            t.matmul(ps[:, 4, 0:TILES * E], before[:], rk[:].rearrange("p t e -> p (t e)"), start=True, stop=True)
            t.matmul(ps[:, 5, 0:TILES * E], ones[:], rk[:].rearrange("p t e -> p (t e)"),
                     start=True, stop=True).then_inc(rank_sum, 1)
            pe.wait_ge(lg_ready, NBLK + 1)
            t.matmul(ps[:, 3, 0:3 * N_TILES], zer[:, 0:P], zer[:], start=True, stop=False,
                     skip_group_check=True)
            with pe.Fori(0, TILES) as i:
                for k in range(K):
                    pe.wait_ge(oh_ready, i * 2 + k + 1)
                    t.matmul(ps[:, 3, 0:3 * N_TILES], ohl[:, k], ohh[:, k].rearrange("p a n -> p (a n)"),
                             start=False, stop=False, skip_group_check=True).then_inc(oh_sum, 1)
            t.matmul(ps[:, 3, 0:3 * N_TILES], zer[:, 0:P], zer[:], start=False, stop=True,
                     skip_group_check=True).then_inc(oh_sum, 1)

            def turn_rows(slot_, landed, freed):
                pe.wait_ge(gathered[slot_], landed)
                if freed is not None:
                    pe.wait_ge(eT_ready, freed)
                t.transpose(ps[:, 2, 0:P], xg[:, slot_], ident[:]).then_inc(e_turned, 1)

            def hidden(par, expert, turned):
                pe.wait_ge(eT_ready, turned)
                t.matmul(ps[:, 0, 0:EH], xgT[:, par], w13[:, ds(expert, 1), 0:EH].rearrange("p a n -> p (a n)"),
                         start=True, stop=True).then_inc(e_a, 1)
                t.matmul(ps[:, 1, 0:EH], xgT[:, par], w13[:, ds(expert, 1), EH:2 * EH].rearrange("p a n -> p (a n)"),
                         start=True, stop=True).then_inc(e_c, 1)

            pe.wait_ge(texi_ready, 1)
            pe.wait_ge(w_exp, 16 * (2 + EC))
            pe.wait_ge(acc_ready, NBLK + 2)
            expert_of = [t.value_load(texi[0:1, 0:1], min_val=0, max_val=E - 1)]
            turn_rows(0, 16, None)
            turn_rows(1, 16, 1)
            hidden(0, expert_of[0], 1)
            with pe.Fori(0, N_TILES // 8) as i:
                for k in range(1, 9):
                    now = t.value_load(texi[0:1, ds(i * 8 + k, 1)], min_val=0, max_val=E - 1)
                    was = t.value_load(texi[0:1, ds(i * 8 + (k - 1), 1)], min_val=0, max_val=E - 1)
                    turn_rows((k + 1) % 4, 16 * (i * 2 + (k + 1) // 4 + 1), i * 8 + k + 1)
                    pe.wait_ge(e_h, i * 8 + k)
                    for c in range(EC):
                        w = min(P, EH - c * P)
                        last = t.transpose(ps[0:w, 3, c * P:(c + 1) * P], eh[:, c * P:c * P + w], ident[:])
                    last.then_inc(eh_turned, 1)
                    hidden(k % 2, now, i * 8 + k + 1)
                    pe.wait_ge(ehT_ready, i * 16 + 2 * k)
                    pe.wait_ge(e_out, i * 8 + k)
                    for c in range(EC):
                        w = min(P, EH - c * P)
                        last = t.matmul(ps[:, 4 + (k - 1) % 2, 0:DM], ehT[0:w, c],
                                        w2s[0:w, ds(was, 1), c, :].rearrange("p a n -> p (a n)"),
                                        start=(c == 0), stop=(c == EC - 1))
                    last.then_inc(e_sum, 1)

        @block.vector
        def _(dve):
            v = nc.vector
            own = Steps(dve, dve_step)

            def loop(count, per):
                return SteppedLoop(dve, own, count, per)

            dve.sem_inc(xT_ready, 2)
            dve.sem_inc(xd_ready, 2)
            dve.sem_inc(dl_ready, 2)
            dve.sem_inc(chunk_done, 1)
            dve.sem_inc(res_ready, 2)
            dve.sem_inc(sh_h, 2)
            dve.sem_inc(lg_ready, 1)
            dve.sem_inc(acc_ready, 2)
            dve.sem_inc(fin_read, 2)
            dve.wait_ge(w_first, 32)
            for k in range(TAPS):
                v.tensor_tensor(wk[:, k], win[:, 0:DIN], cwb[:, :, k], ALU.mult).then_inc(wk_ready, 1)
            with dve.Fori(0, BATCH) as b:
                with dve.Fori(0, BPS // 2) as h:
                    for r in range(2):
                        n = b * BPS + h * 2 + r
                        dve.wait_ge(x_turned, n + 1)
                        v.tensor_copy(xT[:, ds(b * XTW + h * (2 * BLK) + (r * BLK + HALO), BLK)], ps[:, 6 + r]
                                      ).then_inc(xT_ready, 1)
            dve.wait_ge(w_mix, 16 * 5)
            v.tensor_scalar(alog[:], alog[:], MAX_EXP, None, ALU.min).then_inc(alog_ready, 1)
            with dve.Fori(0, NBLK // 2) as i:
                for r in range(2):
                    cols = ds(i * 2 * BLK + r * BLK, BLK)
                    dve.wait_ge(xd_sum, i * 2 + r + 1)
                    v.tensor_copy(xdl[:, cols], ps[0:RANK, 4]).then_inc(xd_ready, 1)
                    v.tensor_copy(bc[:, cols], ps[RANK:RANK + 2 * NST, 4]).then_inc(xd_ready, 1)
                    dve.wait_ge(u_ready, i * 4 + 2 * r + 4)
                    dve.wait_ge(g_ready, i * 4 + 2 * r + 4)
                    for c in range(DC):
                        v.scalar_tensor_tensor(out=y_all[:, c, cols], in0=u_all[:, c, cols],
                                               scalar=dskip[:, c:c + 1], in1=y_all[:, c, cols],
                                               op0=ALU.mult, op1=ALU.mult).then_inc(y_ready, 1)
            csum_n = csum[:].rearrange("p c b q -> p c (b q)")
            per = 2 * 5
            with loop(NBLK // 2, per) as i:
                for r in range(2):
                    dve.wait_ge(z_ready, i * 4 + 2 * r + 2)
                    zr = z_buf[:, r].rearrange("p c t -> p (c t)")
                    v.tensor_scalar(zr, zr, float(2 ** 40), None, ALU.min).then_inc(z_clamped, 1)
                    dve.wait_ge(z_clamped, i * 2 + r + 1)
                    own.settle(v.scalar_tensor_tensor(out=sq_buf[:, r].rearrange("p c t -> p (c t)"), in0=zr,
                                                      scalar=2.0, in1=zr, op0=ALU.subtract, op1=ALU.mult))
                for r in range(2):
                    cols = ds(i * 2 * BLK + r * BLK, BLK)
                    zr = z_buf[:, r].rearrange("p c t -> p (c t)")
                    lr = ln_buf[:, r].rearrange("p c t -> p (c t)")
                    sr = sq_buf[:, r].rearrange("p c t -> p (c t)")
                    dve.wait_ge(ln_ready, i * 2 + r + 1)
                    own.settle(v.scalar_tensor_tensor(out=lr, in0=zr, scalar=SOFT_CUT, in1=lr,
                                                      op0=ALU.is_ge, op1=ALU.mult))
                    own.settle(v.scalar_tensor_tensor(out=sr, in0=sr, scalar=-0.5, in1=lr,
                                                      op0=ALU.mult, op1=ALU.max))
                    own.settle(v.scalar_tensor_tensor(out=dl_all[:, 0, cols], in0=ps[:, 2 * r],
                                                      scalar=bdel[:, 0:1], in1=sq_buf[:, r, 0],
                                                      op0=ALU.add, op1=ALU.max))
                    v.scalar_tensor_tensor(out=dl_all[:, 1, cols], in0=ps[:, 2 * r + 1],
                                           scalar=bdel[:, 1:2], in1=sq_buf[:, r, 1],
                                           op0=ALU.add, op1=ALU.max).then_inc(dl_ready, 1)
                    dve.wait_ge(dl_ready, i * 2 + r + 3)
                    own.settle(v.tensor_reduce(csum_n[:, :, ds(i * 2 * CPB + r * CPB, CPB)],
                                               dl_all[:, :, cols].rearrange("p c (q t) -> p c q t", t=CH),
                                               AX.X, ALU.add))
            dve.wait_ge(a_exp, 1)
            own.settle(v.tensor_scalar(aneg[:], aneg[:], -1.0 / A_UNIT, None, ALU.mult))
            own.settle(v.tensor_reduce(amax[:], aneg[:], AX.X, ALU.max))
            own.settle(v.memset(rend[:, :, :, CPS - 1:CPS], 0.0))
            dve.wait_ge(consts, 13)
            for c in range(DC):
                for b in range(BATCH):
                    own.settle(v.tensor_tensor_scan(rend[:, c, b, CPS - 2::-1], ones[:, 0:CPS - 1],
                                                    csum[:, c, b, CPS - 1:0:-1], 0.0, ALU.mult, ALU.add))
            own.settle(v.tensor_tensor(live[:], rend[:].rearrange("p c b q -> p c (b q)"),
                                       amax[:].unsqueeze(2).to_broadcast([P, DC, NCH]), ALU.mult))
            v.tensor_scalar(live[:], live[:], DEAD / A_UNIT, None, ALU.is_ge).then_inc(live_ready, 1)
            dve.wait_ge(live_sum, 1)
            pf = ps[0:1, 4, 0:DC * NCH].rearrange("p (c q) -> p q c", c=DC)
            own.settle(v.tensor_reduce(flagf[:], pf, AX.X, ALU.max))
            v.tensor_scalar(flags[:], flagf[:], 1.0, None, ALU.min).then_inc(flags_ready, 1)
            dve.wait_ge(flags_ready, 1)

            STEPS_PER_CHUNK = 2 * 2 + 3 + DC * 11

            def chunk(q):
                col0 = q * CH
                dve.wait_ge(chunk_done, q + 1)
                rend_q = rend[:].rearrange("p c b q -> p c (b q)")
                own.settle(v.tensor_copy(dch[:], dl_all[:, :, ds(col0, CH)]))
                for c in range(DC):
                    own.settle(v.tensor_copy(rch[:, c, CH - 1:CH], rend_q[:, c, ds(q, 1)]))
                for c in range(DC):
                    own.settle(v.tensor_tensor_scan(rch[:, c, CH - 2::-1], ones[:, 0:CH - 1],
                                                    dch[:, c, CH - 1:0:-1],
                                                    rch[:, c, CH - 1:CH], ALU.mult, ALU.add))
                v.nop().then_inc(r_ready, 1)
                own.settle(v.tensor_tensor(du[:], dch[:], u_all[:, :, ds(col0, CH)], ALU.mult))
                dve.wait_ge(bc_sum, q + 1)
                dve.wait_ge(decay_ready, q + 1)
                for c in range(DC):
                    bvals = ps[:, 4:6].rearrange("p a (n t) -> p (a n) t", t=CH)
                    cvals = ps[:, 6:8].rearrange("p a (n t) -> p (a n) t", t=CH)
                    own.settle(v.tensor_tensor(dbu, bvals, du[:, c, :].unsqueeze(1).to_broadcast([P, NST, CH]), ALU.mult))
                    own.settle(v.tensor_tensor(hmul[:], decay[:, c, :, 0], hcar[:, c], ALU.mult))
                    own.settle(v.tensor_tensor(dbu[:, :, 0], dbu[:, :, 0], hmul[:], ALU.add))
                    own.settle(v.memset(decay[:, c, :, 0], 0.0))
                    own.settle(v.tensor_tensor_scan(scratch[:, 5, :], decay[:, c].rearrange("p n t -> p (n t)"),
                                                    scratch[:, 4, :], 0.0, ALU.mult, ALU.add))
                    own.settle(v.tensor_copy(hcar[:, c], hs[:, :, CH - 1]))
                    if c == 0:
                        dve.wait_ge(gain_ready, q + 1)
                        own.settle(v.tensor_tensor(gch[:], gch[:], ps[:, 2, 0:DC * CH].rearrange(
                            "p (c t) -> p c t", c=DC), ALU.mult))
                    own.settle(v.tensor_tensor(scratch[:, 5, :], scratch[:, 5, :],
                                               gain[:, c].rearrange("p n t -> p (n t)"), ALU.mult))
                    own.settle(v.tensor_tensor(hs, cvals, hs, ALU.mult))
                    own.settle(v.tensor_reduce(ysum[:], hs.rearrange("p n t -> p t n"), AX.X, ALU.add))
                    own.settle(v.tensor_tensor(ysum[:], ysum[:], gch[:, c], ALU.mult))
                    own.settle(v.tensor_tensor(y_all[:, c, ds(col0, CH)], y_all[:, c, ds(col0, CH)], ysum[:], ALU.add))
                v.nop().then_inc(chunk_done, 1)

            def skip(n, q):
                own.count, own.shift = start, q * STEPS_PER_CHUNK
                own.settle(v.memset(hcar[:], 0.0))
                own.count, own.shift = start, 0
                dve.sem_inc(r_ready, n)
                dve.sem_inc(dve_step, n * STEPS_PER_CHUNK - 1)
                dve.sem_inc(chunk_done, n)

            start = own.count

            def counted(q, b):
                own.count, own.shift = start, q * STEPS_PER_CHUNK
                chunk(q)
                assert own.count == start + STEPS_PER_CHUNK, own.count - start
                own.count, own.shift = start, 0

            def start_batch(b):
                v.memset(hcar[:], 0.0).then_inc(batch_start, 1)
                dve.wait_ge(batch_start, b + 1)
                hold(dve, dve_held)

            dve.wait_ge(y_ready, DC * NBLK)
            chunk_loops(dve, v, counted, skip, start_batch)
            own.count = start + NCH * STEPS_PER_CHUNK

            def statistics(rows, r):
                hold(dve, dve_held)
                for j in range(TPB):
                    last = v.bn_stats(bst[:, r, j], rows(j))
                own.settle(last)
                hold(dve, dve_held)
                for j in range(TPB):
                    last = v.bn_aggr(bag[:, r, j], bst[:, r, j])
                own.settle(last)

            with loop(NBLK // 2, 2 * (2 + 1)) as i:
                for r in range(2):
                    tiles = ds(i * 2 * TPB + r * TPB, TPB)
                    dve.wait_ge(mix_sum, i * 2 + r + 3)
                    dve.wait_ge(xres_in[r], 16 * (i + 1))
                    v.tensor_tensor(res1[:, tiles, :], ps[:, r].rearrange("p (i d) -> p i d", d=DM), xres[:, r],
                                    ALU.add).then_inc(res_ready, 1)
                    dve.wait_ge(res_ready, i * 2 + r + 3)
                    statistics(lambda j: res1[:, ds(i * 2 * TPB + (r * TPB + j), 1), :].rearrange("p a d -> p (a d)"), r)
                    own.settle(v.tensor_copy(mv[:, tiles, :], bag[:, r]))
            v.nop().then_inc(mv_ready, 1)
            dve.wait_ge(std_ready, 1)
            own.settle(v.reciprocal(rstd[:], rstd[:]))
            dve.wait_ge(gwT_sum, 1)
            v.tensor_copy(gwT[:], ps[:, 3, 0:E]).then_inc(gwT_ready, 1)

            with dve.Fori(0, NBLK // 2) as i:
                for r in range(2):
                    dve.wait_ge(x1_stored[r], 16 * (i + 1))
                    dve.wait_ge(x1_turned, i * 2 + r + 1)
                    dve.wait_ge(acc_ready, i * 2 + r + 1)
                    for j in range(TPB):
                        tile = i * 2 * TPB + (r * TPB + j)
                        last = v.tensor_scalar(x1b[:, r, j], res1[:, ds(tile, 1), :].rearrange("p a d -> p (a d)"),
                                               mv[:, ds(tile, 1), 0], rstd[:, ds(tile, 1)],
                                               ALU.subtract, ALU.mult)
                    last.then_inc(x1_ready, 1)
                for r in range(2):
                    for h in range(2):
                        m = i * 4 + 2 * r + h
                        dve.wait_ge(sh_silu, m + 1)
                        dve.wait_ge(sh_c, m + 1)
                        v.tensor_tensor(shT[:, r, h], ps[0:SHH, 6 + h], sgate[:, h], ALU.mult).then_inc(sh_h, 1)
                    dve.wait_ge(gate_sum, i * 2 + r + 1)
                    v.tensor_copy(lg[:, ds(i * 2 * TPB + r * TPB, TPB), :],
                                  ps[:, 3, 0:TPB * E].rearrange("p (i e) -> p i e", e=E)).then_inc(lg_ready, 1)
                for r in range(2):
                    dve.wait_ge(sh_sum, i * 2 + r + 1)
                    dve.wait_ge(x1_ready, i * 2 + r + 1)
                    v.tensor_tensor(acc[:, ds(i * 2 * TPB + r * TPB, TPB), :],
                                    ps[:, r].rearrange("p (i d) -> p i d", d=DM), x1b[:, r],
                                    ALU.add).then_inc(acc_ready, 1)

            def over_e(a):
                return a.unsqueeze(2).to_broadcast([P, TILES, E])

            def over_t(a):
                return a.unsqueeze(1).to_broadcast([P, TILES, E])

            dve.wait_ge(lg_ready, NBLK + 1)
            own.settle(v.tensor_reduce(col[:], lg[:], AX.X, ALU.max))
            v.tensor_tensor(t3[:], lg[:], over_e(col[:]), ALU.subtract).then_inc(lgx_ready, 1)
            dve.wait_ge(sce_ready, 1)
            own.settle(v.tensor_reduce(col[:], sc[:], AX.X, ALU.add))
            own.settle(v.reciprocal(col[:], col[:]))
            own.settle(v.tensor_tensor(sc[:], sc[:], over_e(col[:]), ALU.mult))
            for k, m in enumerate((m1, m2)):
                own.settle(v.tensor_reduce(wk2[:, k], sc[:], AX.X, ALU.max))
                own.settle(v.tensor_tensor(t3[:], sc[:], over_e(wk2[:, k]), ALU.is_equal))
                own.settle(v.tensor_tensor(t3[:], t3[:], over_t(desc[:]), ALU.mult))
                own.settle(v.tensor_reduce(col[:], t3[:], AX.X, ALU.max))
                own.settle(v.tensor_tensor(m[:], t3[:], over_e(col[:]), ALU.is_equal))
                if k == 0:
                    own.settle(v.scalar_tensor_tensor(out=sc[:].rearrange("p t e -> p (t e)"),
                                                      in0=m1[:].rearrange("p t e -> p (t e)"), scalar=-2.0,
                                                      in1=sc[:].rearrange("p t e -> p (t e)"),
                                                      op0=ALU.mult, op1=ALU.add))
            v.tensor_tensor(rk[:], m1[:], m2[:], ALU.add).then_inc(m_ready, 1)
            dve.wait_ge(rank_sum, 1)
            within = ps[:, 4, 0:TILES * E].rearrange("p (t e) -> p t e", e=E)
            totals = ps[:, 5, 0:TILES * E].rearrange("p (t e) -> p t e", e=E)
            own.settle(v.memset(ex[:, 0, :], 0.0))
            for e in range(E):
                own.settle(v.tensor_tensor_scan(ex[:, 1:TILES, e], ones[:, 0:TILES - 1], totals[:, 0:TILES - 1, e],
                                                0.0, ALU.mult, ALU.add))
            own.settle(v.tensor_tensor(cnt[:], totals[:, TILES - 1, :], ex[:, TILES - 1, :], ALU.add))
            own.settle(v.tensor_scalar(cnti[:], cnt[:], float(P - 1), None, ALU.add))
            own.settle(v.tensor_scalar(nti[:], cnti[:], 7, None, ALU.logical_shift_right))
            own.settle(v.tensor_copy(ntf[:], nti[:]))
            own.settle(v.tensor_tensor_scan(tend[:], ones[:, 0:E], ntf[:], 0.0, ALU.mult, ALU.add))
            own.settle(v.tensor_tensor(tbeg[:], tend[:], ntf[:], ALU.subtract))
            own.settle(v.tensor_scalar(tbeg[:], tbeg[:], float(P), None, ALU.mult))
            own.settle(v.tensor_tensor(ex[:], within, ex[:], ALU.add))
            own.settle(v.tensor_tensor(ex[:], ex[:], over_t(tbeg[:]), ALU.add))
            for k, m in enumerate((m1, m2)):
                own.settle(v.tensor_tensor(t3[:], m[:], ex[:], ALU.mult))
                own.settle(v.tensor_reduce(slot[:, k], t3[:], AX.X, ALU.add))
            own.settle(v.tensor_copy(sloti[:], slot[:]))
            own.settle(v.tensor_scalar(hii[:], sloti[:], 7, None, ALU.logical_shift_right))
            own.settle(v.tensor_scalar(loi[:], sloti[:], P - 1, None, ALU.bitwise_and))
            own.settle(v.tensor_copy(hif[:], hii[:]))
            own.settle(v.tensor_copy(lof[:], loi[:]))
            own.settle(v.tensor_tensor(tex[:], tex[:], tend[0:1, :].unsqueeze(1).to_broadcast([1, IDXC, E]), ALU.is_ge))
            own.settle(v.tensor_reduce(texs[:], tex[:], AX.X, ALU.add))
            v.tensor_scalar(texi[:], texs[:], float(E - 1), None, ALU.min).then_inc(texi_ready, 1)
            with dve.Fori(0, TILES) as i:
                for k in range(K):
                    dve.wait_ge(oh_sum, i * 2 + k + 1)
                    v.tensor_scalar(ohl[:, k], iota[:], lof[:, k, ds(i, 1)], None, ALU.is_equal)
                    hi = hif[:, k, ds(i, 1)]
                    v.tensor_scalar(ohh[:, k, 0], iota[:, 0:N_TILES], hi, None, ALU.is_equal)
                    v.tensor_scalar(ohh[:, k, 1], iota[:, 0:N_TILES], hi, pcol[:], ALU.is_equal, ALU.mult)
                    v.tensor_scalar(ohh[:, k, 2], iota[:, 0:N_TILES], hi, tcol[:, ds(i + k * TILES, 1)],
                                    ALU.is_equal, ALU.mult).then_inc(oh_ready, 1)
            dve.wait_ge(oh_sum, K * TILES + 3)
            own.settle(v.tensor_copy(pid[:], ps[:, 3, 0:3 * N_TILES].rearrange("p (a n) -> p a n", a=3)))
            own.settle(v.scalar_tensor_tensor(out=tokf[:], in0=pid[:, 2], scalar=float(P), in1=pid[:, 1],
                                              op0=ALU.mult, op1=ALU.add))
            own.settle(v.tensor_copy(toki[:], tokf[:]))
            own.settle(v.tensor_scalar(idx_src[:, 0:N_TILES], toki[:], TOK - 1, None, ALU.bitwise_and))
            own.settle(v.tensor_scalar(dstf[:], pid[:, 0], -float(NO_ROW), float(NO_ROW), ALU.mult, ALU.add))
            own.settle(v.tensor_tensor(idx_dst[:, 0:N_TILES], dstf[:], tokf[:], ALU.add))
            v.tensor_copy(ring_src[:, 0], idx_src[:, 0:HALF]).then_inc(src_ready, 1)
            v.tensor_copy(ring_dst[:, 0], idx_dst[:, 0:HALF]).then_inc(dst_ready, 1)

            def rows_out(par, turned):
                dve.wait_ge(e_turned, turned)
                v.tensor_copy(xgT[:, par], ps[:, 2, 0:P]).then_inc(eT_ready, 1)

            def gated(n):
                dve.wait_ge(e_c, n)
                dve.wait_ge(e_silu, n)
                v.tensor_tensor(eh, ps[:, 1, 0:EH], egate, ALU.mult).then_inc(e_h, 1)

            rows_out(0, 1)
            rows_out(1, 2)
            gated(1)

            def eight_tiles(i, first):
                for k in range(1, 9):
                    if k in (1, 5):
                        g_ = (k + 3) // HALF
                        v.tensor_copy(ring_src[:, g_ % 2], idx_src[:, ds(i * 8 + g_ * HALF, HALF)]).then_inc(src_ready, 1)
                    if k in (4, 8):
                        g_ = k // HALF
                        for r in range(4 if k == 8 or not first else 0):
                            dve.wait_ge(scattered[r], 16 * (i * 2 + g_ - 1))
                        v.tensor_copy(ring_dst[:, g_ % 2], idx_dst[:, ds(i * 8 + g_ * HALF, HALF)]).then_inc(dst_ready, 1)
                    dve.wait_ge(e_c, i * 8 + k)
                    rows_out((k + 1) % 2, i * 8 + k + 2)
                    dve.wait_ge(eh_turned, i * 8 + k)
                    v.tensor_copy(ehT[:, 0:2], ps[:, 3, 0:2 * P].rearrange("p (c t) -> p c t", c=2)).then_inc(ehT_ready, 1)
                    v.tensor_copy(ehT[0:EH - 2 * P, 2], ps[0:EH - 2 * P, 3, 2 * P:3 * P]).then_inc(ehT_ready, 1)
                    gated(i * 8 + k + 1)

            eight_tiles(0, True)
            with dve.Fori(1, N_TILES // 8) as i:
                eight_tiles(i, False)

            with loop(NBLK // 2, 2 * (K + 2 + 1)) as i:
                for r in range(2):
                    dve.wait_ge(y_in[r], 32 * (i + 1))
                    for k, ring in enumerate((y0r, y1r)):
                        for j in range(TPB):
                            tile = i * 2 * TPB + (r * TPB + j)
                            row = acc[:, ds(tile, 1), :].rearrange("p a d -> p (a d)")
                            last = v.scalar_tensor_tensor(out=row, in0=ring[:, r, j],
                                                          scalar=wk2[:, k, ds(tile, 1)], in1=row,
                                                          op0=ALU.mult, op1=ALU.add)
                        own.settle(last)
                    v.nop().then_inc(fin_read, 1)
                    statistics(lambda j: acc[:, ds(i * 2 * TPB + (r * TPB + j), 1), :].rearrange("p a d -> p (a d)"), r)
                    own.settle(v.tensor_copy(mv[:, ds(i * 2 * TPB + r * TPB, TPB), :], bag[:, r]))
            v.nop().then_inc(fmv_ready, 1)
            dve.wait_ge(fstd_ready, 1)
            own.settle(v.reciprocal(rstd[:], rstd[:]))
            with dve.Fori(0, NBLK // 2) as i:
                for r in range(2):
                    dve.wait_ge(o_stored[r], 16 * (i + 1))
                    for j in range(TPB):
                        tile = i * 2 * TPB + (r * TPB + j)
                        last = v.tensor_scalar(outr[:, r, j], acc[:, ds(tile, 1), :].rearrange("p a d -> p (a d)"),
                                               mv[:, ds(tile, 1), 0], rstd[:, ds(tile, 1)], ALU.subtract, ALU.mult)
                    last.then_inc(o_ready, 1)


_INS = ['L0_attn_x', 'L0_attn_W_in', 'L0_attn_conv_w', 'L0_attn_W_x', 'L0_attn_W_delta', 'L0_attn_b_delta',
        'L0_attn_A_log', 'L0_attn_D', 'L0_attn_W_out', 'L0_ffn_gate_w', 'L0_ffn_w1', 'L0_ffn_w2', 'L0_ffn_w3',
        'L0_ffn_sw1', 'L0_ffn_sw2', 'L0_ffn_sw3']
_OUTS = [((BATCH, SEQ, DM), 'float32')]


def kernel(**inputs):
    import numpy as _np
    import concourse.bacc as _bacc
    from concourse import mybir as _mybir
    from concourse.bass_utils import run_bass_kernel_spmd as _run

    nc = _bacc.Bacc("TRN2", target_bir_lowering=False, num_devices=1)
    arrays, args = {}, []
    for name in _INS:
        a = _np.ascontiguousarray(inputs[name])
        arrays[f"in_{name}_dram"] = a
        args.append(nc.dram_tensor(f"in_{name}_dram", a.shape, _mybir.dt.from_np(a.dtype), kind="ExternalInput").ap())
    for i, (shape, dtype) in enumerate(_OUTS):
        dt = _mybir.dt.from_np(_np.dtype(dtype))
        args.append(nc.dram_tensor(f"out_{i}_dram", shape, dt, kind="ExternalOutput").ap())
    build(nc, *args)
    r = _run(nc, [arrays], core_ids=[0])
    got = tuple(r.results[0][f"out_{i}_dram"] for i in range(len(_OUTS)))
    return got[0]
```

```python
from contextlib import ExitStack

import concourse.bass as bass
from concourse import mybir

F32 = mybir.dt.float32
BF16 = mybir.dt.bfloat16
I32 = mybir.dt.int32
U32 = mybir.dt.uint32
ACT = mybir.ActivationFunctionType
ALU = mybir.AluOpType
AX = mybir.AxisListType

P = 128
BATCH, SEQ, DM = 2, 2048, 128
TOK = BATCH * SEQ
DIN, NST, RANK, TAPS = 256, 16, 64, 3
DC = DIN // P
BLK = 512
NBLK = TOK // BLK
TPB = BLK // P
TILES = TOK // P
HALO = TAPS - 1
XTW = SEQ + HALO
CH = 64
CPB = BLK // CH
NCH = TOK // CH
CPS = SEQ // CH
BPS = SEQ // BLK
E, K = 8, 2
EH = 352
EC = 3
SH = 192
SHH = SH // 2
N_TILES = TOK * K // P + E
GROUP = 4 * K
HALF = 4
XG = 8
AHEAD = 5
IDXC = N_TILES + 2 * HALF
FIN = 4
LN_EPS = 1e-5
NEG_LN_SCAN_EPS = 27.631021115928547
DEAD = -104.0
MAX_EXP = 88.5
FLOOR = -200.0
A_UNIT = float(2 ** 30)
SOFT_CUT = 1.0 / 256.0
NO_ROW = 1 << 20


class Steps:

    def __init__(self, engine, semaphore):
        self.engine, self.semaphore, self.count, self.shift = engine, semaphore, 0, 0

    def settle(self, instruction):
        instruction.then_inc(self.semaphore, 1)
        self.count += 1
        self.engine.wait_ge(self.semaphore, self.count + self.shift)


class SteppedLoop:

    def __init__(self, engine, steps, count, per):
        self.loop, self.steps, self.turns, self.per = engine.Fori(0, count), steps, count, per

    def __enter__(self):
        i = self.loop.__enter__()
        self.start = self.steps.count
        self.steps.shift = i * self.per
        return i

    def __exit__(self, *what):
        if what[0] is None:
            assert self.steps.count == self.start + self.per, self.steps.count - self.start
        self.steps.shift = 0
        self.steps.count = self.start + self.turns * self.per
        return self.loop.__exit__(*what)


def hold(engine, waited):
    engine.sem_inc(waited, 1)


def ds(start, size):
    return bass.ds(start, size)


def load_registers(nc, engine_type, values, top):
    _, registers = nc.values_load_multi_w_load_instructions(
        values, engines=(engine_type,), min_val=0, max_val=top,
        skip_runtime_bounds_check_because="the instruction that makes them clamps them, and sums of 0 and 1 are not negative")
    return registers


def build(nc, x, W_in, conv_w, W_x, W_delta, b_delta, A_log, D, W_out,
          gate_w, w1, w2, w3, sw1, sw2, sw3, out):
    with ExitStack() as ctx:
        def sb(name, shape, dt=F32):
            return ctx.enter_context(nc.sbuf_tensor(name, shape, dt))

        def sem(name):
            return ctx.enter_context(nc.semaphore(name))

        u_all = sb("u_all", [P, DC, TOK])
        y_all = sb("y_all", [P, DC, TOK])
        dl_all = sb("dl_all", [P, DC, TOK])
        xT = sb("xT", [P, BATCH * XTW])
        xdl = sb("xdl", [RANK, TOK])
        bc = sb("bc", [2 * NST, TOK])
        scratch = sb("scratch", [P, 6, DC * BLK])

        uf = u_all[:].rearrange("p c t -> p (c t)")
        w13 = uf[:, 0:E * 2 * EH].rearrange("p (e n) -> p e n", e=E)
        acc = xT[:, 0:TOK].rearrange("p (t d) -> p t d", d=DM)
        y0r, y1r, outr = (uf[:, m * FIN * BLK:(m + 1) * FIN * BLK].rearrange("p (r i d) -> p r i d", r=FIN, d=DM)
                          for m in range(3))
        df = dl_all[:].rearrange("p c t -> p (c t)")
        res1 = df[:, 0:TOK].rearrange("p (t d) -> p t d", d=DM)
        x1b = df[:, TOK:TOK + 2 * BLK].rearrange("p (r i d) -> p r i d", r=2, d=DM)
        x1T = df[:, TOK + 2 * BLK:TOK + 4 * BLK].rearrange("p (r t) -> p r t", r=2)
        shT = df[0:SHH, TOK + 4 * BLK:TOK + 8 * BLK].rearrange("p (r h t) -> p r h t", r=2, h=2)
        yf = y_all[:].rearrange("p c t -> p (c t)")
        w2s = yf[:, 0:E * EC * DM].rearrange("p (e c n) -> p e c n", e=E, c=EC)
        xin = scratch[:, 0:2, 0:BLK].rearrange("p r (i d) -> p r i d", d=DM)
        z_buf = scratch[:, 0:2, :].rearrange("p r (c t) -> p r c t", c=DC)
        ln_buf = scratch[:, 2:4, :].rearrange("p r (c t) -> p r c t", c=DC)
        sq_buf = scratch[:, 4:6, :].rearrange("p r (c t) -> p r c t", c=DC)
        decay = scratch[:, 0:2, :].rearrange("p c (n t) -> p c n t", n=NST)
        gain = scratch[:, 2:4, :].rearrange("p c (n t) -> p c n t", n=NST)
        dbu = scratch[:, 4, :].rearrange("p (n t) -> p n t", n=NST)
        hs = scratch[:, 5, :].rearrange("p (n t) -> p n t", n=NST)
        ybuf = scratch[:, 0:2, :].rearrange("p r (c t) -> p r c t", c=DC)
        sgate = scratch[0:SHH, 4, :].rearrange("p (h t) -> p h t", h=2)
        sf = scratch[:].rearrange("p a n -> p (a n)").bitcast(BF16)
        oh_at = [0, 2 * GROUP * P, 2 * GROUP * (P + 2 * N_TILES), 2 * GROUP * (P + 2 * N_TILES) + GROUP * N_TILES]
        ohl = sf[:, oh_at[0]:oh_at[1]].rearrange("p (r g n) -> p r g n", r=2, g=GROUP)
        ohh = sf[:, oh_at[1]:oh_at[2]].rearrange("p (r g a n) -> p r g a n", r=2, g=GROUP, a=2)
        ohe = sf[:, oh_at[2]:oh_at[3]].rearrange("p (g n) -> p g n", g=GROUP)
        xg = scratch[:, 0, :].rearrange("p (r d) -> p r d", r=XG)
        egate = scratch[:, 1, 0:EH]
        eh = scratch[:, 1, 512:512 + EH]
        ehT = scratch[:, 2, 0:EC * P].rearrange("p (c t) -> p c t", c=EC)
        yo = scratch[:, 3, 0:4 * DM].rearrange("p (r d) -> p r d", r=4)
        xgT = scratch[:, 3, 4 * DM:6 * DM].rearrange("p (r d) -> p r d", r=2)

        win = sb("win", [P, 2 * DIN])
        cwb = sb("cwb", [P, DIN, TAPS])
        wk = sb("wk", [P, TAPS, DIN])
        wx = sb("wx", [P, DC, RANK + 2 * NST])
        wdel = sb("wdel", [RANK, DIN])
        bdel = sb("bdel", [P, DC])
        dskip = sb("dskip", [P, DC])
        alog = sb("alog", [P, DC, NST])
        aneg = sb("aneg", [P, DC, NST])
        amax = sb("amax", [P, DC])
        wout = sb("wout", [P, DC, DM])
        gw = sb("gw", [E, DM])
        gwT = sb("gwT", [P, E])
        s1 = sb("s1", [P, SH])
        s3 = sb("s3", [P, SH])
        s2 = sb("s2", [SHH, 2, DM])
        ident = sb("ident", [P, P])
        ones = sb("ones", [P, P])
        before = sb("before", [P, P])
        iota = sb("iota", [P, P])
        pcol = sb("pcol", [P, 1])
        csum = sb("csum", [P, DC, BATCH, CPS])
        rend = sb("rend", [P, DC, BATCH, CPS])
        dch = sb("dch", [P, DC, CH])
        rch = sb("rch", [P, DC, CH])
        live = sb("live", [P, DC, NCH])
        flagf = sb("flagf", [1, NCH])
        flags = sb("flags", [1, NCH], I32)
        hcar = sb("hcar", [P, DC, NST])
        hmul = sb("hmul", [P, NST])
        du = sb("du", [P, DC, CH])
        ysum = sb("ysum", [P, CH])
        gch = sb("gch", [P, DC, CH])
        bst = sb("bst", [P, 2, TPB, 6])
        bag = sb("bag", [P, 2, TPB, 2])
        vare = sb("vare", [P, 2, TPB])
        rstd = sb("rstd", [P, 2, TPB])
        shift = sb("shift", [P, 2, TPB])
        lnc = sb("lnc", [P, 3, TPB])
        epst = sb("epst", [P, 3])
        lg = sb("lg", [P, TILES, E])
        sc = sb("sc", [P, TILES, E])
        t3 = sb("t3", [P, TILES, E])
        m1 = sb("m1", [P, TILES, E])
        m2 = sb("m2", [P, TILES, E])
        rk = sb("rk", [P, TILES, E])
        ex = sb("ex", [P, TILES, E])
        col = sb("col", [P, TILES])
        wk2 = sb("wk2", [P, K, TILES])
        slot = sb("slot", [P, K, TILES])
        sloti = sb("sloti", [P, K, TILES], I32)
        hii = sb("hii", [P, K, TILES], I32)
        loi = sb("loi", [P, K, TILES], I32)
        hif = sb("hif", [P, TILES, K])
        lof = sb("lof", [P, TILES, K])
        cnt = sb("cnt", [P, E])
        cnti = sb("cnti", [P, E], I32)
        nti = sb("nti", [P, E], I32)
        ntf = sb("ntf", [P, E])
        tend = sb("tend", [P, E])
        tbeg = sb("tbeg", [P, E])
        desc = sb("desc", [P, E])
        tcol = sb("tcol", [P, TILES, K])
        tex = sb("tex", [1, IDXC, E])
        texs = sb("texs", [1, IDXC])
        texi = sb("texi", [1, IDXC], I32)
        zer = sb("zer", [P, 2 * N_TILES], BF16)
        pid = sb("pid", [P, 2, N_TILES])
        dstf = sb("dstf", [P, N_TILES])
        tokf = sb("tokf", [P, N_TILES])
        toki = sb("toki", [P, N_TILES], I32)
        idx_src = sb("idx_src", [P, IDXC], I32)
        idx_dst = sb("idx_dst", [P, IDXC], I32)
        ring_src = sb("ring_src", [P, 2, HALF], I32)
        ring_dst = sb("ring_dst", [P, 2, HALF], I32)

        ps = ctx.enter_context(nc.psum_tensor("ps", [P, 8, BLK], F32))

        x1_rows = nc.dram_tensor("x1_rows", [TOK, DM], F32).ap()
        y_rows = nc.dram_tensor("y_rows", [K * TOK, DM], F32).ap()

        x_in = [sem(f"x_in{r}") for r in range(2)]
        w_first, w_mix, w_ffn, w_exp = sem("w_first"), sem("w_mix"), sem("w_ffn"), sem("w_exp")
        const_step, consts, halo = sem("const_step"), sem("consts"), sem("halo")
        pool_held, act_held, dve_held = sem("pool_held"), sem("act_held"), sem("dve_held")
        pool_step, dve_step = sem("pool_step"), sem("dve_step")
        wk_ready, alog_ready = sem("wk_ready"), sem("alog_ready")
        gwT_sum, gwT_ready = sem("gwT_sum"), sem("gwT_ready")
        x_turned, xT_ready = sem("x_turned"), sem("xT_ready")
        u_sum, u_ready, g_sum, g_ready = sem("u_sum"), sem("u_ready"), sem("g_sum"), sem("g_ready")
        xd_sum, xd_ready, y_ready = sem("xd_sum"), sem("xd_ready"), sem("y_ready")
        pd_sum, z_ready, z_clamped, ln_ready = sem("pd_sum"), sem("z_ready"), sem("z_clamped"), sem("ln_ready")
        dl_ready, a_exp = sem("dl_ready"), sem("a_exp")
        live_ready, live_sum, flags_ready = sem("live_ready"), sem("live_sum"), sem("flags_ready")
        b_sum, c_sum, za_raw = sem("b_sum"), sem("c_sum"), sem("za_raw")
        za_ready, zr_ready, decay_ready, gain_ready = sem("za_ready"), sem("zr_ready"), sem("decay_ready"), sem("gain_ready")
        chunk_done, batch_start = sem("chunk_done"), sem("batch_start")
        yb_ready, mix_sum, res_ready = sem("yb_ready"), sem("mix_sum"), sem("res_ready")
        xres_in = [sem(f"xres_in{r}") for r in range(2)]
        var_ready, rstd_ready = sem("var_ready"), sem("rstd_ready")
        x1_ready, x1_turned, x1T_ready = sem("x1_ready"), sem("x1_turned"), sem("x1T_ready")
        x1_stored = [sem(f"x1_stored{r}") for r in range(2)]
        gate_sum, lg_ready = sem("gate_sum"), sem("lg_ready")
        sh_a, sh_c, sh_silu, sh_h, sh_sum, acc_ready = (sem("sh_a"), sem("sh_c"), sem("sh_silu"),
                                                        sem("sh_h"), sem("sh_sum"), sem("acc_ready"))
        lgx_ready, sce_ready = sem("lgx_ready"), sem("sce_ready")
        m_ready, rank_sum = sem("m_ready"), sem("rank_sum")
        oh_ready, oh_sum = sem("oh_ready"), sem("oh_sum")
        texi_ready = sem("texi_ready")
        src_ready, dst_ready = sem("src_ready"), sem("dst_ready")
        gathered = [sem(f"gathered{r}") for r in range(XG)]
        scattered = [sem(f"scattered{r}") for r in range(4)]
        e_turned, eT_ready, e_a, e_c, e_silu, e_h = (sem("e_turned"), sem("eT_ready"), sem("e_a"),
                                                     sem("e_c"), sem("e_silu"), sem("e_h"))
        eh_turned, ehT_ready, e_sum, e_out = sem("eh_turned"), sem("ehT_ready"), sem("e_sum"), sem("e_out")
        y_in = [sem(f"y_in{r}") for r in range(FIN)]
        y0_scaled, fin_read, fvar_ready = sem("y0_scaled"), sem("fin_read"), sem("fvar_ready")
        frstd_ready, o_ready = sem("frstd_ready"), sem("o_ready")
        o_stored = [sem(f"o_stored{r}") for r in range(FIN)]

        x_rows = x.rearrange("b s d -> (b s) d").rearrange("(n i p) d -> n p i d", i=TPB, p=P)
        o_rows = out.rearrange("b s d -> (b s) d").rearrange("(n i p) d -> n p i d", i=TPB, p=P)
        x1_blocks = x1_rows.rearrange("(n i p) d -> n p i d", i=TPB, p=P)
        y_blocks = y_rows.rearrange("(k n i p) d -> k n p i d", k=K, i=TPB, p=P)

        def row_block(view, n):
            return view[ds(n, 1)].rearrange("a p i d -> (a p) i d")

        def chunk_loops(engine, ops, which, chunk, skip, start_batch=None):
            with engine.Fori(0, BATCH) as b:
                if start_batch:
                    start_batch(b)
                with engine.Fori(0, BPS) as n:
                    any_live, = load_registers(nc, which, flags[0:1, ds(b * CPS + n * CPB + (CPB - 1), 1)], 1)
                    with engine.If(any_live > 0):
                        with engine.Fori(0, CPB) as k:
                            q = b * CPS + n * CPB + k
                            is_live, = load_registers(nc, which, flags[0:1, ds(q, 1)], 1)
                            with engine.If(is_live > 0):
                                chunk(q, b)
                            with engine.Else():
                                skip(1, q)
                            ops.nop()
                        ops.nop()
                    with engine.Else():
                        skip(CPB, b * CPS + n * CPB)
                    ops.nop()

        block = ctx.enter_context(nc.Block())

        @block.sync
        def _(sp):
            for r in range(2):
                sp.sem_inc(x1_stored[r], 16)
            for r in range(FIN):
                sp.sem_inc(o_stored[r], 16)
            for r in range(2):
                sp.dma_start(xin[:, r], x_rows[r]).then_inc(x_in[r], 16)
                if r == 0:
                    sp.dma_start(win[:], W_in).then_inc(w_first, 16)
                    sp.dma_start(cwb[:].rearrange("p d k -> p (d k)"),
                                 conv_w.rearrange("d a k -> (a d k)").partition_broadcast(P)
                                 ).then_inc(w_first, 16)
            mix_loads = [
                (wx[:], W_x.rearrange("(c p) n -> p c n", p=P)),
                (wdel[:], W_delta),
                (bdel[:], b_delta.rearrange("(c p) -> p c", p=P)),
                (dskip[:], D.rearrange("(c p) -> p c", p=P)),
                (alog[:], A_log.rearrange("(c p) n -> p c n", p=P)),
            ]
            ffn_loads = [
                (wout[:], W_out.rearrange("(c p) n -> p c n", p=P)),
                (gw[:], gate_w), (s1[:], sw1), (s3[:], sw3),
                (s2[:], sw2.rearrange("(h p) n -> p h n", p=SHH)),
            ]
            with nc.allow_non_contiguous_dma(reason="columns of 256 numbers"):
                for dst, src in mix_loads:
                    sp.dma_start(dst, src).then_inc(w_mix, 16)
                for dst, src in ffn_loads:
                    sp.dma_start(dst, src).then_inc(w_ffn, 16)
            with sp.Fori(1, NBLK // 2) as i:
                for r in range(2):
                    sp.wait_ge(x_turned, i * 2 + r - 1)
                    sp.dma_start(xin[:, r], row_block(x_rows, i * 2 + r)).then_inc(x_in[r], 16)
            sp.wait_ge(chunk_done, NCH + 1)
            for r in range(2):
                half = NBLK // 2
                sp.dma_start(res1[:, r * half * TPB:(r + 1) * half * TPB, :].rearrange("p (n i) d -> p n i d", i=TPB),
                             x_rows[r * half:(r + 1) * half].rearrange("n p i d -> p n i d")).then_inc(xres_in[r], 16)
            sp.dma_start(w13[:, :, 0:EH], w1.rearrange("e p n -> p e n")).then_inc(w_exp, 16)
            sp.dma_start(w13[:, :, EH:2 * EH], w3.rearrange("e p n -> p e n")).then_inc(w_exp, 16)
            with sp.Fori(0, NBLK // 2) as i:
                for r in range(2):
                    sp.wait_ge(x1_ready, i * 2 + r + 1)
                    sp.dma_start(row_block(x1_blocks, i * 2 + r), x1b[:, r]).then_inc(x1_stored[r], 16)
            sp.wait_ge(yb_ready, NBLK)
            for c in range(EC):
                w = min(P, EH - c * P)
                sp.dma_start(w2s[0:w, :, c, :], w2[:, c * P:c * P + w, :].rearrange("e p n -> p e n")
                             ).then_inc(w_exp, 16)
            for r in range(4):
                sp.wait_ge(scattered[r], 16 * (N_TILES // 4))
            def load_y(n, r):
                for k, ring in enumerate((y0r, y1r)):
                    sp.dma_start(ring[:, r], row_block(y_blocks[k], n)).then_inc(y_in[r], 16)

            def store_out(n, r):
                sp.wait_ge(o_ready, n + 3)
                sp.dma_start(row_block(o_rows, n), outr[:, r]).then_inc(o_stored[r], 16)

            for r in range(FIN):
                load_y(r, r)
            with sp.Fori(0, NBLK // FIN - 1) as i:
                for r in range(FIN):
                    n = i * FIN + r
                    sp.wait_ge(fin_read, n + 1)
                    load_y(n + FIN, r)
                    store_out(n, r)
            for r in range(FIN):
                store_out(NBLK - FIN + r, r)
            for r in range(FIN):
                sp.wait_ge(o_stored[r], 16 * (NBLK // FIN + 1))

        @block.gpsimd
        def _(pool):
            g = nc.gpsimd
            own = Steps(pool, pool_step)
            g.memset(xT[:, 0:HALO], 0.0).then_inc(halo, 1)
            g.memset(xT[:, XTW:XTW + HALO], 0.0).then_inc(halo, 1)
            own.settle(g.memset(ones[:], 1.0))
            own.settle(g.memset(ident[:], 0.0))
            g.affine_select(out=ident[:], in_=ident[:], compare_op=ALU.not_equal, fill=1.0, base=0,
                            pattern=[[-1, P]], channel_multiplier=1).then_inc(consts, 1)
            g.affine_select(out=before[:], in_=ones[:], compare_op=ALU.is_gt, fill=0.0, base=0,
                            pattern=[[1, P]], channel_multiplier=-1).then_inc(consts, 1)
            g.iota(iota[:], pattern=[[1, P]], base=0, channel_multiplier=0,
                   allow_small_or_imprecise_dtypes=True).then_inc(consts, 1)
            g.iota(pcol[:], pattern=[[0, 1]], base=0, channel_multiplier=1,
                   allow_small_or_imprecise_dtypes=True).then_inc(consts, 1)
            g.iota(desc[:], pattern=[[-1, E]], base=E, channel_multiplier=0,
                   allow_small_or_imprecise_dtypes=True).then_inc(consts, 1)
            g.iota(tcol[:], pattern=[[1, TILES], [TILES, K]], base=1, channel_multiplier=0,
                   allow_small_or_imprecise_dtypes=True).then_inc(consts, 1)
            g.memset(zer[:], 0.0).then_inc(consts, 1)
            g.memset(idx_src[:], 0).then_inc(consts, 1)
            g.memset(idx_dst[:], NO_ROW).then_inc(consts, 1)
            g.memset(epst[:, 0:1], LN_EPS).then_inc(consts, 1)
            g.memset(epst[:, 1:2], NEG_LN_SCAN_EPS).then_inc(consts, 1)
            g.memset(epst[:, 2:3], 1.0).then_inc(consts, 1)
            for m, value in enumerate((-0.5, LN_EPS, -1.0)):
                g.memset(lnc[:, m], value).then_inc(consts, 1)
            g.iota(tex[:], pattern=[[1, IDXC], [0, E]], base=0, channel_multiplier=0,
                   allow_small_or_imprecise_dtypes=True).then_inc(consts, 1)

            def chunk(q, b):
                col0 = q * CH
                pool.wait_ge(chunk_done, q + 1)
                for c in range(DC):
                    ins = g.tensor_tensor(decay[:, c],
                                          dl_all[:, c, ds(col0, CH)].unsqueeze(1).to_broadcast([P, NST, CH]),
                                          aneg[:, c, :].unsqueeze(2).to_broadcast([P, NST, CH]), ALU.mult)
                ins.then_inc(za_raw, 1)
                pool.wait_ge(za_raw, q + 1)
                hold(pool, pool_held)

            def skip(n, q):
                pool.sem_inc(za_raw, n)

            pool.wait_ge(flags_ready, 1)
            chunk_loops(pool, g, mybir.EngineType.Pool, chunk, skip)

            def deviations(i, ready, done, with_shift):
                for r in range(2):
                    pool.wait_ge(ready, i * 2 + r + 1)
                    hold(pool, pool_held)
                    own.settle(g.tensor_tensor(vare[:, r], bag[:, r, :, 1], lnc[:, 1], ALU.add))
                    if with_shift:
                        own.settle(g.tensor_tensor(rstd[:, r], vare[:, r], lnc[:, 0], ALU.pow))
                        own.settle(g.tensor_tensor(shift[:, r], bag[:, r, :, 0], rstd[:, r], ALU.mult))
                        g.tensor_tensor(shift[:, r], shift[:, r], lnc[:, 2], ALU.mult).then_inc(done, 1)
                    else:
                        g.tensor_tensor(rstd[:, r], vare[:, r], lnc[:, 0], ALU.pow).then_inc(done, 1)

            with SteppedLoop(pool, own, NBLK // 2, 2) as i:
                deviations(i, var_ready, rstd_ready, False)

            def gather(slot_, half_ring, j):
                hold(pool, pool_held)
                g.indirect_dma_start(xg[:, slot_], None, x1_rows,
                                     bass.IndirectOffsetOnAxis(ap=ring_src[:, half_ring, j:j + 1].bitcast(U32), axis=0)
                                     ).then_inc(gathered[slot_], 16)

            for r in range(2):
                pool.wait_ge(x1_stored[r], 16 * (NBLK // 2 + 1))
            pool.wait_ge(src_ready, 1)
            for t in range(AHEAD + 1):
                gather(t, t // HALF, t % HALF)
            with pool.Fori(0, N_TILES // 8) as i:
                for k in range(1, 9):
                    ahead = k + AHEAD
                    if ahead % HALF == 0:
                        pool.wait_ge(src_ready, i * 2 + ahead // HALF)
                    pool.wait_ge(e_turned, i * 8 + k)
                    gather(ahead % XG, (ahead // HALF) % 2, ahead % HALF)
                    behind = k - 1
                    if behind % HALF == 0:
                        pool.wait_ge(dst_ready, i * 2 + behind // HALF + 1)
                    pool.wait_ge(e_out, i * 8 + k + 2)
                    hold(pool, pool_held)
                    g.indirect_dma_start(y_rows,
                                         bass.IndirectOffsetOnAxis(ap=ring_dst[:, (behind // HALF) % 2, behind % HALF:behind % HALF + 1].bitcast(U32), axis=0),
                                         yo[:, behind % 4], None, bounds_check=K * TOK - 1, oob_is_err=False
                                         ).then_inc(scattered[behind % 4], 16)
            for ahead in range(2, AHEAD + 1):
                pool.wait_ge(gathered[ahead], 16 * (N_TILES // XG + 1))
            with SteppedLoop(pool, own, NBLK // 2, 6) as i:
                deviations(i, fvar_ready, frstd_ready, True)

        @block.scalar
        def _(act):
            s = nc.scalar
            act.sem_inc(u_ready, 2)
            act.sem_inc(g_ready, 2)
            act.sem_inc(e_out, 2)
            act.sem_inc(o_ready, 2)
            with act.Fori(0, NBLK // 2) as i:
                for r in range(2):
                    cols = ds(i * 2 * BLK + r * BLK, BLK)
                    for c in range(DC):
                        act.wait_ge(u_sum, i * 4 + 2 * r + c + 1)
                        s.activation(u_all[:, c, cols], ps[:, c], ACT.Silu).then_inc(u_ready, 1)
                    for c in range(DC):
                        act.wait_ge(g_sum, i * 4 + 2 * r + c + 1)
                        s.activation(y_all[:, c, cols], ps[:, 2 + c], ACT.Silu).then_inc(g_ready, 1)
            act.wait_ge(alog_ready, 1)
            act.wait_ge(consts, 16)
            s.activation(aneg[:], alog[:], ACT.Exp).then_inc(a_exp, 1)
            with act.Fori(0, NBLK // 2) as i:
                for r in range(2):
                    act.wait_ge(pd_sum, i * 2 + r + 1)
                    act.wait_ge(dl_ready, i * 2 + r + 1)
                    for c in range(DC):
                        s.activation(z_buf[:, r, c], ps[:, 2 * r + c], ACT.Exp,
                                     bias=bdel[:, c:c + 1]).then_inc(z_ready, 1)
                for r in range(2):
                    act.wait_ge(z_clamped, i * 2 + r + 1)
                    s.activation(ln_buf[:, r], z_buf[:, r], ACT.Ln, bias=epst[:, 2:3]).then_inc(ln_ready, 1)

            def chunk(q, b):
                act.wait_ge(za_ready, q + 1)
                s.activation(decay[:], decay[:], ACT.Exp, scale=A_UNIT).then_inc(decay_ready, 1)
                act.wait_ge(zr_ready, q + 1)
                act.wait_ge(c_sum, q + 1)
                s.activation(gch[:], ps[:, 2, 0:DC * CH].rearrange("p (c t) -> p c t", c=DC), ACT.Sigmoid)
                s.activation(gain[:], gain[:], ACT.Sigmoid, bias=epst[:, 1:2],
                             scale=A_UNIT).then_inc(gain_ready, 1)
                act.wait_ge(gain_ready, q + 1)
                hold(act, act_held)

            def skip(n, q):
                act.sem_inc(decay_ready, n)
                act.sem_inc(gain_ready, n)

            act.wait_ge(flags_ready, 1)
            chunk_loops(act, s, mybir.EngineType.Activation, chunk, skip)
            def keep_y(n, r):
                s.copy(ybuf[:, r], y_all[:, :, ds(n * BLK, BLK)]).then_inc(yb_ready, 1)

            def keep_x1T(n, r):
                act.wait_ge(x1_turned, n + 1)
                s.copy(x1T[:, r], ps[:, 2]).then_inc(x1T_ready, 1)

            def two_blocks(i, last):
                for r in range(2):
                    n = i * 2 + r
                    for h in range(2):
                        act.wait_ge(sh_a, n * 2 + h + 1)
                        act.wait_ge(sh_h, n * 2 + h + 1)
                        s.activation(sgate[:, h], ps[0:SHH, 4 + h], ACT.Silu).then_inc(sh_silu, 1)
                    if not last:
                        act.wait_ge(mix_sum, n + 1)
                        keep_y(n + 2, r)
                    if not last or r == 0:
                        keep_x1T(n + 1, (r + 1) % 2)

            act.wait_ge(chunk_done, NCH + 1)
            for r in range(2):
                keep_y(r, r)
            keep_x1T(0, 0)
            with act.Fori(0, NBLK // 2 - 1) as i:
                two_blocks(i, False)
            two_blocks(NBLK // 2 - 1, True)
            act.wait_ge(lgx_ready, 1)
            s.activation(sc[:], t3[:], ACT.Exp).then_inc(sce_ready, 1)
            act.wait_ge(e_a, 1)
            s.activation(egate, ps[:, 0, 0:EH], ACT.Silu).then_inc(e_silu, 1)

            def eight_tiles(i, first):
                for k in range(1, 9):
                    act.wait_ge(e_a, i * 8 + k + 1)
                    s.activation(egate, ps[:, 0, 0:EH], ACT.Silu).then_inc(e_silu, 1)
                    behind = k - 1
                    act.wait_ge(e_sum, i * 8 + k)
                    if behind >= 4 or not first:
                        act.wait_ge(scattered[behind % 4], 16 * (i * 2 + behind // 4))
                    s.copy(yo[:, behind % 4], ps[:, 4 + behind % 2, 0:DM]).then_inc(e_out, 1)

            eight_tiles(0, True)
            with act.Fori(1, N_TILES // 8) as i:
                eight_tiles(i, False)
            def scale_y0(i, r):
                act.wait_ge(y_in[r], 32 * (i + 1))
                for j in range(TPB):
                    last = s.activation(y0r[:, r, j], y0r[:, r, j], ACT.Copy,
                                        scale=wk2[:, 0, ds(i * FIN * TPB + (r * TPB + j), 1)])
                last.then_inc(y0_scaled, 1)

            def normalise(i, r):
                act.wait_ge(frstd_ready, i * FIN + r + 1)
                act.wait_ge(o_stored[r], 16 * (i + 1))
                for j in range(TPB):
                    last = s.activation(outr[:, r, j],
                                        acc[:, ds(i * FIN * TPB + (r * TPB + j), 1), :].rearrange("p a d -> p (a d)"),
                                        ACT.Identity, bias=shift[:, r % 2, j:j + 1], scale=rstd[:, r % 2, j:j + 1])
                last.then_inc(o_ready, 1)

            def four_blocks(i, last):
                for r in range(FIN):
                    if not last or r + 1 < FIN:
                        scale_y0(i + (r + 1) // FIN, (r + 1) % FIN)
                    normalise(i, r)

            scale_y0(0, 0)
            with act.Fori(0, NBLK // FIN - 1) as i:
                four_blocks(i, False)
            four_blocks(NBLK // FIN - 1, True)

        @block.tensor
        def _(pe):
            t = nc.tensor
            pe.sem_inc(oh_sum, 2)
            pe.wait_ge(consts, 1)
            with pe.Fori(0, NBLK // 2) as i:
                for r in range(2):
                    pe.wait_ge(x_in[r], 16 * (i + 1))
                    pe.wait_ge(xT_ready, i * 2 + r + 1)
                    for j in range(TPB):
                        last = t.transpose(ps[:, 6 + r, j * P:(j + 1) * P], xin[:, r, j], ident[:])
                    last.then_inc(x_turned, 1)
            pe.wait_ge(wk_ready, TAPS)
            pe.wait_ge(halo, 2)
            pe.wait_ge(w_mix, 16 * 5)
            with pe.Fori(0, BATCH) as b:
                with pe.Fori(0, BPS // 2) as h:
                    for r in range(2):
                        n = b * BPS + h * 2 + r
                        base = b * XTW + h * (2 * BLK) + r * BLK
                        pe.wait_ge(xT_ready, n + 3)
                        for c in range(DC):
                            pe.wait_ge(u_ready, n * 2 + c + 1)
                            for k in range(TAPS):
                                last = t.matmul(ps[:, c], wk[:, k, c * P:(c + 1) * P], xT[:, ds(base + k, BLK)],
                                                start=(k == 0), stop=(k == TAPS - 1))
                            last.then_inc(u_sum, 1)
                        for c in range(DC):
                            pe.wait_ge(g_ready, n * 2 + c + 1)
                            t.matmul(ps[:, 2 + c], win[:, DIN + c * P:DIN + (c + 1) * P],
                                     xT[:, ds(base + HALO, BLK)], start=True, stop=True).then_inc(g_sum, 1)
                        pe.wait_ge(u_ready, n * 2 + 4)
                        pe.wait_ge(xd_ready, n * 2 + 2)
                        for c in range(DC):
                            last = t.matmul(ps[0:RANK + 2 * NST, 4], wx[:, c], u_all[:, c, ds(n * BLK, BLK)],
                                            start=(c == 0), stop=(c == DC - 1))
                        last.then_inc(xd_sum, 1)
            pe.wait_ge(g_ready, 2 * NBLK + 2)
            pe.wait_ge(xd_ready, 2 * NBLK + 2)
            with pe.Fori(0, NBLK // 2) as i:
                for r in range(2):
                    pe.wait_ge(dl_ready, i * 2 + r + 1)
                    for c in range(DC):
                        last = t.matmul(ps[:, 2 * r + c], wdel[:, c * P:(c + 1) * P],
                                        xdl[:, ds(i * 2 * BLK + r * BLK, BLK)], start=True, stop=True)
                    last.then_inc(pd_sum, 1)
            pe.wait_ge(live_ready, 1)
            t.matmul(ps[0:1, 4, 0:DC * NCH], ones[:, 0:1], live[:].rearrange("p c q -> p (c q)"),
                     start=True, stop=True).then_inc(live_sum, 1)

            def chunk(q, b):
                xcol = q * CH + b * HALO + HALO
                pe.wait_ge(chunk_done, q + 1)
                for half, done in enumerate((b_sum, c_sum)):
                    if half == 1:
                        for c in range(DC):
                            t.matmul(ps[:, 2, c * CH:(c + 1) * CH], win[:, DIN + c * P:DIN + (c + 1) * P],
                                     xT[:, ds(xcol, CH)], start=True, stop=True)
                    for n in range(NST):
                        row = half * NST + n
                        last = t.matmul(ps[:, 4 + 2 * half + n // 8, (n % 8) * CH:(n % 8 + 1) * CH],
                                        ident[0:2 * NST, row:row + 1].to_broadcast([2 * NST, P]),
                                        bc[:, ds(q * CH, CH)], start=True, stop=True)
                    last.then_inc(done, 1)
                pe.wait_ge(b_sum, q + 1)
                pe.wait_ge(c_sum, q + 1)

            def skip(n, q):
                pe.sem_inc(b_sum, n)
                pe.sem_inc(c_sum, n)

            pe.wait_ge(flags_ready, 1)
            chunk_loops(pe, t, mybir.EngineType.PE, chunk, skip)

            def mix(n, r):
                pe.wait_ge(yb_ready, n + 1)
                for j in range(TPB):
                    for c in range(DC):
                        last = t.matmul(ps[:, r, j * P:(j + 1) * P], ybuf[:, r, c, j * P:(j + 1) * P],
                                        wout[:, c], start=(c == 0), stop=(c == DC - 1))
                last.then_inc(mix_sum, 1)

            def turn_x1(n, r):
                pe.wait_ge(x1_ready, n + 1)
                for j in range(TPB):
                    last = t.transpose(ps[:, 2, j * P:(j + 1) * P], x1b[:, r, j], ident[:])
                last.then_inc(x1_turned, 1)

            def two_blocks(i, last_two):
                for r in range(2):
                    n = i * 2 + r
                    pe.wait_ge(x1T_ready, n + 1)
                    for j in range(TPB):
                        last = t.matmul(ps[:, 2, j * E:(j + 1) * E], x1T[:, r, j * P:(j + 1) * P], gwT[:],
                                        start=True, stop=True)
                    last.then_inc(gate_sum, 1)
                    for h in range(2):
                        pe.wait_ge(sh_h, n * 2 + h + 1)
                        t.matmul(ps[0:SHH, 4 + h], s1[:, h * SHH:(h + 1) * SHH], x1T[:, r],
                                 start=True, stop=True).then_inc(sh_a, 1)
                        t.matmul(ps[0:SHH, 6 + h], s3[:, h * SHH:(h + 1) * SHH], x1T[:, r],
                                 start=True, stop=True).then_inc(sh_c, 1)
                    if not last_two or r == 0:
                        pe.wait_ge(lg_ready, n + 2)
                        turn_x1(n + 1, (r + 1) % 2)
                    if not last_two:
                        pe.wait_ge(res_ready, n + 1)
                        mix(n + 2, r)
                    pe.wait_ge(sh_h, n * 2 + 4)
                    pe.wait_ge(acc_ready, n + 1)
                    for j in range(TPB):
                        for h in range(2):
                            last = t.matmul(ps[:, 3, j * P:(j + 1) * P], shT[:, r, h, j * P:(j + 1) * P],
                                            s2[:, h], start=(h == 0), stop=(h == 1))
                    last.then_inc(sh_sum, 1)

            pe.wait_ge(w_ffn, 16 * 5)
            t.transpose(ps[:, 3, 0:E], gw[:], ident[0:E, 0:E]).then_inc(gwT_sum, 1)
            for r in range(2):
                mix(r, r)
            pe.wait_ge(gwT_ready, 1)
            turn_x1(0, 0)
            with pe.Fori(0, NBLK // 2 - 1) as i:
                two_blocks(i, False)
            two_blocks(NBLK // 2 - 1, True)
            pe.wait_ge(m_ready, 1)
            t.matmul(ps[:, 4, 0:TILES * E], before[:], rk[:].rearrange("p t e -> p (t e)"), start=True, stop=True)
            t.matmul(ps[:, 5, 0:TILES * E], ones[:], rk[:].rearrange("p t e -> p (t e)"),
                     start=True, stop=True).then_inc(rank_sum, 1)
            pe.wait_ge(acc_ready, NBLK + 1)
            t.matmul(ps[:, 3, 0:2 * N_TILES], zer[:, 0:P], zer[:], start=True, stop=False,
                     skip_group_check=True)
            with pe.Fori(0, TILES * K // GROUP // 2) as i:
                for r in range(2):
                    pe.wait_ge(oh_ready, i * 2 + r + 1)
                    for j in range(GROUP):
                        last = t.matmul(ps[:, 3, 0:2 * N_TILES], ohl[:, r, j],
                                        ohh[:, r, j].rearrange("p a n -> p (a n)"),
                                        start=False, stop=False, skip_group_check=True)
                    last.then_inc(oh_sum, 1)
            t.matmul(ps[:, 3, 0:2 * N_TILES], zer[:, 0:P], zer[:], start=False, stop=True,
                     skip_group_check=True).then_inc(oh_sum, 1)

            def turn_rows(slot_, landed, freed):
                pe.wait_ge(gathered[slot_], landed)
                if freed is not None:
                    pe.wait_ge(eT_ready, freed)
                t.transpose(ps[:, 2, 0:P], xg[:, slot_], ident[:]).then_inc(e_turned, 1)

            def hidden(par, expert, turned):
                pe.wait_ge(eT_ready, turned)
                t.matmul(ps[:, 0, 0:EH], xgT[:, par], w13[:, ds(expert, 1), 0:EH].rearrange("p a n -> p (a n)"),
                         start=True, stop=True).then_inc(e_a, 1)
                t.matmul(ps[:, 1, 0:EH], xgT[:, par], w13[:, ds(expert, 1), EH:2 * EH].rearrange("p a n -> p (a n)"),
                         start=True, stop=True).then_inc(e_c, 1)

            pe.wait_ge(texi_ready, 1)
            pe.wait_ge(w_exp, 16 * (2 + EC))
            first_expert, = load_registers(nc, mybir.EngineType.PE, texi[0:1, 0:1], E - 1)
            turn_rows(0, 16, None)
            turn_rows(1, 16, 1)
            hidden(0, first_expert, 1)
            with pe.Fori(0, N_TILES // 8) as i:
                experts = load_registers(nc, mybir.EngineType.PE, texi[0:1, ds(i * 8, 9)], E - 1)
                for k in range(1, 9):
                    was, now = experts[k - 1], experts[k]
                    turn_rows((k + 1) % XG, 16 * (i + (k + 1) // XG + 1), i * 8 + k + 1)
                    pe.wait_ge(e_h, i * 8 + k)
                    for c in range(EC):
                        w = min(P, EH - c * P)
                        last = t.transpose(ps[0:w, 3, c * P:(c + 1) * P], eh[:, c * P:c * P + w], ident[:])
                    last.then_inc(eh_turned, 1)
                    hidden(k % 2, now, i * 8 + k + 1)
                    pe.wait_ge(ehT_ready, i * 16 + 2 * k)
                    pe.wait_ge(e_out, i * 8 + k)
                    for c in range(EC):
                        w = min(P, EH - c * P)
                        last = t.matmul(ps[:, 4 + (k - 1) % 2, 0:DM], ehT[0:w, c],
                                        w2s[0:w, ds(was, 1), c, :].rearrange("p a n -> p (a n)"),
                                        start=(c == 0), stop=(c == EC - 1))
                    last.then_inc(e_sum, 1)

        @block.vector
        def _(dve):
            v = nc.vector
            own = Steps(dve, dve_step)

            def loop(count, per):
                return SteppedLoop(dve, own, count, per)

            dve.sem_inc(xT_ready, 2)
            dve.sem_inc(xd_ready, 2)
            dve.sem_inc(dl_ready, 2)
            dve.sem_inc(chunk_done, 1)
            dve.sem_inc(sh_h, 2)
            dve.sem_inc(lg_ready, 1)
            dve.sem_inc(acc_ready, 1)
            dve.wait_ge(w_first, 32)
            for k in range(TAPS):
                v.tensor_tensor(wk[:, k], win[:, 0:DIN], cwb[:, :, k], ALU.mult).then_inc(wk_ready, 1)
            with dve.Fori(0, BATCH) as b:
                with dve.Fori(0, BPS // 2) as h:
                    for r in range(2):
                        n = b * BPS + h * 2 + r
                        dve.wait_ge(x_turned, n + 1)
                        v.tensor_copy(xT[:, ds(b * XTW + h * (2 * BLK) + (r * BLK + HALO), BLK)], ps[:, 6 + r]
                                      ).then_inc(xT_ready, 1)
            dve.wait_ge(w_mix, 16 * 5)
            v.tensor_scalar(alog[:], alog[:], MAX_EXP, None, ALU.min).then_inc(alog_ready, 1)
            with dve.Fori(0, NBLK // 2) as i:
                for r in range(2):
                    cols = ds(i * 2 * BLK + r * BLK, BLK)
                    dve.wait_ge(xd_sum, i * 2 + r + 1)
                    v.tensor_copy(xdl[:, cols], ps[0:RANK, 4]).then_inc(xd_ready, 1)
                    v.tensor_copy(bc[:, cols], ps[RANK:RANK + 2 * NST, 4]).then_inc(xd_ready, 1)
                    dve.wait_ge(u_ready, i * 4 + 2 * r + 4)
                    dve.wait_ge(g_ready, i * 4 + 2 * r + 4)
                    for c in range(DC):
                        v.scalar_tensor_tensor(out=y_all[:, c, cols], in0=u_all[:, c, cols],
                                               scalar=dskip[:, c:c + 1], in1=y_all[:, c, cols],
                                               op0=ALU.mult, op1=ALU.mult).then_inc(y_ready, 1)
            csum_n = csum[:].rearrange("p c b q -> p c (b q)")
            per = 2 * 5
            with loop(NBLK // 2, per) as i:
                for r in range(2):
                    dve.wait_ge(z_ready, i * 4 + 2 * r + 2)
                    zr = z_buf[:, r].rearrange("p c t -> p (c t)")
                    v.tensor_scalar(zr, zr, float(2 ** 40), None, ALU.min).then_inc(z_clamped, 1)
                    dve.wait_ge(z_clamped, i * 2 + r + 1)
                    own.settle(v.scalar_tensor_tensor(out=sq_buf[:, r].rearrange("p c t -> p (c t)"), in0=zr,
                                                      scalar=2.0, in1=zr, op0=ALU.subtract, op1=ALU.mult))
                for r in range(2):
                    cols = ds(i * 2 * BLK + r * BLK, BLK)
                    zr = z_buf[:, r].rearrange("p c t -> p (c t)")
                    lr = ln_buf[:, r].rearrange("p c t -> p (c t)")
                    sr = sq_buf[:, r].rearrange("p c t -> p (c t)")
                    dve.wait_ge(ln_ready, i * 2 + r + 1)
                    own.settle(v.scalar_tensor_tensor(out=lr, in0=zr, scalar=SOFT_CUT, in1=lr,
                                                      op0=ALU.is_ge, op1=ALU.mult))
                    own.settle(v.scalar_tensor_tensor(out=sr, in0=sr, scalar=-0.5, in1=lr,
                                                      op0=ALU.mult, op1=ALU.max))
                    own.settle(v.scalar_tensor_tensor(out=dl_all[:, 0, cols], in0=ps[:, 2 * r],
                                                      scalar=bdel[:, 0:1], in1=sq_buf[:, r, 0],
                                                      op0=ALU.add, op1=ALU.max))
                    v.scalar_tensor_tensor(out=dl_all[:, 1, cols], in0=ps[:, 2 * r + 1],
                                           scalar=bdel[:, 1:2], in1=sq_buf[:, r, 1],
                                           op0=ALU.add, op1=ALU.max).then_inc(dl_ready, 1)
                    dve.wait_ge(dl_ready, i * 2 + r + 3)
                    own.settle(v.tensor_reduce(csum_n[:, :, ds(i * 2 * CPB + r * CPB, CPB)],
                                               dl_all[:, :, cols].rearrange("p c (q t) -> p c q t", t=CH),
                                               AX.X, ALU.add))
            dve.wait_ge(a_exp, 1)
            own.settle(v.tensor_scalar(aneg[:], aneg[:], -1.0 / A_UNIT, None, ALU.mult))
            own.settle(v.tensor_reduce(amax[:], aneg[:], AX.X, ALU.max))
            own.settle(v.memset(rend[:, :, :, CPS - 1:CPS], 0.0))
            dve.wait_ge(consts, 16)
            for c in range(DC):
                for b in range(BATCH):
                    own.settle(v.tensor_tensor_scan(rend[:, c, b, CPS - 2::-1], ones[:, 0:CPS - 1],
                                                    csum[:, c, b, CPS - 1:0:-1], 0.0, ALU.mult, ALU.add))
            own.settle(v.tensor_tensor(live[:], rend[:].rearrange("p c b q -> p c (b q)"),
                                       amax[:].unsqueeze(2).to_broadcast([P, DC, NCH]), ALU.mult))
            v.tensor_scalar(live[:], live[:], DEAD / A_UNIT, None, ALU.is_ge).then_inc(live_ready, 1)
            dve.wait_ge(live_sum, 1)
            pf = ps[0:1, 4, 0:DC * NCH].rearrange("p (c q) -> p q c", c=DC)
            own.settle(v.tensor_reduce(flagf[:], pf, AX.X, ALU.max))
            v.tensor_scalar(flags[:], flagf[:], 1.0, None, ALU.min).then_inc(flags_ready, 1)
            dve.wait_ge(flags_ready, 1)

            STEPS_PER_CHUNK = 2 * 2 + 4 + DC * 11

            def chunk(q):
                col0 = q * CH
                dve.wait_ge(chunk_done, q + 1)
                rend_q = rend[:].rearrange("p c b q -> p c (b q)")
                own.settle(v.tensor_copy(dch[:], dl_all[:, :, ds(col0, CH)]))
                for c in range(DC):
                    own.settle(v.tensor_copy(rch[:, c, CH - 1:CH], rend_q[:, c, ds(q, 1)]))
                for c in range(DC):
                    own.settle(v.tensor_tensor_scan(rch[:, c, CH - 2::-1], ones[:, 0:CH - 1],
                                                    dch[:, c, CH - 1:0:-1],
                                                    rch[:, c, CH - 1:CH], ALU.mult, ALU.add))
                for c in range(DC):
                    last = v.tensor_tensor(gain[:, c], rch[:, c, :].unsqueeze(1).to_broadcast([P, NST, CH]),
                                           aneg[:, c, :].unsqueeze(2).to_broadcast([P, NST, CH]), ALU.mult)
                own.settle(last)
                dve.wait_ge(za_raw, q + 1)
                v.tensor_scalar(decay[:], decay[:], 0.0, FLOOR / A_UNIT, ALU.min, ALU.max).then_inc(za_ready, 1)
                v.tensor_scalar(gain[:], gain[:], 0.0, FLOOR / A_UNIT, ALU.min, ALU.max).then_inc(zr_ready, 1)
                own.settle(v.tensor_tensor(du[:], dch[:], u_all[:, :, ds(col0, CH)], ALU.mult))
                dve.wait_ge(b_sum, q + 1)
                dve.wait_ge(decay_ready, q + 1)
                for c in range(DC):
                    bvals = ps[:, 4:6].rearrange("p a (n t) -> p (a n) t", t=CH)
                    cvals = ps[:, 6:8].rearrange("p a (n t) -> p (a n) t", t=CH)
                    own.settle(v.tensor_tensor(dbu, bvals, du[:, c, :].unsqueeze(1).to_broadcast([P, NST, CH]), ALU.mult))
                    own.settle(v.tensor_tensor(hmul[:], decay[:, c, :, 0], hcar[:, c], ALU.mult))
                    own.settle(v.tensor_tensor(dbu[:, :, 0], dbu[:, :, 0], hmul[:], ALU.add))
                    own.settle(v.memset(decay[:, c, :, 0], 0.0))
                    own.settle(v.tensor_tensor_scan(scratch[:, 5, :], decay[:, c].rearrange("p n t -> p (n t)"),
                                                    scratch[:, 4, :], 0.0, ALU.mult, ALU.add))
                    own.settle(v.tensor_copy(hcar[:, c], hs[:, :, CH - 1]))
                    if c == 0:
                        dve.wait_ge(gain_ready, q + 1)
                        own.settle(v.tensor_tensor(gch[:], gch[:], ps[:, 2, 0:DC * CH].rearrange(
                            "p (c t) -> p c t", c=DC), ALU.mult))
                    own.settle(v.tensor_tensor(scratch[:, 5, :], scratch[:, 5, :],
                                               gain[:, c].rearrange("p n t -> p (n t)"), ALU.mult))
                    if c == 0:
                        dve.wait_ge(c_sum, q + 1)
                    own.settle(v.tensor_tensor(hs, cvals, hs, ALU.mult))
                    own.settle(v.tensor_reduce(ysum[:], hs.rearrange("p n t -> p t n"), AX.X, ALU.add))
                    own.settle(v.tensor_tensor(ysum[:], ysum[:], gch[:, c], ALU.mult))
                    own.settle(v.tensor_tensor(y_all[:, c, ds(col0, CH)], y_all[:, c, ds(col0, CH)], ysum[:], ALU.add))
                dve.wait_ge(zr_ready, q + 1)
                v.nop().then_inc(chunk_done, 1)

            def skip(n, q):
                own.count, own.shift = start, q * STEPS_PER_CHUNK
                own.settle(v.memset(hcar[:], 0.0))
                own.count, own.shift = start, 0
                dve.sem_inc(za_ready, n)
                dve.sem_inc(zr_ready, n)
                dve.sem_inc(dve_step, n * STEPS_PER_CHUNK - 1)
                dve.sem_inc(chunk_done, n)

            start = own.count

            def counted(q, b):
                own.count, own.shift = start, q * STEPS_PER_CHUNK
                chunk(q)
                assert own.count == start + STEPS_PER_CHUNK, own.count - start
                own.count, own.shift = start, 0

            def start_batch(b):
                v.memset(hcar[:], 0.0).then_inc(batch_start, 1)
                dve.wait_ge(batch_start, b + 1)
                hold(dve, dve_held)

            dve.wait_ge(y_ready, DC * NBLK)
            chunk_loops(dve, v, mybir.EngineType.DVE, counted, skip, start_batch)
            own.count = start + NCH * STEPS_PER_CHUNK

            def statistics(rows, r, n, done):
                hold(dve, dve_held)
                for j in range(TPB):
                    last = v.bn_stats(bst[:, r, j], rows(j))
                own.settle(last)
                hold(dve, dve_held)
                for j in range(TPB):
                    last = v.bn_aggr(bag[:, r, j], bst[:, r, j])
                last.then_inc(done, 1)
                dve.wait_ge(done, n + 1)

            def residual(n, r):
                tiles = ds(n * TPB, TPB)
                dve.wait_ge(mix_sum, n + 1)
                v.tensor_tensor(res1[:, tiles, :], ps[:, r].rearrange("p (i d) -> p i d", d=DM), res1[:, tiles, :],
                                ALU.add).then_inc(res_ready, 1)
                dve.wait_ge(res_ready, n + 1)
                statistics(lambda j: res1[:, ds(n * TPB + j, 1), :].rearrange("p a d -> p (a d)"), r, n, var_ready)

            def layer_norm(n, r):
                dve.wait_ge(rstd_ready, n + 1)
                for j in range(TPB):
                    last = v.tensor_scalar(x1b[:, r, j], res1[:, ds(n * TPB + j, 1), :].rearrange("p a d -> p (a d)"),
                                           bag[:, r, j, 0:1], rstd[:, r, j:j + 1], ALU.subtract, ALU.mult)
                last.then_inc(x1_ready, 1)

            def two_blocks(i, last_two):
                for r in range(2):
                    n = i * 2 + r
                    dve.wait_ge(gate_sum, n + 1)
                    v.tensor_copy(lg[:, ds(n * TPB, TPB), :],
                                  ps[:, 2, 0:TPB * E].rearrange("p (i e) -> p i e", e=E)).then_inc(lg_ready, 1)
                    for h in range(2):
                        dve.wait_ge(sh_silu, n * 2 + h + 1)
                        dve.wait_ge(sh_c, n * 2 + h + 1)
                        v.tensor_tensor(shT[:, r, h], ps[0:SHH, 6 + h], sgate[:, h], ALU.mult).then_inc(sh_h, 1)
                    if not last_two:
                        residual(n + 2, r)
                    dve.wait_ge(sh_sum, n + 1)
                    v.tensor_tensor(acc[:, ds(n * TPB, TPB), :],
                                    ps[:, 3].rearrange("p (i d) -> p i d", d=DM), x1b[:, r],
                                    ALU.add).then_inc(acc_ready, 1)
                    if not last_two:
                        dve.wait_ge(x1_stored[r], 16 * (i + 2))
                        dve.wait_ge(x1_turned, n + 1)
                        dve.wait_ge(acc_ready, n + 2)
                        layer_norm(n + 2, r)

            dve.wait_ge(gwT_sum, 1)
            v.tensor_copy(gwT[:], ps[:, 3, 0:E]).then_inc(gwT_ready, 1)
            for r in range(2):
                dve.wait_ge(xres_in[r], 16)
            for r in range(2):
                residual(r, r)
            for r in range(2):
                layer_norm(r, r)
            dve.wait_ge(x1_ready, 2)
            with loop(NBLK // 2 - 1, 2) as i:
                two_blocks(i, False)
            two_blocks(NBLK // 2 - 1, True)

            def over_e(a):
                return a.unsqueeze(2).to_broadcast([P, TILES, E])

            def over_t(a):
                return a.unsqueeze(1).to_broadcast([P, TILES, E])

            dve.wait_ge(lg_ready, NBLK + 1)
            own.settle(v.tensor_reduce(col[:], lg[:], AX.X, ALU.max))
            v.tensor_tensor(t3[:], lg[:], over_e(col[:]), ALU.subtract).then_inc(lgx_ready, 1)
            dve.wait_ge(sce_ready, 1)
            own.settle(v.tensor_reduce(col[:], sc[:], AX.X, ALU.add))
            own.settle(v.reciprocal(col[:], col[:]))
            own.settle(v.tensor_tensor(sc[:], sc[:], over_e(col[:]), ALU.mult))
            for k, m in enumerate((m1, m2)):
                own.settle(v.tensor_reduce(wk2[:, k], sc[:], AX.X, ALU.max))
                own.settle(v.tensor_tensor(t3[:], sc[:], over_e(wk2[:, k]), ALU.is_equal))
                own.settle(v.tensor_tensor(t3[:], t3[:], over_t(desc[:]), ALU.mult))
                own.settle(v.tensor_reduce(col[:], t3[:], AX.X, ALU.max))
                own.settle(v.tensor_tensor(m[:], t3[:], over_e(col[:]), ALU.is_equal))
                if k == 0:
                    own.settle(v.scalar_tensor_tensor(out=sc[:].rearrange("p t e -> p (t e)"),
                                                      in0=m1[:].rearrange("p t e -> p (t e)"), scalar=-2.0,
                                                      in1=sc[:].rearrange("p t e -> p (t e)"),
                                                      op0=ALU.mult, op1=ALU.add))
            v.tensor_tensor(rk[:], m1[:], m2[:], ALU.add).then_inc(m_ready, 1)
            dve.wait_ge(rank_sum, 1)
            within = ps[:, 4, 0:TILES * E].rearrange("p (t e) -> p t e", e=E)
            totals = ps[:, 5, 0:TILES * E].rearrange("p (t e) -> p t e", e=E)
            own.settle(v.memset(ex[:, 0, :], 0.0))
            for e in range(E):
                own.settle(v.tensor_tensor_scan(ex[:, 1:TILES, e], ones[:, 0:TILES - 1], totals[:, 0:TILES - 1, e],
                                                0.0, ALU.mult, ALU.add))
            own.settle(v.tensor_tensor(cnt[:], totals[:, TILES - 1, :], ex[:, TILES - 1, :], ALU.add))
            own.settle(v.tensor_scalar(cnti[:], cnt[:], float(P - 1), None, ALU.add))
            own.settle(v.tensor_scalar(nti[:], cnti[:], 7, None, ALU.logical_shift_right))
            own.settle(v.tensor_copy(ntf[:], nti[:]))
            own.settle(v.tensor_tensor_scan(tend[:], ones[:, 0:E], ntf[:], 0.0, ALU.mult, ALU.add))
            own.settle(v.tensor_tensor(tbeg[:], tend[:], ntf[:], ALU.subtract))
            own.settle(v.tensor_scalar(tbeg[:], tbeg[:], float(P), None, ALU.mult))
            own.settle(v.tensor_tensor(ex[:], within, ex[:], ALU.add))
            own.settle(v.tensor_tensor(ex[:], ex[:], over_t(tbeg[:]), ALU.add))
            for k, m in enumerate((m1, m2)):
                own.settle(v.tensor_tensor(t3[:], m[:], ex[:], ALU.mult))
                own.settle(v.tensor_reduce(slot[:, k], t3[:], AX.X, ALU.add))
            own.settle(v.tensor_copy(sloti[:], slot[:]))
            own.settle(v.tensor_scalar(hii[:], sloti[:], 7, None, ALU.logical_shift_right))
            own.settle(v.tensor_scalar(loi[:], sloti[:], P - 1, None, ALU.bitwise_and))
            own.settle(v.tensor_copy(hif[:], hii[:].rearrange("p k t -> p t k")))
            own.settle(v.tensor_copy(lof[:], loi[:].rearrange("p k t -> p t k")))
            own.settle(v.tensor_tensor(tex[:], tex[:], tend[0:1, :].unsqueeze(1).to_broadcast([1, IDXC, E]), ALU.is_ge))
            own.settle(v.tensor_reduce(texs[:], tex[:], AX.X, ALU.add))
            v.tensor_scalar(texi[:], texs[:], float(E - 1), None, ALU.min).then_inc(texi_ready, 1)
            hi_cols, lo_cols, t_cols = (a[:].rearrange("p t k -> p (t k)") for a in (hif, lof, tcol))
            with loop(TILES * K // GROUP // 2, 2) as i:
                for r in range(2):
                    pairs = ds(i * 2 * GROUP + r * GROUP, GROUP)
                    dve.wait_ge(oh_sum, i * 2 + r + 1)
                    own.settle(v.tensor_tensor(ohe, iota[:, 0:N_TILES].unsqueeze(1).to_broadcast([P, GROUP, N_TILES]),
                                               hi_cols[:, pairs].unsqueeze(2).to_broadcast([P, GROUP, N_TILES]),
                                               ALU.is_equal))
                    v.tensor_scalar(ohh[:, r, :, 0], ohe, pcol[:], None, ALU.mult)
                    v.tensor_tensor(ohh[:, r, :, 1], ohe,
                                    t_cols[:, pairs].unsqueeze(2).to_broadcast([P, GROUP, N_TILES]), ALU.mult)
                    v.tensor_tensor(ohl[:, r], iota[:].unsqueeze(1).to_broadcast([P, GROUP, P]),
                                    lo_cols[:, pairs].unsqueeze(2).to_broadcast([P, GROUP, P]),
                                    ALU.is_equal).then_inc(oh_ready, 1)
                    dve.wait_ge(oh_ready, i * 2 + r + 1)
            dve.wait_ge(oh_sum, TILES * K // GROUP + 3)
            own.settle(v.tensor_copy(pid[:], ps[:, 3, 0:2 * N_TILES].rearrange("p (a n) -> p a n", a=2)))
            own.settle(v.tensor_scalar(tokf[:], pid[:, 1], float(P), -float(P), ALU.mult, ALU.add))
            own.settle(v.tensor_tensor(tokf[:], tokf[:], pid[:, 0], ALU.add))
            own.settle(v.tensor_copy(toki[:], tokf[:]))
            own.settle(v.tensor_scalar(idx_src[:, 0:N_TILES], toki[:], TOK - 1, None, ALU.bitwise_and))
            own.settle(v.tensor_scalar(dstf[:], tokf[:], 0.0, float(NO_ROW), ALU.is_lt, ALU.mult))
            own.settle(v.tensor_tensor(idx_dst[:, 0:N_TILES], dstf[:], tokf[:], ALU.add))
            v.tensor_copy(ring_src[:], idx_src[:, 0:2 * HALF].rearrange("p (h n) -> p h n", h=2)).then_inc(src_ready, 1)
            v.tensor_copy(ring_dst[:, 0], idx_dst[:, 0:HALF]).then_inc(dst_ready, 1)

            def rows_out(par, turned):
                dve.wait_ge(e_turned, turned)
                v.tensor_copy(xgT[:, par], ps[:, 2, 0:P]).then_inc(eT_ready, 1)

            def gated(n):
                dve.wait_ge(e_c, n)
                dve.wait_ge(e_silu, n)
                v.tensor_tensor(eh, ps[:, 1, 0:EH], egate, ALU.mult).then_inc(e_h, 1)

            rows_out(0, 1)
            rows_out(1, 2)
            gated(1)

            def eight_tiles(i, first):
                for k in range(1, 9):
                    if k in (4, 8):
                        g_ = k // HALF
                        for r in range(4 if k == 8 or not first else 0):
                            dve.wait_ge(scattered[r], 16 * (i * 2 + g_ - 1))
                        v.tensor_copy(ring_dst[:, g_ % 2], idx_dst[:, ds(i * 8 + g_ * HALF, HALF)]).then_inc(dst_ready, 1)
                    dve.wait_ge(e_c, i * 8 + k)
                    rows_out((k + 1) % 2, i * 8 + k + 2)
                    if k in (2, 6):
                        g_ = (k + 6) // HALF
                        v.tensor_copy(ring_src[:, g_ % 2], idx_src[:, ds(i * 8 + g_ * HALF, HALF)]).then_inc(src_ready, 1)
                    dve.wait_ge(eh_turned, i * 8 + k)
                    v.tensor_copy(ehT[:, 0:2], ps[:, 3, 0:2 * P].rearrange("p (c t) -> p c t", c=2)).then_inc(ehT_ready, 1)
                    v.tensor_copy(ehT[0:EH - 2 * P, 2], ps[0:EH - 2 * P, 3, 2 * P:3 * P]).then_inc(ehT_ready, 1)
                    gated(i * 8 + k + 1)

            eight_tiles(0, True)
            with dve.Fori(1, N_TILES // 8) as i:
                eight_tiles(i, False)

            with loop(NBLK // FIN, FIN * 3) as i:
                for r in range(FIN):
                    n = i * FIN + r
                    tiles = ds(n * TPB, TPB)
                    dve.wait_ge(y0_scaled, n + 1)
                    own.settle(v.tensor_tensor(acc[:, tiles, :], acc[:, tiles, :], y0r[:, r], ALU.add))
                    for j in range(TPB):
                        row = acc[:, ds(n * TPB + j, 1), :].rearrange("p a d -> p (a d)")
                        last = v.scalar_tensor_tensor(out=row, in0=y1r[:, r, j],
                                                      scalar=wk2[:, 1, ds(n * TPB + j, 1)], in1=row,
                                                      op0=ALU.mult, op1=ALU.add)
                    own.settle(last)
                    v.nop().then_inc(fin_read, 1)
                    dve.wait_ge(o_ready, n + 1)
                    statistics(lambda j: acc[:, ds(n * TPB + j, 1), :].rearrange("p a d -> p (a d)"), r % 2, n, fvar_ready)


_INS = ['L0_attn_x', 'L0_attn_W_in', 'L0_attn_conv_w', 'L0_attn_W_x', 'L0_attn_W_delta', 'L0_attn_b_delta',
        'L0_attn_A_log', 'L0_attn_D', 'L0_attn_W_out', 'L0_ffn_gate_w', 'L0_ffn_w1', 'L0_ffn_w2', 'L0_ffn_w3',
        'L0_ffn_sw1', 'L0_ffn_sw2', 'L0_ffn_sw3']
_OUTS = [((BATCH, SEQ, DM), 'float32')]


def kernel(**inputs):
    import numpy as _np
    import concourse.bacc as _bacc
    from concourse import mybir as _mybir
    from concourse.bass_utils import run_bass_kernel_spmd as _run

    nc = _bacc.Bacc("TRN2", target_bir_lowering=False, num_devices=1)
    arrays, args = {}, []
    for name in _INS:
        a = _np.ascontiguousarray(inputs[name])
        arrays[f"in_{name}_dram"] = a
        args.append(nc.dram_tensor(f"in_{name}_dram", a.shape, _mybir.dt.from_np(a.dtype), kind="ExternalInput").ap())
    for i, (shape, dtype) in enumerate(_OUTS):
        dt = _mybir.dt.from_np(_np.dtype(dtype))
        args.append(nc.dram_tensor(f"out_{i}_dram", shape, dt, kind="ExternalOutput").ap())
    build(nc, *args)
    r = _run(nc, [arrays], core_ids=[0])
    got = tuple(r.results[0][f"out_{i}_dram"] for i in range(len(_OUTS)))
    return got[0]
```

```python
from contextlib import ExitStack

import concourse.bass as bass
from concourse import mybir

F32 = mybir.dt.float32
F32R = mybir.dt.float32r
BF16 = mybir.dt.bfloat16
I32 = mybir.dt.int32
U32 = mybir.dt.uint32
ACT = mybir.ActivationFunctionType
ALU = mybir.AluOpType
AX = mybir.AxisListType

P = 128
BATCH, SEQ, DM = 2, 2048, 128
TOK = BATCH * SEQ
DIN, NST, RANK, TAPS = 256, 16, 64, 3
DC = DIN // P
BLK = 512
NBLK = TOK // BLK
TPB = BLK // P
TILES = TOK // P
HALO = TAPS - 1
XTW = SEQ + HALO
CH = 32
CHN = NST * CH
NPB = BLK // CH
CBK = CHN // BLK
CPB = BLK // CH
NCH = TOK // CH
CPS = SEQ // CH
BPS = SEQ // BLK
SECTIONS = [(CPS - (CPS >> k), CPS >> (k + 1)) for k in range(CPS.bit_length() - 1)] + [(CPS - 1, 1)]
PARTS = 3 * 2 * NST
E, K = 8, 2
EH = 352
EC = 3
SH = 192
SHH = SH // 2
N_TILES = TOK * K // P + E
GROUP = 4 * K
HALF = 4
XG = 8
AHEAD = 5
IDXC = N_TILES + 2 * HALF
FIN = 4
LN_EPS = 1e-5
NEG_LN_SCAN_EPS = 27.631021115928547
DEAD = -104.0
MAX_EXP = 88.5
FLOOR = -200.0
A_UNIT = float(2 ** 30)
SOFT_CUT = 1.0 / 256.0
NO_ROW = 1 << 20


class Steps:

    def __init__(self, engine, semaphore):
        self.engine, self.semaphore, self.count, self.shift = engine, semaphore, 0, 0

    def settle(self, instruction):
        instruction.then_inc(self.semaphore, 1)
        self.count += 1
        self.engine.wait_ge(self.semaphore, self.count + self.shift)


class SteppedLoop:

    def __init__(self, engine, steps, count, per):
        self.loop, self.steps, self.turns, self.per = engine.Fori(0, count), steps, count, per

    def __enter__(self):
        i = self.loop.__enter__()
        self.start = self.steps.count
        self.steps.shift = i * self.per
        return i

    def __exit__(self, *what):
        if what[0] is None:
            assert self.steps.count == self.start + self.per, self.steps.count - self.start
        self.steps.shift = 0
        self.steps.count = self.start + self.turns * self.per
        return self.loop.__exit__(*what)


def hold(engine, waited):
    engine.sem_inc(waited, 1)


def ds(start, size):
    return bass.ds(start, size)


def load_registers(nc, engine_type, values, top):
    _, registers = nc.values_load_multi_w_load_instructions(
        values, engines=(engine_type,), min_val=0, max_val=top,
        skip_runtime_bounds_check_because="the instruction that makes them clamps them, and sums of 0 and 1 are not negative")
    return registers


def build(nc, x, W_in, conv_w, W_x, W_delta, b_delta, A_log, D, W_out,
          gate_w, w1, w2, w3, sw1, sw2, sw3, out):
    with ExitStack() as ctx:
        def sb(name, shape, dt=F32):
            return ctx.enter_context(nc.sbuf_tensor(name, shape, dt))

        def sem(name):
            return ctx.enter_context(nc.semaphore(name))

        dl_all = sb("dl_all", [P, DC, TOK])
        xT = sb("xT", [P, BATCH * XTW])
        low = sb("low", [P, TOK])
        bc_arena = sb("bc_arena", [P, 2 * BLK])
        bcrest = sb("bcrest", [2 * NST, 2, BLK])
        bcmid = sb("bcmid", [2 * NST, 2, BLK], BF16)
        bc3 = sb("bc3", [PARTS, TOK], BF16)
        sel3 = sb("sel3", [PARTS, 2 * NST], BF16)
        scratch = sb("scratch", [P, 6, DC * BLK])

        xdl = low[0:RANK]
        bc = bc_arena[0:2 * NST].rearrange("p (r t) -> p r t", r=2)
        csb = bc_arena[:, 0:CHN].rearrange("p (n t) -> p n t", n=NST)
        acc = xT[:, 0:TOK].rearrange("p (t d) -> p t d", d=DM)
        df = dl_all[:].rearrange("p c t -> p (c t)")
        res1 = low[:].rearrange("p (t d) -> p t d", d=DM)
        x1b = df[:, TOK:TOK + 2 * BLK].rearrange("p (r i d) -> p r i d", r=2, d=DM)
        x1T = df[:, TOK + 2 * BLK:TOK + 4 * BLK].rearrange("p (r t) -> p r t", r=2)
        shT = df[0:SHH, TOK + 4 * BLK:TOK + 8 * BLK].rearrange("p (r h t) -> p r h t", r=2, h=2)
        y0r, y1r, outr = (df[:, m * FIN * BLK:(m + 1) * FIN * BLK].rearrange("p (r i d) -> p r i d", r=FIN, d=DM)
                          for m in range(3))
        w1x = df[:, 0:E * EH].rearrange("p (e n) -> p e n", e=E)
        w3x = low[:, 0:E * EH].rearrange("p (e n) -> p e n", e=E)
        w2s = df[:, 0:E * EC * DM].rearrange("p (e c n) -> p e c n", e=E, c=EC)
        xin = df[:, 0:TOK].rearrange("p (n i d) -> p n i d", i=TPB, d=DM)
        z_buf = scratch[:, 0:2, :].rearrange("p r (c t) -> p r c t", c=DC)
        ln_buf = scratch[:, 2:4, :].rearrange("p r (c t) -> p r c t", c=DC)
        sq_buf = scratch[:, 4:6, :].rearrange("p r (c t) -> p r c t", c=DC)
        decay = scratch[:, 0:2, 0:CHN].rearrange("p c (n t) -> p c n t", n=NST)
        gain = scratch[:, 2:4, 0:CHN].rearrange("p c (n t) -> p c n t", n=NST)
        hs = scratch[:, 4:6, 0:CHN].rearrange("p c (n t) -> p c n t", n=NST)
        ybuf = scratch[:, 0:2, :].rearrange("p r (c t) -> p r c t", c=DC)
        sgate = scratch[0:SHH, 4, :].rearrange("p (h t) -> p h t", h=2)
        sf = scratch[:].rearrange("p a n -> p (a n)").bitcast(BF16)
        oh_at = [0, 2 * GROUP * P, 2 * GROUP * (P + 2 * N_TILES), 2 * GROUP * (P + 3 * N_TILES)]
        ohl = sf[:, oh_at[0]:oh_at[1]].rearrange("p (r g n) -> p r g n", r=2, g=GROUP)
        ohh = sf[:, oh_at[1]:oh_at[2]].rearrange("p (r g a n) -> p r g a n", r=2, g=GROUP, a=2)
        ohe = sf[:, oh_at[2]:oh_at[3]].rearrange("p (r g n) -> p r g n", r=2, g=GROUP)
        xg = scratch[:, 0, :].rearrange("p (r d) -> p r d", r=XG)
        egate = scratch[:, 1, 0:EH]
        eh = scratch[:, 1, 512:512 + EH]
        ehT = scratch[:, 2, 0:EC * P].rearrange("p (c t) -> p c t", c=EC)
        yo = scratch[:, 3, 0:4 * DM].rearrange("p (r d) -> p r d", r=4)

        win = sb("win", [P, 2 * DIN])
        cwb = sb("cwb", [P, DIN, TAPS])
        wk = sb("wk", [P, TAPS, DIN])
        wx = sb("wx", [P, DC, RANK + 2 * NST])
        wdel = sb("wdel", [RANK, DIN])
        bdel = sb("bdel", [P, DC])
        dskip = sb("dskip", [P, DC])
        alog = sb("alog", [P, DC, NST])
        aneg = sb("aneg", [P, DC, NST])
        amax = sb("amax", [P, DC])
        wout = sb("wout", [P, DC, DM])
        gw = sb("gw", [E, DM])
        gwT = sb("gwT", [P, E])
        s1 = sb("s1", [P, SH])
        s3 = sb("s3", [P, SH])
        s2 = sb("s2", [SHH, 2, DM])
        ident = sb("ident", [P, P])
        ones = sb("ones", [P, P])
        before = sb("before", [P, P])
        iota = sb("iota", [P, P])
        pcol = sb("pcol", [P, 1])
        csum = sb("csum", [P, DC, BATCH, CPS])
        rend = sb("rend", [P, DC, BATCH, CPS])
        dch = sb("dch", [P, DC, CH])
        rch = sb("rch", [P, DC, CH])
        live = sb("live", [P, DC, NCH])
        flagf = sb("flagf", [1, CPS])
        flagr = sb("flagr", [1, 1])
        flags = sb("flags", [1, 1], I32)
        hcar = sb("hcar", [P, BATCH, DC, NST])
        hmul = sb("hmul", [P, NST])
        du = sb("du", [P, DC, CH])
        ysum = sb("ysum", [P, CH])
        gch = sb("gch", [P, DC, CH])
        bst = sb("bst", [P, 2, TPB, 6])
        bag = sb("bag", [P, 2, TPB, 2])
        vare = sb("vare", [P, 2, TPB])
        rstd = sb("rstd", [P, 2, TPB])
        shift = sb("shift", [P, 2, TPB])
        lnc = sb("lnc", [P, 3, TPB])
        epst = sb("epst", [P, 4])
        lg = sb("lg", [P, TILES, E])
        sc = sb("sc", [P, TILES, E])
        t3 = sb("t3", [P, TILES, E])
        m1 = sb("m1", [P, TILES, E])
        m2 = sb("m2", [P, TILES, E])
        rk = sb("rk", [P, TILES, E])
        ex = sb("ex", [P, TILES, E])
        col = sb("col", [P, TILES])
        wk2 = sb("wk2", [P, K, TILES])
        slot = sb("slot", [P, K, TILES])
        sloti = sb("sloti", [P, K, TILES], I32)
        hii = sb("hii", [P, K, TILES], I32)
        loi = sb("loi", [P, K, TILES], I32)
        hif = sb("hif", [P, TILES, K])
        lof = sb("lof", [P, TILES, K])
        cnt = sb("cnt", [P, E])
        cnti = sb("cnti", [P, E], I32)
        nti = sb("nti", [P, E], I32)
        ntf = sb("ntf", [P, E])
        tend = sb("tend", [P, E])
        tbeg = sb("tbeg", [P, E])
        desc = sb("desc", [P, E])
        tcol = sb("tcol", [P, TILES, K])
        tex = sb("tex", [1, IDXC, E])
        texs = sb("texs", [1, IDXC])
        texi = sb("texi", [1, IDXC], I32)
        zer = sb("zer", [P, 2 * N_TILES], BF16)
        pid = cwb[:].rearrange("p d k -> p (d k)")[:, 0:2 * N_TILES].rearrange("p (a n) -> p a n", a=2)
        tokf, dstf = (cwb[:].rearrange("p d k -> p (d k)")[:, m * N_TILES:(m + 1) * N_TILES] for m in (2, 3))
        toki = sb("toki", [P, N_TILES], I32)
        idx_src = sb("idx_src", [P, IDXC], I32)
        idx_dst = sb("idx_dst", [P, IDXC], I32)
        ring_src = sb("ring_src", [P, 2, HALF], I32)
        ring_dst = sb("ring_dst", [P, 2, HALF], I32)

        xgT = sb("xgT", [P, 2, 2, P], F32R)

        with (nc.sbuf_tensor("y_all", [P, DC, TOK], F32) as y_all,
              nc.sbuf_tensor("u_all", [P, DC, TOK], F32) as u_all):
            pass
        x1T_all = sb("x1T_all", [P, TOK])
        w13h = sb("w13h", [P, E, 2, EH], F32R)
        w13l = sb("w13l", [P, E, 2, EH], F32R)

        ps = ctx.enter_context(nc.psum_tensor("ps", [P, 8, BLK], F32))

        x1_rows = nc.dram_tensor("x1_rows", [TOK, DM], F32).ap()
        y_rows = nc.dram_tensor("y_rows", [K * TOK, DM], F32).ap()

        x_in = [sem(f"x_in{m}") for m in range(NBLK // 2)]
        w_exp1, w_exp3 = sem("w_exp1"), sem("w_exp3")
        w_alog, w_first, w_mix, w_ffn, w_exp = sem("w_alog"), sem("w_first"), sem("w_mix"), sem("w_ffn"), sem("w_exp")
        const_step, consts, halo = sem("const_step"), sem("consts"), sem("halo")
        pool_held, act_held, dve_held = sem("pool_held"), sem("act_held"), sem("dve_held")
        pool_step, dve_step = sem("pool_step"), sem("dve_step")
        wk_ready, alog_ready = sem("wk_ready"), sem("alog_ready")
        gwT_sum, gwT_ready = sem("gwT_sum"), sem("gwT_ready")
        x_turned, xT_even, xT_odd = sem("x_turned"), sem("xT_even"), sem("xT_odd")
        ug_sum, ug_ready = sem("ug_sum"), sem("ug_ready")
        xd_sum, xd_ready, y_ready = sem("xd_sum"), sem("xd_ready"), sem("y_ready")
        pd_sum, z_ready, z_clamped, ln_ready = sem("pd_sum"), sem("z_ready"), sem("z_clamped"), sem("ln_ready")
        dl_ready, a_exp = sem("dl_ready"), sem("a_exp")
        live_ready, live_sum, flags_ready = sem("live_ready"), sem("live_sum"), sem("flags_ready")
        bc_rounded, bc_split, sel_ready = sem("bc_rounded"), sem("bc_split"), sem("sel_ready")
        b_sum, c_sum, za_raw = sem("b_sum"), sem("c_sum"), sem("za_raw")
        csb_ready, gc_ready, scan_done, res_again = sem("csb_ready"), sem("gc_ready"), sem("scan_done"), sem("res_again")
        za_ready, zr_ready, decay_ready, gain_ready = sem("za_ready"), sem("zr_ready"), sem("decay_ready"), sem("gain_ready")
        chunk_done = sem("chunk_done")
        yb_ready, mix_sum, res_ready = sem("yb_ready"), sem("mix_sum"), sem("res_ready")
        xres_in = [sem(f"xres_in{r}") for r in range(2)]
        var_ready, rstd_ready = sem("var_ready"), sem("rstd_ready")
        x1_ready, x1_turned, x1T_ready = sem("x1_ready"), sem("x1_turned"), sem("x1T_ready")
        x1_kept, x1T_kept = sem("x1_kept"), sem("x1T_kept")
        x1_stored = [sem(f"x1_stored{r}") for r in range(2)]
        gate_sum, lg_ready = sem("gate_sum"), sem("lg_ready")
        sh_a, sh_c, sh_silu, sh_h, sh_sum, acc_ready = (sem("sh_a"), sem("sh_c"), sem("sh_silu"),
                                                        sem("sh_h"), sem("sh_sum"), sem("acc_ready"))
        lgx_ready, sce_ready = sem("lgx_ready"), sem("sce_ready")
        m_ready, rank_sum = sem("m_ready"), sem("rank_sum")
        ohe_ready, oht_ready = sem("ohe_ready"), sem("oht_ready")
        oh_ready, oh_sum = sem("oh_ready"), sem("oh_sum")
        texi_ready = sem("texi_ready")
        src_ready, dst_ready = sem("src_ready"), sem("dst_ready")
        gathered = [sem(f"gathered{r}") for r in range(XG)]
        scattered = [sem(f"scattered{r}") for r in range(4)]
        wh_ready, wl_ready, eT_high = sem("wh_ready"), sem("wl_ready"), sem("eT_high")
        e_turned, eT_ready, e_a, e_c, e_silu, e_h = (sem("e_turned"), sem("eT_ready"), sem("e_a"),
                                                     sem("e_c"), sem("e_silu"), sem("e_h"))
        eh_turned, ehT_ready, e_sum, e_out = sem("eh_turned"), sem("ehT_ready"), sem("e_sum"), sem("e_out")
        y_in = [sem(f"y_in{r}") for r in range(FIN)]
        y0_scaled, y0_added, fin_read, fvar_ready = sem("y0_scaled"), sem("y0_added"), sem("fin_read"), sem("fvar_ready")
        frstd_ready, o_ready = sem("frstd_ready"), sem("o_ready")
        o_stored = [sem(f"o_stored{r}") for r in range(FIN)]

        x_rows = x.rearrange("b s d -> (b s) d").rearrange("(n i p) d -> n p i d", i=TPB, p=P)
        o_rows = out.rearrange("b s d -> (b s) d").rearrange("(n i p) d -> n p i d", i=TPB, p=P)
        x1_blocks = x1_rows.rearrange("(n i p) d -> n p i d", i=TPB, p=P)
        y_blocks = y_rows.rearrange("(k n i p) d -> k n p i d", k=K, i=TPB, p=P)

        def row_block(view, n):
            return view[ds(n, 1)].rearrange("a p i d -> (a p) i d")

        def xT_block(n):
            start = n // BPS * XTW + HALO + n % BPS * BLK
            return xT[:, start:start + BLK]

        def chunk_loops(engine, ops, which, chunk, skip):
            dead, = load_registers(nc, which, flags[0:1, 0:1], CPS)

            for first, count in SECTIONS:
                with engine.If(first + count - dead > 0):
                    if count > 1:
                        with engine.Fori(first, first + count) as q:
                            for b in range(BATCH):
                                chunk(q, b, q * BATCH + b)
                    else:
                        for b in range(BATCH):
                            chunk(first, b, first * BATCH + b)
                    ops.nop()
                with engine.Else():
                    skip(count * BATCH, first * BATCH)
                ops.nop()

        block = ctx.enter_context(nc.Block())

        @block.sync
        def _(sp):
            for r in range(2):
                sp.sem_inc(x1_stored[r], 16)
            for r in range(FIN):
                sp.sem_inc(o_stored[r], 16)
            sp.dma_start(xin[:, 0:2], x_rows[0:2].rearrange("n p i d -> p n i d")).then_inc(x_in[0], 16)
            sp.dma_start(win[:], W_in).then_inc(w_first, 16)
            sp.dma_start(cwb[:].rearrange("p d k -> p (d k)"),
                         conv_w.rearrange("d a k -> (a d k)").partition_broadcast(P)).then_inc(w_first, 16)
            sp.dma_start(alog[:], A_log.rearrange("(c p) n -> p c n", p=P)).then_inc(w_alog, 16)
            for m in range(1, NBLK // 2):
                sp.dma_start(xin[:, 2 * m:2 * m + 2], x_rows[2 * m:2 * m + 2].rearrange("n p i d -> p n i d")
                             ).then_inc(x_in[m], 16)
            mix_loads = [
                (wx[:], W_x.rearrange("(c p) n -> p c n", p=P)),
                (wdel[:], W_delta),
                (bdel[:], b_delta.rearrange("(c p) -> p c", p=P)),
                (dskip[:], D.rearrange("(c p) -> p c", p=P)),
            ]
            ffn_loads = [
                (wout[:], W_out.rearrange("(c p) n -> p c n", p=P)),
                (gw[:], gate_w), (s1[:], sw1), (s3[:], sw3),
                (s2[:], sw2.rearrange("(h p) n -> p h n", p=SHH)),
            ]
            with nc.allow_non_contiguous_dma(reason="columns of 256 numbers"):
                for dst, src in mix_loads:
                    sp.dma_start(dst, src).then_inc(w_mix, 16)
                for dst, src in ffn_loads:
                    sp.dma_start(dst, src).then_inc(w_ffn, 16)
            sp.wait_ge(pd_sum, NBLK)
            for r in range(2):
                half = NBLK // 2
                sp.dma_start(res1[:, r * half * TPB:(r + 1) * half * TPB, :].rearrange("p (n i) d -> p n i d", i=TPB),
                             x_rows[r * half:(r + 1) * half].rearrange("n p i d -> p n i d")).then_inc(xres_in[r], 16)
            sp.wait_ge(chunk_done, NCH + 1)
            sp.dma_start(w1x, w1.rearrange("e p n -> p e n")).then_inc(w_exp1, 16)
            with sp.Fori(0, NBLK // 2) as i:
                for r in range(2):
                    sp.wait_ge(x1_ready, i * 2 + r + 1)
                    sp.dma_start(row_block(x1_blocks, i * 2 + r), x1b[:, r]).then_inc(x1_stored[r], 16)
            sp.dma_start(w3x, w3.rearrange("e p n -> p e n")).then_inc(w_exp3, 16)
            sp.wait_ge(wl_ready, 1)
            for c in range(EC):
                w = min(P, EH - c * P)
                sp.dma_start(w2s[0:w, :, c, :], w2[:, c * P:c * P + w, :].rearrange("e p n -> p e n")
                             ).then_inc(w_exp, 16)
            for r in range(4):
                sp.wait_ge(scattered[r], 16 * (N_TILES // 4))
            def load_y(n, r):
                for k, ring in enumerate((y0r, y1r)):
                    sp.dma_start(ring[:, r], row_block(y_blocks[k], n)).then_inc(y_in[r], 16)

            def store_out(n, r):
                sp.wait_ge(o_ready, n + 3)
                sp.dma_start(row_block(o_rows, n), outr[:, r]).then_inc(o_stored[r], 16)

            for r in range(FIN):
                load_y(r, r)
            with sp.Fori(0, NBLK // FIN - 1) as i:
                for r in range(FIN):
                    n = i * FIN + r
                    sp.wait_ge(fin_read, n + 1)
                    load_y(n + FIN, r)
                    store_out(n, r)
            for r in range(FIN):
                store_out(NBLK - FIN + r, r)
            for r in range(FIN):
                sp.wait_ge(o_stored[r], 16 * (NBLK // FIN + 1))

        @block.gpsimd
        def _(pool):
            g = nc.gpsimd
            own = Steps(pool, pool_step)
            g.memset(xT[:, 0:HALO], 0.0).then_inc(halo, 1)
            g.memset(xT[:, XTW:XTW + HALO], 0.0).then_inc(halo, 1)
            own.settle(g.memset(ones[:], 1.0))
            own.settle(g.memset(ident[:], 0.0))
            g.affine_select(out=ident[:], in_=ident[:], compare_op=ALU.not_equal, fill=1.0, base=0,
                            pattern=[[-1, P]], channel_multiplier=1).then_inc(consts, 1)
            g.affine_select(out=before[:], in_=ones[:], compare_op=ALU.is_gt, fill=0.0, base=0,
                            pattern=[[1, P]], channel_multiplier=-1).then_inc(consts, 1)
            g.iota(iota[:], pattern=[[1, P]], base=0, channel_multiplier=0,
                   allow_small_or_imprecise_dtypes=True).then_inc(consts, 1)
            g.iota(pcol[:], pattern=[[0, 1]], base=0, channel_multiplier=1,
                   allow_small_or_imprecise_dtypes=True).then_inc(consts, 1)
            g.iota(desc[:], pattern=[[-1, E]], base=E, channel_multiplier=0,
                   allow_small_or_imprecise_dtypes=True).then_inc(consts, 1)
            g.iota(tcol[:], pattern=[[1, TILES], [TILES, K]], base=1, channel_multiplier=0,
                   allow_small_or_imprecise_dtypes=True).then_inc(consts, 1)
            g.memset(zer[:], 0.0).then_inc(consts, 1)
            g.memset(idx_src[:], 0).then_inc(consts, 1)
            g.memset(idx_dst[:], NO_ROW).then_inc(consts, 1)
            g.memset(epst[:, 0:1], LN_EPS).then_inc(consts, 1)
            g.memset(epst[:, 1:2], NEG_LN_SCAN_EPS).then_inc(consts, 1)
            g.memset(epst[:, 2:3], 1.0).then_inc(consts, 1)
            g.memset(epst[:, 3:4], 0.0).then_inc(consts, 1)
            for m, value in enumerate((-0.5, LN_EPS, -1.0)):
                g.memset(lnc[:, m], value).then_inc(consts, 1)
            g.iota(tex[:], pattern=[[1, IDXC], [0, E]], base=0, channel_multiplier=0,
                   allow_small_or_imprecise_dtypes=True).then_inc(consts, 1)

            zeros = epst[0:2 * NST, 3:4].to_broadcast([2 * NST, BLK])
            pool.wait_ge(consts, 17)
            with SteppedLoop(pool, own, NBLK // 2, 2 * 4) as i:
                for r in range(2):
                    cols = ds(i * 2 * BLK + r * BLK, BLK)
                    high, middle, low = (bc3[m * 2 * NST:(m + 1) * 2 * NST, cols] for m in range(3))
                    pool.wait_ge(xd_ready, i * 4 + 2 * r + 4)
                    hold(pool, pool_held)
                    own.settle(g.tensor_tensor(high, bc[:, r], zeros, ALU.add))
                    hold(pool, pool_held)
                    own.settle(g.tensor_tensor(bcrest[:, r], bc[:, r], high, ALU.subtract))
                    own.settle(g.tensor_tensor(bcmid[:, r], bcrest[:, r], zeros, ALU.add))
                    hold(pool, pool_held)
                    own.settle(g.tensor_tensor(middle, bcmid[:, r], zeros, ALU.add))
                    hold(pool, pool_held)
                    g.tensor_tensor(low, bcrest[:, r], bcmid[:, r], ALU.subtract).then_inc(bc_split, 1)
                    pool.wait_ge(bc_split, i * 2 + r + 1)

            def chunk(q, b, m):
                pool.wait_ge(scan_done, m + 1)
                for c in range(DC):
                    ins = g.tensor_tensor(decay[:, c],
                                          dl_all[:, c, ds(q * CH + b * SEQ, CH)].unsqueeze(1).to_broadcast([P, NST, CH]),
                                          aneg[:, c, :].unsqueeze(2).to_broadcast([P, NST, CH]), ALU.mult)
                ins.then_inc(za_raw, 1)
                pool.wait_ge(gain_ready, m + 1)
                pool.wait_ge(csb_ready, m + 1)
                hold(pool, pool_held)
                for c in range(DC):
                    g.tensor_tensor(gain[:, c], gain[:, c], csb, ALU.mult).then_inc(gc_ready, 1)
                pool.wait_ge(za_raw, m + 1)
                pool.wait_ge(gc_ready, m * 2 + 2)
                hold(pool, pool_held)

            def skip(n, m):
                pool.sem_inc(za_raw, n)
                pool.sem_inc(gc_ready, 2 * n)

            pool.wait_ge(flags_ready, 1)
            chunk_loops(pool, g, mybir.EngineType.Pool, chunk, skip)

            def deviations(n, r, ready, done, with_shift):
                pool.wait_ge(ready, n + 1)
                hold(pool, pool_held)
                own.settle(g.tensor_tensor(vare[:, r], bag[:, r, :, 1], lnc[:, 1], ALU.add))
                if with_shift:
                    own.settle(g.tensor_tensor(rstd[:, r], vare[:, r], lnc[:, 0], ALU.pow))
                    own.settle(g.tensor_tensor(shift[:, r], bag[:, r, :, 0], rstd[:, r], ALU.mult))
                    g.tensor_tensor(shift[:, r], shift[:, r], lnc[:, 2], ALU.mult).then_inc(done, 1)
                else:
                    g.tensor_tensor(rstd[:, r], vare[:, r], lnc[:, 0], ALU.pow).then_inc(done, 1)

            zero_rows = epst[:, 3:4].unsqueeze(2).to_broadcast([P, TPB, DM])
            pool.sem_inc(x1_kept, 1)
            with SteppedLoop(pool, own, NBLK // 2, 2) as i:
                for r in range(2):
                    n = i * 2 + r
                    deviations(n, r, var_ready, rstd_ready, False)
                    pool.wait_ge(x1_ready, n + 1)
                    hold(pool, pool_held)
                    g.tensor_tensor(acc[:, ds(n * TPB, TPB), :], x1b[:, r], zero_rows, ALU.add).then_inc(x1_kept, 1)

            def gather(slot_, half_ring, j):
                hold(pool, pool_held)
                g.indirect_dma_start(xg[:, slot_], None, x1_rows,
                                     bass.IndirectOffsetOnAxis(ap=ring_src[:, half_ring, j:j + 1].bitcast(U32), axis=0)
                                     ).then_inc(gathered[slot_], 16)

            zero_weights = epst[:, 3:4].unsqueeze(2).to_broadcast([P, E, EH])
            for m, (weights, loaded) in enumerate(((w1x, w_exp1), (w3x, w_exp3))):
                pool.wait_ge(loaded, 16)
                pool.wait_ge(yb_ready, NBLK)
                g.tensor_tensor(w13h[:, :, m], weights, zero_weights, ALU.add).then_inc(wh_ready, 1)
                pool.wait_ge(wh_ready, m + 1)
                g.tensor_tensor(w13l[:, :, m], weights, w13h[:, :, m].bitcast(F32), ALU.subtract).then_inc(wl_ready, 1)

            t_cols = tcol[:].rearrange("p t k -> p (t k)")
            with pool.Fori(0, TILES * K // GROUP // 2) as i:
                for r in range(2):
                    pool.wait_ge(ohe_ready, i * 2 + r + 1)
                    hold(pool, pool_held)
                    g.tensor_tensor(ohh[:, r, :, 1], ohe[:, r],
                                    t_cols[:, ds(i * 2 * GROUP + r * GROUP, GROUP)].unsqueeze(2).to_broadcast(
                                        [P, GROUP, N_TILES]), ALU.mult).then_inc(oht_ready, 1)

            for r in range(2):
                pool.wait_ge(x1_stored[r], 16 * (NBLK // 2 + 1))
            pool.wait_ge(src_ready, 1)
            for t in range(AHEAD + 1):
                gather(t, t // HALF, t % HALF)
            with pool.Fori(0, N_TILES // 8) as i:
                for k in range(1, 9):
                    ahead = k + AHEAD
                    if ahead % HALF == 0:
                        pool.wait_ge(src_ready, i * 2 + ahead // HALF)
                    pool.wait_ge(e_turned, i * 8 + k)
                    gather(ahead % XG, (ahead // HALF) % 2, ahead % HALF)
                    behind = k - 1
                    if behind % HALF == 0:
                        pool.wait_ge(dst_ready, i * 2 + behind // HALF + 1)
                    pool.wait_ge(e_out, i * 8 + k + 2)
                    hold(pool, pool_held)
                    g.indirect_dma_start(y_rows,
                                         bass.IndirectOffsetOnAxis(ap=ring_dst[:, (behind // HALF) % 2, behind % HALF:behind % HALF + 1].bitcast(U32), axis=0),
                                         yo[:, behind % 4], None, bounds_check=K * TOK - 1, oob_is_err=False
                                         ).then_inc(scattered[behind % 4], 16)
            for ahead in range(2, AHEAD + 1):
                pool.wait_ge(gathered[ahead], 16 * (N_TILES // XG + 1))
            def add_y0(n, r):
                pool.wait_ge(y0_scaled, n + 1)
                hold(pool, pool_held)
                tiles = ds(n * TPB, TPB)
                g.tensor_tensor(acc[:, tiles, :], acc[:, tiles, :], y0r[:, r], ALU.add).then_inc(y0_added, 1)

            add_y0(0, 0)
            with SteppedLoop(pool, own, NBLK // FIN - 1, FIN * 3) as i:
                for r in range(FIN):
                    n = i * FIN + r
                    add_y0(n + 1, (r + 1) % FIN)
                    deviations(n, r % 2, fvar_ready, frstd_ready, True)
            for n in range(NBLK - FIN, NBLK):
                if n + 1 < NBLK:
                    add_y0(n + 1, (n + 1) % FIN)
                deviations(n, n % 2, fvar_ready, frstd_ready, True)

        @block.scalar
        def _(act):
            s = nc.scalar
            act.sem_inc(ug_ready, 3)
            act.sem_inc(e_out, 2)
            act.sem_inc(o_ready, 2)
            act.wait_ge(alog_ready, 1)
            s.activation(aneg[:], alog[:], ACT.Exp).then_inc(a_exp, 1)
            for n in range(1, NBLK, 2):
                act.wait_ge(x_turned, n + 1)
                s.copy(xT_block(n), ps[:, 4 + n % 4]).then_inc(xT_odd, 1)
            act.wait_ge(consts, 17)
            with act.Fori(0, NBLK // 2) as i:
                for r in range(2):
                    cols = ds(i * 2 * BLK + r * BLK, BLK)
                    for j in range(2 * DC):
                        act.wait_ge(ug_sum, i * 8 + 4 * r + j + 1)
                        out_ = (u_all, y_all)[j // DC]
                        s.activation(out_[:, j % DC, cols], ps[:, (4 * r + j) % 3], ACT.Silu).then_inc(ug_ready, 1)
                for r in range(2):
                    act.wait_ge(pd_sum, i * 2 + r + 1)
                    act.wait_ge(dl_ready, i * 2 + r + 1)
                    for c in range(DC):
                        s.activation(z_buf[:, r, c], ps[:, 4 + 2 * r + c], ACT.Exp,
                                     bias=bdel[:, c:c + 1]).then_inc(z_ready, 1)
                for r in range(2):
                    act.wait_ge(z_clamped, i * 2 + r + 1)
                    s.activation(ln_buf[:, r], z_buf[:, r], ACT.Ln, bias=epst[:, 2:3]).then_inc(ln_ready, 1)

            def chunk(q, b, m):
                act.wait_ge(c_sum, m + 1)
                s.copy(csb, ps[:, 6:6 + CBK].rearrange("p a (n t) -> p (a n) t", t=CH)).then_inc(csb_ready, 1)
                act.wait_ge(za_ready, m + 1)
                s.activation(decay[:], decay[:], ACT.Exp, scale=A_UNIT).then_inc(decay_ready, 1)
                act.wait_ge(zr_ready, m + 1)
                act.wait_ge(res_again, m + 1)
                s.activation(gch[:], ps[:, 2, 0:DC * CH].rearrange("p (c t) -> p c t", c=DC), ACT.Sigmoid)
                s.activation(gain[:], gain[:], ACT.Sigmoid, bias=epst[:, 1:2],
                             scale=A_UNIT).then_inc(gain_ready, 1)
                act.wait_ge(csb_ready, m + 1)
                act.wait_ge(gain_ready, m + 1)
                hold(act, act_held)

            def skip(n, m):
                act.sem_inc(csb_ready, n)
                act.sem_inc(decay_ready, n)
                act.sem_inc(gain_ready, n)

            act.wait_ge(flags_ready, 1)
            chunk_loops(act, s, mybir.EngineType.Activation, chunk, skip)
            def keep_y(n, r):
                s.copy(ybuf[:, r], y_all[:, :, ds(n * BLK, BLK)]).then_inc(yb_ready, 1)

            def keep_x1T(n, r):
                act.wait_ge(x1_turned, n + 2)
                act.wait_ge(yb_ready, n + 1)
                s.copy(x1T[:, r], ps[:, 2]).then_inc(x1T_ready, 1)
                s.copy(x1T_all[:, ds(n * BLK, BLK)], ps[:, 2]).then_inc(x1T_kept, 1)

            def two_blocks(i, more_y, last_two=False):
                for r in range(2):
                    n = i * 2 + r
                    if more_y:
                        act.wait_ge(mix_sum, n + 3)
                        keep_y(n + 4, r)
                    if not last_two or r == 0:
                        keep_x1T(n + 1, (r + 1) % 2)

            def shared(n):
                for h in range(2):
                    act.wait_ge(sh_a, n * 2 + h + 1)
                    act.wait_ge(sh_h, n * 2 + h + 1)
                    s.activation(sgate[:, h], ps[0:SHH, 4 + h], ACT.Silu).then_inc(sh_silu, 1)

            act.wait_ge(chunk_done, NCH + 1)
            for n in range(4):
                if n >= 2:
                    act.wait_ge(mix_sum, n - 1)
                keep_y(n, n % 2)
            keep_x1T(0, 0)
            with act.Fori(0, NBLK // 2 - 2) as i:
                two_blocks(i, True)
            two_blocks(NBLK // 2 - 2, False)
            two_blocks(NBLK // 2 - 1, False, True)
            act.wait_ge(lgx_ready, 1)
            s.activation(sc[:], t3[:], ACT.Exp).then_inc(sce_ready, 1)
            with act.Fori(0, NBLK) as n:
                shared(n)
            act.wait_ge(e_a, 1)
            s.activation(egate, ps[:, 0, 0:EH], ACT.Silu).then_inc(e_silu, 1)

            def eight_tiles(i, first):
                for k in range(1, 9):
                    act.wait_ge(e_a, i * 8 + k + 1)
                    s.activation(egate, ps[:, 0, 0:EH], ACT.Silu).then_inc(e_silu, 1)
                    behind = k - 1
                    act.wait_ge(e_sum, i * 8 + k)
                    if behind >= 4 or not first:
                        act.wait_ge(scattered[behind % 4], 16 * (i * 2 + behind // 4))
                    s.copy(yo[:, behind % 4], ps[:, 4 + behind % 2, 0:DM]).then_inc(e_out, 1)

            eight_tiles(0, True)
            with act.Fori(1, N_TILES // 8) as i:
                eight_tiles(i, False)
            def scale_y0(i, r):
                act.wait_ge(y_in[r], 32 * (i + 1))
                for j in range(TPB):
                    last = s.activation(y0r[:, r, j], y0r[:, r, j], ACT.Copy,
                                        scale=wk2[:, 0, ds(i * FIN * TPB + (r * TPB + j), 1)])
                last.then_inc(y0_scaled, 1)

            def normalise(i, r):
                act.wait_ge(frstd_ready, i * FIN + r + 1)
                act.wait_ge(o_stored[r], 16 * (i + 1))
                for j in range(TPB):
                    last = s.activation(outr[:, r, j],
                                        acc[:, ds(i * FIN * TPB + (r * TPB + j), 1), :].rearrange("p a d -> p (a d)"),
                                        ACT.Identity, bias=shift[:, r % 2, j:j + 1], scale=rstd[:, r % 2, j:j + 1])
                last.then_inc(o_ready, 1)

            def four_blocks(i, last):
                for r in range(FIN):
                    if not last or r + 2 < FIN:
                        scale_y0(i + (r + 2) // FIN, (r + 2) % FIN)
                    normalise(i, r)

            scale_y0(0, 0)
            scale_y0(0, 1)
            with act.Fori(0, NBLK // FIN - 1) as i:
                four_blocks(i, False)
            four_blocks(NBLK // FIN - 1, True)

        @block.tensor
        def _(pe):
            t = nc.tensor
            pe.sem_inc(oh_sum, 2)
            pe.sem_inc(x1_turned, 1)
            pe.wait_ge(consts, 1)
            for n in range(NBLK):
                pe.wait_ge(x_in[n // 2], 16)
                if n >= 4:
                    pe.wait_ge((xT_even, xT_odd)[n % 2], (n - 4) // 2 + 1)
                for j in range(TPB):
                    last = t.transpose(ps[:, 4 + n % 4, j * P:(j + 1) * P], xin[:, n, j], ident[:])
                last.then_inc(x_turned, 1)
            pe.wait_ge(wk_ready, TAPS)
            pe.wait_ge(halo, 2)
            pe.wait_ge(w_mix, 16 * 4)
            pe.wait_ge(xT_even, NBLK // 2)
            pe.wait_ge(xT_odd, NBLK // 2)
            with pe.Fori(0, BATCH) as b:
                with pe.Fori(0, BPS // 2) as h:
                    pair = b * (BPS // 2) + h
                    for r in range(2):
                        base = b * XTW + h * (2 * BLK) + r * BLK
                        for j in range(2 * DC):
                            unit = 4 * r + j
                            pe.wait_ge(ug_ready, pair * 8 + (unit + 1 if unit >= 3 else (2, 3, 1)[unit]))
                            taps = range(TAPS) if j < DC else (HALO,)
                            for k in taps:
                                w = wk[:, k, j * P:(j + 1) * P] if j < DC else win[:, j * P:(j + 1) * P]
                                last = t.matmul(ps[:, unit % 3], w, xT[:, ds(base + k, BLK)],
                                                start=(k == taps[0]), stop=(k == taps[-1]))
                            last.then_inc(ug_sum, 1)
                        n = pair * 2 + r
                        pe.wait_ge(ug_ready, pair * 8 + 4 * r + 5)
                        pe.wait_ge(xd_ready, n * 2 + 2)
                        for c in range(DC):
                            last = t.matmul(ps[0:RANK + 2 * NST, 3], wx[:, c], u_all[:, c, ds(n * BLK, BLK)],
                                            start=(c == 0), stop=(c == DC - 1))
                        last.then_inc(xd_sum, 1)
                    for r in range(2):
                        n = pair * 2 + r
                        pe.wait_ge(xd_ready, n * 2 + 3)
                        pe.wait_ge(dl_ready, n + 1)
                        for c in range(DC):
                            last = t.matmul(ps[:, 4 + 2 * r + c], wdel[:, c * P:(c + 1) * P],
                                            xdl[:, ds(n * BLK, BLK)], start=True, stop=True)
                        last.then_inc(pd_sum, 1)
            pe.wait_ge(live_ready, 1)
            t.matmul(ps[0:1, 4, 0:DC * NCH], ones[:, 0:1], live[:].rearrange("p c q -> p (c q)"),
                     start=True, stop=True).then_inc(live_sum, 1)

            def chunk(q, b, m):
                for half, done in enumerate((b_sum, c_sum)):
                    pe.wait_ge(chunk_done if half else scan_done, m + 1)
                    for n in range(NST):
                        row = half * NST + n
                        last = t.matmul(ps[:, 4 + 2 * half + n // NPB, (n % NPB) * CH:(n % NPB + 1) * CH],
                                        sel3[:, row:row + 1].to_broadcast([PARTS, P]),
                                        bc3[:, ds(q * CH + b * SEQ, CH)], start=True, stop=True)
                    last.then_inc(done, 1)
                for c in range(DC):
                    last = t.matmul(ps[:, 2, c * CH:(c + 1) * CH], win[:, DIN + c * P:DIN + (c + 1) * P],
                                    xT[:, ds(q * CH + (b * XTW + HALO), CH)], start=True, stop=True)
                last.then_inc(res_again, 1)
                pe.wait_ge(res_again, m + 1)

            def skip(n, m):
                pe.sem_inc(b_sum, n)
                pe.sem_inc(c_sum, n)
                pe.sem_inc(res_again, n)

            pe.wait_ge(sel_ready, 3)
            pe.wait_ge(bc_split, NBLK)
            pe.wait_ge(flags_ready, 1)
            chunk_loops(pe, t, mybir.EngineType.PE, chunk, skip)

            def mix(n, r):
                pe.wait_ge(yb_ready, n + 1)
                for j in range(TPB):
                    for c in range(DC):
                        last = t.matmul(ps[:, r, j * P:(j + 1) * P], ybuf[:, r, c, j * P:(j + 1) * P],
                                        wout[:, c], start=(c == 0), stop=(c == DC - 1))
                last.then_inc(mix_sum, 1)

            def turn_x1(n, r):
                pe.wait_ge(x1_ready, n + 1)
                for j in range(TPB):
                    last = t.transpose(ps[:, 2, j * P:(j + 1) * P], x1b[:, r, j], ident[:])
                last.then_inc(x1_turned, 1)

            def two_blocks(i, mixes, last_two=False):
                for r in range(2):
                    n = i * 2 + r
                    if r < mixes:
                        pe.wait_ge(res_ready, n + 2)
                        mix(n + 3, 1 - r)
                    pe.wait_ge(x1T_ready, n + 1)
                    pe.wait_ge(x1T_kept, n + 1)
                    pe.wait_ge(lg_ready, n + 1)
                    for j in range(TPB):
                        last = t.matmul(ps[:, 3, j * E:(j + 1) * E], x1T[:, r, j * P:(j + 1) * P], gwT[:],
                                        start=True, stop=True)
                    last.then_inc(gate_sum, 1)
                    if not last_two or r == 0:
                        turn_x1(n + 1, (r + 1) % 2)

            pe.wait_ge(w_ffn, 16 * 5)
            t.transpose(ps[:, 3, 0:E], gw[:], ident[0:E, 0:E]).then_inc(gwT_sum, 1)
            for r in range(2):
                mix(r, r)
            pe.wait_ge(gwT_ready, 1)
            turn_x1(0, 0)
            pe.wait_ge(res_ready, 1)
            mix(2, 0)
            def shared_out(n, r):
                pe.wait_ge(sh_h, n * 2 + 4)
                for j in range(TPB):
                    for h in range(2):
                        last = t.matmul(ps[:, r, j * P:(j + 1) * P], shT[:, r, h, j * P:(j + 1) * P],
                                        s2[:, h], start=(h == 0), stop=(h == 1))
                last.then_inc(sh_sum, 1)

            def shared_hidden(n):
                for h in range(2):
                    pe.wait_ge(sh_h, n * 2 + h + 1)
                    for w, bank, done in ((s1, 4 + h, sh_a), (s3, 6 + h, sh_c)):
                        t.matmul(ps[0:SHH, bank], w[:, h * SHH:(h + 1) * SHH], x1T_all[:, ds(n * BLK, BLK)],
                                 start=True, stop=True).then_inc(done, 1)

            def shared(n, r, first=False):
                if not first:
                    pe.wait_ge(acc_ready, n - 1)
                shared_out(n - 1, 1 - r)
                shared_hidden(n)

            with pe.Fori(0, NBLK // 2 - 2) as i:
                two_blocks(i, 2)
            two_blocks(NBLK // 2 - 2, 1)
            two_blocks(NBLK // 2 - 1, 0, True)
            shared_hidden(0)
            pe.wait_ge(res_ready, NBLK)
            shared(1, 1, True)
            pe.wait_ge(m_ready, 1)
            t.matmul(ps[:, 2, 0:TILES * E], before[:], rk[:].rearrange("p t e -> p (t e)"), start=True, stop=True)
            t.matmul(ps[:, 2, TILES * E:2 * TILES * E], ones[:], rk[:].rearrange("p t e -> p (t e)"),
                     start=True, stop=True).then_inc(rank_sum, 1)
            for n in (2, 3):
                shared(n, n % 2)
            t.matmul(ps[:, 3, 0:2 * N_TILES], zer[:, 0:P], zer[:], start=True, stop=False,
                     skip_group_check=True)
            with pe.Fori(0, 2) as i:
                for u in range(2):
                    shared(i * 2 + (4 + u), u)
                    for r in range(2):
                        pe.wait_ge(oh_ready, i * 4 + 2 * u + r + 1)
                        pe.wait_ge(oht_ready, i * 4 + 2 * u + r + 1)
                        for j in range(GROUP):
                            last = t.matmul(ps[:, 3, 0:2 * N_TILES], ohl[:, r, j],
                                            ohh[:, r, j].rearrange("p a n -> p (a n)"),
                                            start=False, stop=False, skip_group_check=True)
                        last.then_inc(oh_sum, 1)
            t.matmul(ps[:, 3, 0:2 * N_TILES], zer[:, 0:P], zer[:], start=False, stop=True,
                     skip_group_check=True).then_inc(oh_sum, 1)
            shared_out(NBLK - 1, 1)

            def turn_rows(slot_, landed, freed):
                pe.wait_ge(gathered[slot_], landed)
                if freed is not None:
                    pe.wait_ge(eT_ready, freed)
                t.transpose(ps[:, 2, 0:P], xg[:, slot_], ident[:]).then_inc(e_turned, 1)

            def hidden(par, expert, turned):
                pe.wait_ge(eT_ready, turned)
                for m, done in enumerate((e_a, e_c)):
                    high, rest = (w[:, ds(expert, 1), m].rearrange("p a n -> p (a n)") for w in (w13h, w13l))
                    t.matmul(ps[:, m, 0:EH], xgT[:, 0, par], rest, start=True, stop=False)
                    t.matmul(ps[:, m, 0:EH], xgT[:, 1, par], high, start=False, stop=False)
                    t.matmul(ps[:, m, 0:EH], xgT[:, 0, par], high, start=False, stop=True).then_inc(done, 1)

            pe.wait_ge(texi_ready, 1)
            pe.wait_ge(w_exp, 16 * EC)
            pe.wait_ge(wl_ready, 2)
            pe.wait_ge(acc_ready, NBLK + 1)
            first_expert, = load_registers(nc, mybir.EngineType.PE, texi[0:1, 0:1], E - 1)
            turn_rows(0, 16, None)
            turn_rows(1, 16, 1)
            hidden(0, first_expert, 1)
            with pe.Fori(0, N_TILES // 8) as i:
                experts = load_registers(nc, mybir.EngineType.PE, texi[0:1, ds(i * 8, 9)], E - 1)
                for k in range(1, 9):
                    was, now = experts[k - 1], experts[k]
                    turn_rows((k + 1) % XG, 16 * (i + (k + 1) // XG + 1), i * 8 + k + 1)
                    pe.wait_ge(e_h, i * 8 + k)
                    for c in range(EC):
                        w = min(P, EH - c * P)
                        last = t.transpose(ps[0:w, 3, c * P:(c + 1) * P], eh[:, c * P:c * P + w], ident[:])
                    last.then_inc(eh_turned, 1)
                    hidden(k % 2, now, i * 8 + k + 1)
                    pe.wait_ge(ehT_ready, i * 16 + 2 * k)
                    pe.wait_ge(e_out, i * 8 + k)
                    for c in range(EC):
                        w = min(P, EH - c * P)
                        last = t.matmul(ps[:, 4 + (k - 1) % 2, 0:DM], ehT[0:w, c],
                                        w2s[0:w, ds(was, 1), c, :].rearrange("p a n -> p (a n)"),
                                        start=(c == 0), stop=(c == EC - 1))
                    last.then_inc(e_sum, 1)

        @block.vector
        def _(dve):
            v = nc.vector
            own = Steps(dve, dve_step)

            def loop(count, per):
                return SteppedLoop(dve, own, count, per)

            dve.sem_inc(xd_ready, 2)
            dve.sem_inc(dl_ready, 2)
            dve.sem_inc(chunk_done, 1)
            dve.sem_inc(scan_done, 1)
            dve.sem_inc(sh_h, 2)
            dve.sem_inc(lg_ready, 1)
            dve.sem_inc(acc_ready, 1)
            dve.wait_ge(w_alog, 16)
            v.tensor_scalar(alog[:], alog[:], MAX_EXP, None, ALU.min).then_inc(alog_ready, 1)
            dve.wait_ge(w_first, 32)
            for k in range(TAPS):
                v.tensor_tensor(wk[:, k], win[:, 0:DIN], cwb[:, :, k], ALU.mult).then_inc(wk_ready, 1)
            for n in range(0, NBLK, 2):
                dve.wait_ge(x_turned, n + 1)
                v.tensor_copy(xT_block(n), ps[:, 4 + n % 4]).then_inc(xT_even, 1)
            for j in range(3):
                rows = slice(j * 2 * NST, (j + 1) * 2 * NST)
                v.tensor_copy(sel3[rows], ident[rows, rows]).then_inc(sel_ready, 1)
            dve.wait_ge(a_exp, 1)
            own.settle(v.tensor_scalar(aneg[:], aneg[:], -1.0 / A_UNIT, None, ALU.mult))
            own.settle(v.tensor_reduce(amax[:], aneg[:], AX.X, ALU.max))
            dve.wait_ge(w_mix, 16 * 4)
            dve.wait_ge(x_turned, NBLK)

            def low_rank(n, r, n_first=None):
                cols = ds(n * BLK, BLK)
                dve.wait_ge(xd_sum, n + 1)
                v.tensor_copy(xdl[:, cols], ps[0:RANK, 3]).then_inc(xd_ready, 1)
                if n_first is None:
                    dve.wait_ge(bc_split, n - 1)
                v.tensor_copy(bc[:, r], ps[RANK:RANK + 2 * NST, 3]).then_inc(xd_ready, 1)
                dve.wait_ge(ug_ready, n * 4 + 7)
                for c in range(DC):
                    v.scalar_tensor_tensor(out=y_all[:, c, cols], in0=u_all[:, c, cols],
                                           scalar=dskip[:, c:c + 1], in1=y_all[:, c, cols],
                                           op0=ALU.mult, op1=ALU.mult).then_inc(y_ready, 1)

            csum_n = csum[:].rearrange("p c b q -> p c (b q)")

            def soft_start(i, r):
                dve.wait_ge(z_ready, i * 4 + 2 * r + 2)
                zr = z_buf[:, r].rearrange("p c t -> p (c t)")
                v.tensor_scalar(zr, zr, float(2 ** 40), None, ALU.min).then_inc(z_clamped, 1)
                dve.wait_ge(z_clamped, i * 2 + r + 1)
                own.settle(v.scalar_tensor_tensor(out=sq_buf[:, r].rearrange("p c t -> p (c t)"), in0=zr,
                                                  scalar=2.0, in1=zr, op0=ALU.subtract, op1=ALU.mult))

            def soft_end(i, r):
                cols = ds(i * 2 * BLK + r * BLK, BLK)
                zr = z_buf[:, r].rearrange("p c t -> p (c t)")
                lr = ln_buf[:, r].rearrange("p c t -> p (c t)")
                sr = sq_buf[:, r].rearrange("p c t -> p (c t)")
                dve.wait_ge(ln_ready, i * 2 + r + 1)
                own.settle(v.scalar_tensor_tensor(out=lr, in0=zr, scalar=SOFT_CUT, in1=lr,
                                                  op0=ALU.is_ge, op1=ALU.mult))
                own.settle(v.scalar_tensor_tensor(out=sr, in0=sr, scalar=-0.5, in1=lr,
                                                  op0=ALU.mult, op1=ALU.max))
                own.settle(v.scalar_tensor_tensor(out=dl_all[:, 0, cols], in0=ps[:, 4 + 2 * r],
                                                  scalar=bdel[:, 0:1], in1=sq_buf[:, r, 0],
                                                  op0=ALU.add, op1=ALU.max))
                v.scalar_tensor_tensor(out=dl_all[:, 1, cols], in0=ps[:, 5 + 2 * r],
                                       scalar=bdel[:, 1:2], in1=sq_buf[:, r, 1],
                                       op0=ALU.add, op1=ALU.max).then_inc(dl_ready, 1)
                dve.wait_ge(dl_ready, i * 2 + r + 3)
                own.settle(v.tensor_reduce(csum_n[:, :, ds(i * 2 * CPB + r * CPB, CPB)],
                                           dl_all[:, :, cols].rearrange("p c (q t) -> p c q t", t=CH),
                                           AX.X, ALU.add))

            for r in range(2):
                low_rank(r, r, n_first=True)
            with loop(NBLK // 2 - 1, 2 * 5) as i:
                for r in range(2):
                    soft_start(i, r)
                for r in range(2):
                    soft_end(i, r)
                    low_rank(i * 2 + (2 + r), r)
            for r in range(2):
                soft_start(NBLK // 2 - 1, r)
            for r in range(2):
                soft_end(NBLK // 2 - 1, r)
            own.settle(v.memset(rend[:, :, :, CPS - 1:CPS], 0.0))
            dve.wait_ge(consts, 17)
            for c in range(DC):
                for b in range(BATCH):
                    own.settle(v.tensor_tensor_scan(rend[:, c, b, CPS - 2::-1], ones[:, 0:CPS - 1],
                                                    csum[:, c, b, CPS - 1:0:-1], 0.0, ALU.mult, ALU.add))
            own.settle(v.tensor_tensor(live[:], rend[:].rearrange("p c b q -> p c (b q)"),
                                       amax[:].unsqueeze(2).to_broadcast([P, DC, NCH]), ALU.mult))
            v.tensor_scalar(live[:], live[:], DEAD / A_UNIT, None, ALU.is_ge).then_inc(live_ready, 1)
            dve.wait_ge(live_sum, 1)
            pf = ps[0:1, 4, 0:DC * NCH].rearrange("p (m q) -> p q m", q=CPS)
            own.settle(v.tensor_reduce(flagf[:], pf, AX.X, ALU.max))
            own.settle(v.tensor_scalar(flagf[:], flagf[:], 0.0, None, ALU.is_le))
            own.settle(v.tensor_reduce(flagr[:], flagf[:], AX.X, ALU.add))
            v.tensor_scalar(flags[:], flagr[:], float(CPS), None, ALU.min).then_inc(flags_ready, 1)
            dve.wait_ge(flags_ready, 1)

            STEPS_PER_CHUNK = 2 * DC + 4 + DC * 5 + 1 + DC * 4

            def chunk(q, b, m):
                tokens = ds(q * CH + b * SEQ, CH)
                own.settle(v.tensor_copy(dch[:], dl_all[:, :, tokens]))
                for c in range(DC):
                    own.settle(v.tensor_copy(rch[:, c, CH - 1:CH], rend[:, c, b, ds(q, 1)]))
                for c in range(DC):
                    own.settle(v.tensor_tensor_scan(rch[:, c, CH - 2::-1], ones[:, 0:CH - 1],
                                                    dch[:, c, CH - 1:0:-1],
                                                    rch[:, c, CH - 1:CH], ALU.mult, ALU.add))
                for c in range(DC):
                    last = v.tensor_tensor(gain[:, c], rch[:, c, :].unsqueeze(1).to_broadcast([P, NST, CH]),
                                           aneg[:, c, :].unsqueeze(2).to_broadcast([P, NST, CH]), ALU.mult)
                own.settle(last)
                dve.wait_ge(za_raw, m + 1)
                v.tensor_scalar(decay[:], decay[:], 0.0, FLOOR / A_UNIT, ALU.min, ALU.max).then_inc(za_ready, 1)
                v.tensor_scalar(gain[:], gain[:], 0.0, FLOOR / A_UNIT, ALU.min, ALU.max).then_inc(zr_ready, 1)
                own.settle(v.tensor_tensor(du[:], dch[:], u_all[:, :, tokens], ALU.mult))
                bvals = ps[:, 4:4 + CBK].rearrange("p a (n t) -> p (a n) t", t=CH)
                dve.wait_ge(b_sum, m + 1)
                for c in range(DC):
                    last = v.tensor_tensor(hs[:, c], bvals, du[:, c, :].unsqueeze(1).to_broadcast([P, NST, CH]),
                                           ALU.mult)
                own.settle(last)
                dve.wait_ge(decay_ready, m + 1)
                for c in range(DC):
                    own.settle(v.tensor_tensor(hmul[:], decay[:, c, :, 0], hcar[:, b, c], ALU.mult))
                    own.settle(v.tensor_tensor(hs[:, c, :, 0], hs[:, c, :, 0], hmul[:], ALU.add))
                    own.settle(v.memset(decay[:, c, :, 0], 0.0))
                    own.settle(v.tensor_tensor_scan(scratch[:, 4 + c, 0:CHN], decay[:, c].rearrange("p n t -> p (n t)"),
                                                    scratch[:, 4 + c, 0:CHN], 0.0, ALU.mult, ALU.add))
                    own.settle(v.tensor_copy(hcar[:, b, c], hs[:, c, :, CH - 1]))
                v.nop().then_inc(scan_done, 1)
                dve.wait_ge(gain_ready, m + 1)
                own.settle(v.tensor_tensor(gch[:], gch[:], ps[:, 2, 0:DC * CH].rearrange(
                    "p (c t) -> p c t", c=DC), ALU.mult))
                for c in range(DC):
                    dve.wait_ge(gc_ready, m * 2 + (c + 1))
                    own.settle(v.tensor_tensor(hs[:, c], hs[:, c], gain[:, c], ALU.mult))
                    own.settle(v.tensor_reduce(ysum[:], hs[:, c].rearrange("p n t -> p t n"), AX.X, ALU.add))
                    own.settle(v.tensor_tensor(ysum[:], ysum[:], gch[:, c], ALU.mult))
                    own.settle(v.tensor_tensor(y_all[:, c, tokens], y_all[:, c, tokens], ysum[:], ALU.add))
                dve.wait_ge(zr_ready, m + 1)
                v.nop().then_inc(chunk_done, 1)

            def skip(n, m):
                own.count, own.shift = start, m * STEPS_PER_CHUNK
                own.settle(v.memset(hcar[:], 0.0))
                own.count, own.shift = start, 0
                dve.sem_inc(za_ready, n)
                dve.sem_inc(zr_ready, n)
                dve.sem_inc(scan_done, n)
                dve.sem_inc(dve_step, n * STEPS_PER_CHUNK - 1)
                dve.sem_inc(chunk_done, n)

            own.settle(v.memset(hcar[:], 0.0))
            start = own.count

            def counted(q, b, m):
                own.count, own.shift = start, m * STEPS_PER_CHUNK
                chunk(q, b, m)
                assert own.count == start + STEPS_PER_CHUNK, own.count - start
                own.count, own.shift = start, 0

            dve.wait_ge(y_ready, DC * NBLK)
            chunk_loops(dve, v, mybir.EngineType.DVE, counted, skip)
            own.count = start + NCH * STEPS_PER_CHUNK

            def statistics(rows, r, n, done):
                hold(dve, dve_held)
                for j in range(TPB):
                    last = v.bn_stats(bst[:, r, j], rows(j))
                own.settle(last)
                hold(dve, dve_held)
                for j in range(TPB):
                    last = v.bn_aggr(bag[:, r, j], bst[:, r, j])
                last.then_inc(done, 1)
                dve.wait_ge(done, n + 1)

            def residual(n, r):
                tiles = ds(n * TPB, TPB)
                dve.wait_ge(mix_sum, n + 1)
                v.tensor_tensor(res1[:, tiles, :], ps[:, r].rearrange("p (i d) -> p i d", d=DM), res1[:, tiles, :],
                                ALU.add).then_inc(res_ready, 1)
                dve.wait_ge(res_ready, n + 1)
                statistics(lambda j: res1[:, ds(n * TPB + j, 1), :].rearrange("p a d -> p (a d)"), r, n, var_ready)

            def layer_norm(n, r):
                dve.wait_ge(rstd_ready, n + 1)
                for j in range(TPB):
                    last = v.tensor_scalar(x1b[:, r, j], res1[:, ds(n * TPB + j, 1), :].rearrange("p a d -> p (a d)"),
                                           bag[:, r, j, 0:1], rstd[:, r, j:j + 1], ALU.subtract, ALU.mult)
                last.then_inc(x1_ready, 1)

            def two_blocks(i, last_two):
                for r in range(2):
                    n = i * 2 + r
                    if not last_two:
                        dve.wait_ge(x1_ready, n + 1)
                        residual(n + 2, r)
                    if not last_two or r == 0:
                        dve.wait_ge(x1_stored[1 - r], 16 * (i + 1 + r))
                        dve.wait_ge(x1_turned, n + 1)
                        dve.wait_ge(x1_kept, n + 1)
                        layer_norm(n + 1, 1 - r)
                    dve.wait_ge(gate_sum, n + 1)
                    v.tensor_copy(lg[:, ds(n * TPB, TPB), :],
                                  ps[:, 3, 0:TPB * E].rearrange("p (i e) -> p i e", e=E)).then_inc(lg_ready, 1)

            dve.wait_ge(gwT_sum, 1)
            v.tensor_copy(gwT[:], ps[:, 3, 0:E]).then_inc(gwT_ready, 1)
            for r in range(2):
                dve.wait_ge(xres_in[r], 16)
            for r in range(2):
                residual(r, r)
            layer_norm(0, 0)
            with loop(NBLK // 2 - 1, 2) as i:
                two_blocks(i, False)
            two_blocks(NBLK // 2 - 1, True)

            def shared_acc(n, r):
                tiles = ds(n * TPB, TPB)
                dve.wait_ge(sh_sum, n + 1)
                v.tensor_tensor(acc[:, tiles, :], ps[:, r].rearrange("p (i d) -> p i d", d=DM), acc[:, tiles, :],
                                ALU.add).then_inc(acc_ready, 1)

            def shared(n, r, first=False):
                for h in range(2):
                    dve.wait_ge(sh_silu, n * 2 + h + 1)
                    dve.wait_ge(sh_c, n * 2 + h + 1)
                    v.tensor_tensor(shT[:, r, h], ps[0:SHH, 6 + h], sgate[:, h], ALU.mult).then_inc(sh_h, 1)
                if not first:
                    shared_acc(n - 1, 1 - r)

            def over_e(a):
                return a.unsqueeze(2).to_broadcast([P, TILES, E])

            def over_t(a):
                return a.unsqueeze(1).to_broadcast([P, TILES, E])

            dve.wait_ge(lg_ready, NBLK + 1)
            own.settle(v.tensor_reduce(col[:], lg[:], AX.X, ALU.max))
            v.tensor_tensor(t3[:], lg[:], over_e(col[:]), ALU.subtract).then_inc(lgx_ready, 1)
            dve.wait_ge(x1_kept, NBLK + 1)
            dve.wait_ge(sce_ready, 1)
            own.settle(v.tensor_reduce(col[:], sc[:], AX.X, ALU.add))
            own.settle(v.reciprocal(col[:], col[:]))
            own.settle(v.tensor_tensor(sc[:], sc[:], over_e(col[:]), ALU.mult))
            shared(0, 0, True)
            for k, m in enumerate((m1, m2)):
                own.settle(v.tensor_reduce(wk2[:, k], sc[:], AX.X, ALU.max))
                own.settle(v.tensor_tensor(t3[:], sc[:], over_e(wk2[:, k]), ALU.is_equal))
                own.settle(v.tensor_tensor(t3[:], t3[:], over_t(desc[:]), ALU.mult))
                own.settle(v.tensor_reduce(col[:], t3[:], AX.X, ALU.max))
                own.settle(v.tensor_tensor(m[:], t3[:], over_e(col[:]), ALU.is_equal))
                if k == 0:
                    own.settle(v.scalar_tensor_tensor(out=sc[:].rearrange("p t e -> p (t e)"),
                                                      in0=m1[:].rearrange("p t e -> p (t e)"), scalar=-2.0,
                                                      in1=sc[:].rearrange("p t e -> p (t e)"),
                                                      op0=ALU.mult, op1=ALU.add))
            v.tensor_tensor(rk[:], m1[:], m2[:], ALU.add).then_inc(m_ready, 1)
            shared(1, 1)
            dve.wait_ge(rank_sum, 1)
            within, totals = (ps[:, 2, m * TILES * E:(m + 1) * TILES * E].rearrange("p (t e) -> p t e", e=E)
                              for m in range(2))
            own.settle(v.memset(ex[:, 0, :], 0.0))
            for e in range(E):
                own.settle(v.tensor_tensor_scan(ex[:, 1:TILES, e], ones[:, 0:TILES - 1], totals[:, 0:TILES - 1, e],
                                                0.0, ALU.mult, ALU.add))
            shared(2, 0)
            own.settle(v.tensor_tensor(cnt[:], totals[:, TILES - 1, :], ex[:, TILES - 1, :], ALU.add))
            own.settle(v.tensor_scalar(cnti[:], cnt[:], float(P - 1), None, ALU.add))
            own.settle(v.tensor_scalar(nti[:], cnti[:], 7, None, ALU.logical_shift_right))
            own.settle(v.tensor_copy(ntf[:], nti[:]))
            own.settle(v.tensor_tensor_scan(tend[:], ones[:, 0:E], ntf[:], 0.0, ALU.mult, ALU.add))
            own.settle(v.tensor_tensor(tbeg[:], tend[:], ntf[:], ALU.subtract))
            own.settle(v.tensor_scalar(tbeg[:], tbeg[:], float(P), None, ALU.mult))
            own.settle(v.tensor_tensor(ex[:], within, ex[:], ALU.add))
            own.settle(v.tensor_tensor(ex[:], ex[:], over_t(tbeg[:]), ALU.add))
            for k, m in enumerate((m1, m2)):
                own.settle(v.tensor_tensor(t3[:], m[:], ex[:], ALU.mult))
                own.settle(v.tensor_reduce(slot[:, k], t3[:], AX.X, ALU.add))
            shared(3, 1)
            own.settle(v.tensor_copy(sloti[:], slot[:]))
            own.settle(v.tensor_scalar(hii[:], sloti[:], 7, None, ALU.logical_shift_right))
            own.settle(v.tensor_scalar(loi[:], sloti[:], P - 1, None, ALU.bitwise_and))
            own.settle(v.tensor_copy(lof[:], loi[:].rearrange("p k t -> p t k")))
            own.settle(v.tensor_copy(hif[:], hii[:].rearrange("p k t -> p t k")))
            hi_cols, lo_cols = (a[:].rearrange("p t k -> p (t k)") for a in (hif, lof))
            with dve.Fori(0, 2) as i:
                for u in range(2):
                    for r in range(2):
                        m = i * 4 + 2 * u + r
                        pairs = ds(i * 4 * GROUP + (2 * u + r) * GROUP, GROUP)
                        dve.wait_ge(oh_sum, m + 1)
                        v.tensor_tensor(ohe[:, r], iota[:, 0:N_TILES].unsqueeze(1).to_broadcast([P, GROUP, N_TILES]),
                                        hi_cols[:, pairs].unsqueeze(2).to_broadcast([P, GROUP, N_TILES]),
                                        ALU.is_equal).then_inc(ohe_ready, 1)
                        v.tensor_tensor(ohl[:, r], iota[:].unsqueeze(1).to_broadcast([P, GROUP, P]),
                                        lo_cols[:, pairs].unsqueeze(2).to_broadcast([P, GROUP, P]), ALU.is_equal)
                        dve.wait_ge(ohe_ready, m + 1)
                        v.tensor_scalar(ohh[:, r, :, 0], ohe[:, r], pcol[:], None, ALU.mult).then_inc(oh_ready, 1)
                        dve.wait_ge(oh_ready, m + 1)
                    shared(i * 2 + (4 + u), u)
            dve.wait_ge(oh_sum, TILES * K // GROUP + 3)
            own.settle(v.tensor_copy(pid, ps[:, 3, 0:2 * N_TILES].rearrange("p (a n) -> p a n", a=2)))
            own.settle(v.tensor_scalar(tokf, pid[:, 1], float(P), -float(P), ALU.mult, ALU.add))
            own.settle(v.tensor_tensor(tokf, tokf, pid[:, 0], ALU.add))
            own.settle(v.tensor_copy(toki[:], tokf))
            own.settle(v.tensor_scalar(idx_src[:, 0:N_TILES], toki[:], TOK - 1, None, ALU.bitwise_and))
            v.tensor_copy(ring_src[:], idx_src[:, 0:2 * HALF].rearrange("p (h n) -> p h n", h=2)).then_inc(src_ready, 1)
            own.settle(v.tensor_tensor(tex[:], tex[:], tend[0:1, :].unsqueeze(1).to_broadcast([1, IDXC, E]), ALU.is_ge))
            own.settle(v.tensor_reduce(texs[:], tex[:], AX.X, ALU.add))
            v.tensor_scalar(texi[:], texs[:], float(E - 1), None, ALU.min).then_inc(texi_ready, 1)
            own.settle(v.tensor_scalar(dstf, tokf, 0.0, float(NO_ROW), ALU.is_lt, ALU.mult))
            own.settle(v.tensor_tensor(idx_dst[:, 0:N_TILES], dstf, tokf, ALU.add))
            v.tensor_copy(ring_dst[:, 0], idx_dst[:, 0:HALF]).then_inc(dst_ready, 1)

            shared_acc(NBLK - 1, 1)

            def rows_out(par, turned):
                dve.wait_ge(e_turned, turned)
                v.tensor_copy(xgT[:, 0, par], ps[:, 2, 0:P]).then_inc(eT_high, 1)
                dve.wait_ge(eT_high, turned)
                v.tensor_tensor(xgT[:, 1, par], ps[:, 2, 0:P], xgT[:, 0, par].bitcast(F32),
                                ALU.subtract).then_inc(eT_ready, 1)

            def gated(n):
                dve.wait_ge(e_c, n)
                dve.wait_ge(e_silu, n)
                v.tensor_tensor(eh, ps[:, 1, 0:EH], egate, ALU.mult).then_inc(e_h, 1)

            rows_out(0, 1)
            rows_out(1, 2)
            gated(1)

            def eight_tiles(i, first):
                for k in range(1, 9):
                    if k in (4, 8):
                        g_ = k // HALF
                        for r in range(4 if k == 8 or not first else 0):
                            dve.wait_ge(scattered[r], 16 * (i * 2 + g_ - 1))
                        v.tensor_copy(ring_dst[:, g_ % 2], idx_dst[:, ds(i * 8 + g_ * HALF, HALF)]).then_inc(dst_ready, 1)
                    dve.wait_ge(eh_turned, i * 8 + k)
                    v.tensor_copy(ehT[:, 0:2], ps[:, 3, 0:2 * P].rearrange("p (c t) -> p c t", c=2)).then_inc(ehT_ready, 1)
                    v.tensor_copy(ehT[0:EH - 2 * P, 2], ps[0:EH - 2 * P, 3, 2 * P:3 * P]).then_inc(ehT_ready, 1)
                    dve.wait_ge(e_c, i * 8 + k)
                    rows_out((k + 1) % 2, i * 8 + k + 2)
                    if k in (2, 6):
                        g_ = (k + 6) // HALF
                        v.tensor_copy(ring_src[:, g_ % 2], idx_src[:, ds(i * 8 + g_ * HALF, HALF)]).then_inc(src_ready, 1)
                    gated(i * 8 + k + 1)

            eight_tiles(0, True)
            with dve.Fori(1, N_TILES // 8) as i:
                eight_tiles(i, False)

            with loop(NBLK // FIN, FIN * 2) as i:
                for r in range(FIN):
                    n = i * FIN + r
                    dve.wait_ge(y_in[r], 32 * (i + 1))
                    dve.wait_ge(y0_added, n + 1)
                    for j in range(TPB):
                        row = acc[:, ds(n * TPB + j, 1), :].rearrange("p a d -> p (a d)")
                        last = v.scalar_tensor_tensor(out=row, in0=y1r[:, r, j],
                                                      scalar=wk2[:, 1, ds(n * TPB + j, 1)], in1=row,
                                                      op0=ALU.mult, op1=ALU.add)
                    own.settle(last)
                    v.nop().then_inc(fin_read, 1)
                    dve.wait_ge(o_ready, n + 1)
                    statistics(lambda j: acc[:, ds(n * TPB + j, 1), :].rearrange("p a d -> p (a d)"), r % 2, n, fvar_ready)


_INS = ['L0_attn_x', 'L0_attn_W_in', 'L0_attn_conv_w', 'L0_attn_W_x', 'L0_attn_W_delta', 'L0_attn_b_delta',
        'L0_attn_A_log', 'L0_attn_D', 'L0_attn_W_out', 'L0_ffn_gate_w', 'L0_ffn_w1', 'L0_ffn_w2', 'L0_ffn_w3',
        'L0_ffn_sw1', 'L0_ffn_sw2', 'L0_ffn_sw3']
_OUTS = [((BATCH, SEQ, DM), 'float32')]


def kernel(**inputs):
    import numpy as _np
    import concourse.bacc as _bacc
    from concourse import mybir as _mybir
    from concourse.bass_utils import run_bass_kernel_spmd as _run

    nc = _bacc.Bacc("TRN2", target_bir_lowering=False, num_devices=1)
    arrays, args = {}, []
    for name in _INS:
        a = _np.ascontiguousarray(inputs[name])
        arrays[f"in_{name}_dram"] = a
        args.append(nc.dram_tensor(f"in_{name}_dram", a.shape, _mybir.dt.from_np(a.dtype), kind="ExternalInput").ap())
    for i, (shape, dtype) in enumerate(_OUTS):
        dt = _mybir.dt.from_np(_np.dtype(dtype))
        args.append(nc.dram_tensor(f"out_{i}_dram", shape, dt, kind="ExternalOutput").ap())
    build(nc, *args)
    r = _run(nc, [arrays], core_ids=[0])
    got = tuple(r.results[0][f"out_{i}_dram"] for i in range(len(_OUTS)))
    return got[0]
```
